# Optimizing a Trainium2 kernel written in Bass

```python
import numpy as np
import jax
import jax.numpy as jnp

def _softmax(x, axis=-1):
    return jax.nn.softmax(x, axis=axis)

def _gelu(x):
    return jax.nn.gelu(x, approximate=True)

def _silu(x):
    return jax.nn.silu(x)

def _sigmoid(x):
    return jax.nn.sigmoid(x)

def _layernorm(x, axis=-1, eps=1e-05):
    m = jnp.mean(x, axis=axis, keepdims=True)
    v = jnp.var(x, axis=axis, keepdims=True)
    return (x - m) / jnp.sqrt(v + eps)

def _scatter_add(tgt, idx, src, axis=0):
    return tgt.at[idx].add(src)

def _segment_sum(src, seg, n):
    return jax.ops.segment_sum(src, seg, n)
kernel_name = 'mk_early_fusion_embed_d1_tok_img1024_r4_f2f66d'

def setup_inputs(seed: int=0):
    np.random.seed(seed)
    _w = jnp.asarray

    def _rec_inputs():
        import jax
        import jax.numpy as jnp
        _rk = jax.random.key(seed)
        x = -0.00016672 + 0.999947 * jax.random.normal(jax.random.fold_in(_rk, 1), (32, 3, 96, 96), jnp.float32)
        x_txt = jax.random.randint(jax.random.fold_in(_rk, 51), (32, 77), 0, 12564, jnp.int32)
        return (x, x_txt)
    x, x_txt = _rec_inputs()

    def _L0_tok_setup():
        import jax, jax.numpy as jnp
        import numpy as np
        B, C, H, W = (64, 3, 96, 96)
        P = 16
        NP = H // P * (W // P)
        PD = C * P * P
        ED = 256
        NCLS = 1

        def _layernorm(x, g, b, eps=1e-05):
            mu = jnp.mean(x, axis=-1, keepdims=True)
            var = jnp.mean(jnp.square(x - mu), axis=-1, keepdims=True)
            return (x - mu) * jax.lax.rsqrt(var + eps) * g + b
        key = jax.random.key(seed)
        ks = jax.random.split(key, 8)
        x = jax.random.normal(ks[0], (B, C, H, W), dtype=jnp.float32)
        ln1_g = jnp.ones((PD,), jnp.float32)
        ln1_b = jnp.zeros((PD,), jnp.float32)
        W_proj = jax.random.normal(ks[1], (PD, ED), jnp.float32) / np.sqrt(PD)
        b_proj = jnp.zeros((ED,), jnp.float32)
        ln2_g = jnp.ones((ED,), jnp.float32)
        ln2_b = jnp.zeros((ED,), jnp.float32)
        cls_token = jax.random.normal(ks[2], (1, NCLS, ED), jnp.float32)
        pos_emb = jax.random.normal(ks[3], (1, NP + NCLS, ED), jnp.float32)
        return {'x': x, 'ln1_g': ln1_g, 'ln1_b': ln1_b, 'W_proj': W_proj, 'b_proj': b_proj, 'ln2_g': ln2_g, 'ln2_b': ln2_b, 'cls_token': cls_token, 'pos_emb': pos_emb}
    _L0_tok_all = _L0_tok_setup()
    _L0_tok_in = {k: v for k, v in _L0_tok_all.items() if k in ('ln1_g', 'ln1_b', 'W_proj', 'b_proj', 'ln2_g', 'ln2_b', 'cls_token', 'pos_emb')}
    del _L0_tok_all

    def _L0_txt_setup():
        import jax, jax.numpy as jnp
        import numpy as np
        VOCAB = 50257
        D_MODEL = 256
        N_BASES = 4
        B, S = (8, 2048)
        key = jax.random.key(seed)
        k1, k2, k3, k4 = jax.random.split(key, 4)
        x = jax.random.randint(k1, (B, S), 0, VOCAB, dtype=jnp.int32).astype(jnp.int64)
        coeff_weight = jax.random.normal(k2, (VOCAB, N_BASES), dtype=jnp.float32)
        base_embed_weight = jax.random.normal(k3, (N_BASES, D_MODEL), dtype=jnp.float32)
        lang_bias = jax.random.normal(k4, (N_BASES, D_MODEL), dtype=jnp.float32)
        return {'x': x, 'lang_id': 2, 'coeff_weight': coeff_weight, 'base_embed_weight': base_embed_weight, 'lang_bias': lang_bias}
    _L0_txt_all = _L0_txt_setup()
    _L0_txt_in = {k: v for k, v in _L0_txt_all.items() if k in ('coeff_weight', 'base_embed_weight', 'lang_bias')}
    del _L0_txt_all

    def _L0_attn_setup():
        import jax, jax.numpy as jnp
        import numpy as np
        B, S, D, H = (4, 1024, 256, 16)
        HD = D // H
        EPS = 1e-06

        def _feature_map(t):
            return jax.nn.elu(t) + 1.0
        key = jax.random.key(seed)
        ks = jax.random.split(key, 5)
        scale = 0.02
        return {'x': jax.random.normal(ks[0], (B, S, D), dtype=jnp.float32), 'wq': jax.random.normal(ks[1], (D, D), dtype=jnp.float32) * scale, 'wk': jax.random.normal(ks[2], (D, D), dtype=jnp.float32) * scale, 'wv': jax.random.normal(ks[3], (D, D), dtype=jnp.float32) * scale, 'wo': jax.random.normal(ks[4], (D, D), dtype=jnp.float32) * scale}
    _L0_attn_all = _L0_attn_setup()
    _L0_attn_in = {k: v for k, v in _L0_attn_all.items() if k in ('wq', 'wk', 'wv', 'wo')}
    del _L0_attn_all

    def _L0_ffn_setup():
        import jax, jax.numpy as jnp
        import numpy as np
        E, TOPK, R = (8, 2, 16)
        D, H, GH = (256, 16, 64)
        HD = D // H
        SCALE = HD ** (-0.5)

        def _svd_moe(x, Wm, U, S, V, b, idx, gates):
            main = jnp.einsum('bsd,od->bso', x, Wm)
            Ug, Sg, Vg = (U[idx], S[idx], V[idx])
            xv = jnp.einsum('bsd,bkrd->bksr', x, Vg)
            xvs = xv * Sg[:, :, None, :]
            eo = jnp.einsum('bksr,bkor->bkso', xvs, Ug)
            expert = jnp.einsum('bkso,bk->bso', eo, gates)
            return main + expert + b
        key = jax.random.key(seed)
        ks = jax.random.split(key, 32)
        B, S = (32, 257)
        inp = {'hidden_states': jax.random.normal(ks[0], (B, S, D), jnp.float32)}
        inp['gw1'] = jax.random.normal(ks[1], (GH, D), jnp.float32) * 0.02
        inp['gb1'] = jnp.zeros((GH,), jnp.float32)
        inp['gw2'] = jax.random.normal(ks[2], (E, GH), jnp.float32) * 0.02
        inp['gb2'] = jnp.zeros((E,), jnp.float32)
        i = 3
        for p in ('q', 'k', 'v', 'o'):
            inp[p + 'Wm'] = jax.random.normal(ks[i], (D, D), jnp.float32) * 0.02
            i += 1
            inp[p + 'U'] = jax.random.normal(ks[i], (E, D, R), jnp.float32) * 0.02
            i += 1
            inp[p + 'S'] = jax.random.normal(ks[i], (E, R), jnp.float32) * 0.1
            i += 1
            inp[p + 'V'] = jax.random.normal(ks[i], (E, R, D), jnp.float32) * 0.02
            i += 1
            inp[p + 'b'] = jnp.zeros((D,), jnp.float32)
        return inp
    _L0_ffn_all = _L0_ffn_setup()
    _L0_ffn_in = {k: v for k, v in _L0_ffn_all.items() if k in ('gw1', 'gb1', 'gw2', 'gb2', 'qWm', 'qU', 'qS', 'qV', 'qb', 'kWm', 'kU', 'kS', 'kV', 'kb', 'vWm', 'vU', 'vS', 'vV', 'vb', 'oWm', 'oU', 'oS', 'oV', 'ob')}
    del _L0_ffn_all
    return {'x': x, 'x_txt': x_txt, 'L0_tok_ln1_g': _L0_tok_in['ln1_g'], 'L0_tok_ln1_b': _L0_tok_in['ln1_b'], 'L0_tok_W_proj': _L0_tok_in['W_proj'], 'L0_tok_b_proj': _L0_tok_in['b_proj'], 'L0_tok_ln2_g': _L0_tok_in['ln2_g'], 'L0_tok_ln2_b': _L0_tok_in['ln2_b'], 'L0_tok_cls_token': _L0_tok_in['cls_token'], 'L0_tok_pos_emb': _L0_tok_in['pos_emb'], 'L0_txt_coeff_weight': _L0_txt_in['coeff_weight'], 'L0_txt_base_embed_weight': _L0_txt_in['base_embed_weight'], 'L0_txt_lang_bias': _L0_txt_in['lang_bias'], 'L0_attn_wq': _L0_attn_in['wq'], 'L0_attn_wk': _L0_attn_in['wk'], 'L0_attn_wv': _L0_attn_in['wv'], 'L0_attn_wo': _L0_attn_in['wo'], 'L0_ffn_gw1': _L0_ffn_in['gw1'], 'L0_ffn_gb1': _L0_ffn_in['gb1'], 'L0_ffn_gw2': _L0_ffn_in['gw2'], 'L0_ffn_gb2': _L0_ffn_in['gb2'], 'L0_ffn_qWm': _L0_ffn_in['qWm'], 'L0_ffn_qU': _L0_ffn_in['qU'], 'L0_ffn_qS': _L0_ffn_in['qS'], 'L0_ffn_qV': _L0_ffn_in['qV'], 'L0_ffn_qb': _L0_ffn_in['qb'], 'L0_ffn_kWm': _L0_ffn_in['kWm'], 'L0_ffn_kU': _L0_ffn_in['kU'], 'L0_ffn_kS': _L0_ffn_in['kS'], 'L0_ffn_kV': _L0_ffn_in['kV'], 'L0_ffn_kb': _L0_ffn_in['kb'], 'L0_ffn_vWm': _L0_ffn_in['vWm'], 'L0_ffn_vU': _L0_ffn_in['vU'], 'L0_ffn_vS': _L0_ffn_in['vS'], 'L0_ffn_vV': _L0_ffn_in['vV'], 'L0_ffn_vb': _L0_ffn_in['vb'], 'L0_ffn_oWm': _L0_ffn_in['oWm'], 'L0_ffn_oU': _L0_ffn_in['oU'], 'L0_ffn_oS': _L0_ffn_in['oS'], 'L0_ffn_oV': _L0_ffn_in['oV'], 'L0_ffn_ob': _L0_ffn_in['ob']}

def reference(x, x_txt, L0_tok_ln1_g, L0_tok_ln1_b, L0_tok_W_proj, L0_tok_b_proj, L0_tok_ln2_g, L0_tok_ln2_b, L0_tok_cls_token, L0_tok_pos_emb, L0_txt_coeff_weight, L0_txt_base_embed_weight, L0_txt_lang_bias, L0_attn_wq, L0_attn_wk, L0_attn_wv, L0_attn_wo, L0_ffn_gw1, L0_ffn_gb1, L0_ffn_gw2, L0_ffn_gb2, L0_ffn_qWm, L0_ffn_qU, L0_ffn_qS, L0_ffn_qV, L0_ffn_qb, L0_ffn_kWm, L0_ffn_kU, L0_ffn_kS, L0_ffn_kV, L0_ffn_kb, L0_ffn_vWm, L0_ffn_vU, L0_ffn_vS, L0_ffn_vV, L0_ffn_vb, L0_ffn_oWm, L0_ffn_oU, L0_ffn_oS, L0_ffn_oV, L0_ffn_ob):
    import jax
    import jax.numpy as jnp

    def _L0_tok_ref(x, ln1_g, ln1_b, W_proj, b_proj, ln2_g, ln2_b, cls_token, pos_emb):
        import jax, jax.numpy as jnp
        import numpy as np
        B, C, H, W = (64, 3, 96, 96)
        P = 16
        NP = H // P * (W // P)
        PD = C * P * P
        ED = 256
        NCLS = 1

        def _layernorm(x, g, b, eps=1e-05):
            mu = jnp.mean(x, axis=-1, keepdims=True)
            var = jnp.mean(jnp.square(x - mu), axis=-1, keepdims=True)
            return (x - mu) * jax.lax.rsqrt(var + eps) * g + b
        b = x.shape[0]
        h, w = (H // P, W // P)
        patches = x.reshape(b, C, h, P, w, P)
        patches = patches.transpose(0, 2, 4, 3, 5, 1).reshape(b, h * w, P * P * C)
        z = _layernorm(patches, ln1_g, ln1_b)
        z = jnp.einsum('bnp,pe->bne', z, W_proj) + b_proj
        z = _layernorm(z, ln2_g, ln2_b)
        cls = jnp.broadcast_to(cls_token, (b, NCLS, ED))
        z = jnp.concatenate([cls, z], axis=1)
        z = z + pos_emb
        return z

    def _L0_txt_ref(x, lang_id, coeff_weight, base_embed_weight, lang_bias):
        import jax, jax.numpy as jnp
        import numpy as np
        VOCAB = 50257
        D_MODEL = 256
        N_BASES = 4
        B, S = (8, 2048)
        coeff = jax.nn.softmax(coeff_weight[x], axis=-1)
        bases = base_embed_weight + lang_bias
        scale = jnp.sqrt(jnp.asarray(bases.shape[1], dtype=bases.dtype))
        out = jnp.einsum('bsn,nd->bsd', coeff, bases) * scale
        out = out + lang_bias[lang_id] * 0.1
        return out

    def _L0_attn_ref(x, wq, wk, wv, wo):
        import jax, jax.numpy as jnp
        import numpy as np
        B, S, D, H = (4, 1024, 256, 16)
        HD = D // H
        EPS = 1e-06

        def _feature_map(t):
            return jax.nn.elu(t) + 1.0
        b, s, d = x.shape
        q = _feature_map((x @ wq).reshape(b, s, H, HD))
        k = _feature_map((x @ wk).reshape(b, s, H, HD))
        v = (x @ wv).reshape(b, s, H, HD)
        qs = jnp.moveaxis(q, 1, 0)
        ks = jnp.moveaxis(k, 1, 0)
        vs = jnp.moveaxis(v, 1, 0)

        def step(carry, qkv):
            S_kv, z = carry
            qt, kt, vt = qkv
            S_kv = S_kv + jnp.einsum('bhd,bhe->bhde', kt, vt)
            z = z + kt
            num = jnp.einsum('bhd,bhde->bhe', qt, S_kv)
            den = jnp.einsum('bhd,bhd->bh', qt, z)[..., None] + EPS
            return ((S_kv, z), num / den)
        init = (jnp.zeros((b, H, HD, HD), x.dtype), jnp.zeros((b, H, HD), x.dtype))
        _, outs = jax.lax.scan(step, init, (qs, ks, vs))
        out = jnp.moveaxis(outs, 0, 1).reshape(b, s, d) @ wo
        return out

    def _L0_ffn_ref(hidden_states, gw1, gb1, gw2, gb2, qWm, qU, qS, qV, qb, kWm, kU, kS, kV, kb, vWm, vU, vS, vV, vb, oWm, oU, oS, oV, ob):
        import jax, jax.numpy as jnp
        import numpy as np
        E, TOPK, R = (8, 2, 16)
        D, H, GH = (256, 16, 64)
        HD = D // H
        SCALE = HD ** (-0.5)

        def _svd_moe(x, Wm, U, S, V, b, idx, gates):
            main = jnp.einsum('bsd,od->bso', x, Wm)
            Ug, Sg, Vg = (U[idx], S[idx], V[idx])
            xv = jnp.einsum('bsd,bkrd->bksr', x, Vg)
            xvs = xv * Sg[:, :, None, :]
            eo = jnp.einsum('bksr,bkor->bkso', xvs, Ug)
            expert = jnp.einsum('bkso,bk->bso', eo, gates)
            return main + expert + b
        B, S, _ = hidden_states.shape
        pooled = hidden_states.mean(axis=1)
        h = jax.nn.relu(pooled @ gw1.T + gb1)
        logits = h @ gw2.T + gb2
        top_vals, top_idx = jax.lax.top_k(logits, TOPK)
        gates = jax.nn.softmax(top_vals, axis=-1)
        q = _svd_moe(hidden_states, qWm, qU, qS, qV, qb, top_idx, gates) * SCALE
        k = _svd_moe(hidden_states, kWm, kU, kS, kV, kb, top_idx, gates)
        v = _svd_moe(hidden_states, vWm, vU, vS, vV, vb, top_idx, gates)

        def shp(t):
            return t.reshape(B, S, H, HD).transpose(0, 2, 1, 3)
        q, k, v = (shp(q), shp(k), shp(v))
        attn = jax.nn.softmax(jnp.einsum('bhsd,bhtd->bhst', q, k), axis=-1)
        ctx = jnp.einsum('bhst,bhtd->bhsd', attn, v)
        ctx = ctx.transpose(0, 2, 1, 3).reshape(B, S, D)
        out = _svd_moe(ctx, oWm, oU, oS, oV, ob, top_idx, gates)
        return out
    h = _L0_tok_ref(x, L0_tok_ln1_g, L0_tok_ln1_b, L0_tok_W_proj, L0_tok_b_proj, L0_tok_ln2_g, L0_tok_ln2_b, L0_tok_cls_token, L0_tok_pos_emb)
    h = jnp.concatenate([h, _L0_txt_ref(x_txt, 2, L0_txt_coeff_weight, L0_txt_base_embed_weight, L0_txt_lang_bias)], axis=1)
    h = h + _L0_attn_ref(_layernorm(h, axis=-1), L0_attn_wq, L0_attn_wk, L0_attn_wv, L0_attn_wo)
    h = h + _L0_ffn_ref(_layernorm(h, axis=-1), L0_ffn_gw1, L0_ffn_gb1, L0_ffn_gw2, L0_ffn_gb2, L0_ffn_qWm, L0_ffn_qU, L0_ffn_qS, L0_ffn_qV, L0_ffn_qb, L0_ffn_kWm, L0_ffn_kU, L0_ffn_kS, L0_ffn_kV, L0_ffn_kb, L0_ffn_vWm, L0_ffn_vU, L0_ffn_vS, L0_ffn_vV, L0_ffn_vb, L0_ffn_oWm, L0_ffn_oU, L0_ffn_oS, L0_ffn_oV, L0_ffn_ob)
    return h

_drawn_inputs = setup_inputs


def setup_inputs(seed=0):
    import zlib

    import numpy as np

    out = dict(_drawn_inputs(seed))
    spreads = {'L0_tok_ln1_g': (1.0, 0.6),
     'L0_tok_ln1_b': (0.0, 0.8),
     'L0_tok_b_proj': (0.0, 0.8),
     'L0_tok_ln2_g': (1.0, 0.6),
     'L0_tok_ln2_b': (0.0, 0.8),
     'L0_ffn_gb1': (0.0, 2.0),
     'L0_ffn_gb2': (0.0, 0.8),
     'L0_ffn_qb': (0.0, 0.8),
     'L0_ffn_kb': (0.0, 2.0),
     'L0_ffn_vb': (0.0, 0.8),
     'L0_ffn_ob': (0.0, 0.8)}
    factors = {'L0_tok_cls_token': 7.052,
     'L0_attn_wq': 8.0,
     'L0_attn_wk': 8.0,
     'L0_attn_wv': 8.0,
     'L0_attn_wo': 8.0,
     'L0_ffn_gw1': 8.0,
     'L0_ffn_gw2': 8.0,
     'L0_ffn_qWm': 8.0,
     'L0_ffn_qU': 8.0,
     'L0_ffn_qS': 8.0,
     'L0_ffn_qV': 8.0,
     'L0_ffn_kWm': 8.0,
     'L0_ffn_kU': 8.0,
     'L0_ffn_kS': 8.0,
     'L0_ffn_kV': 8.0,
     'L0_ffn_vWm': 8.0,
     'L0_ffn_vU': 8.0,
     'L0_ffn_vS': 8.0,
     'L0_ffn_vV': 8.0,
     'L0_ffn_oWm': 8.0,
     'L0_ffn_oU': 8.0,
     'L0_ffn_oS': 8.0,
     'L0_ffn_oV': 8.0}
    for name, (base, spread) in spreads.items():
        noise = np.random.default_rng([zlib.crc32(name.encode()), seed]).standard_normal(out[name].shape)
        drawn = base * np.exp(spread * noise) if base else spread * noise
        out[name] = jnp.asarray(drawn.astype(out[name].dtype))
    for name, factor in factors.items():
        out[name] = (out[name] * factor).astype(out[name].dtype)
    return out
```

```python
from contextlib import ExitStack

import concourse.bass as bass
from concourse import mybir

F32 = mybir.dt.float32
BF16 = mybir.dt.bfloat16
I32 = mybir.dt.int32
U32 = mybir.dt.uint32
ALU = mybir.AluOpType
ACT = mybir.ActivationFunctionType
AX = mybir.AxisListType

B = 32
D = 256
KC = D // 128
HEADS, HD = 16, 16
HALF_HEADS = HEADS // 2
PATCH, CH, SIDE = 16, 3, 96
GRID = SIDE // PATCH
NP = GRID * GRID
PD = CH * PATCH * PATCH
PCH = PD // 128
TXT = 77
IMG = NP + 1
T = TXT + IMG
G = 4
GT = G * T
NG = B // G
NB = 4
GATHER_P = 112
GATHER_N = B * TXT // GATHER_P
E, R, GH = 8, 16, 64
ER = E * R
VW = 32
LN_EPS = 1e-5
DEN_EPS = 1e-6
Q_SCALE = HD ** -0.5
PROJ = ("q", "k", "v", "o")
PARTS = 3
ROWS = 6 * HD


class Event:

    def __init__(self, sem, per_group=1, unit=1):
        self.sem, self.per_group, self.unit = sem, per_group, unit

    def value(self, it, shift, n):
        j, base = it
        v = self.unit * (self.per_group * (base + shift) + n + 1)
        return v if j is None else j * (2 * self.unit * self.per_group) + v

    def wait(self, eng, it, shift, n, alone=None):
        v = self.value(it, shift, n)
        if not isinstance(v, int) or v > 0:
            eng.wait_ge(self.sem, v)
            if alone is not None and not isinstance(v, int):
                eng.sem_inc(alone, 1)


class ParityEvent:

    def __init__(self, sems, per_group):
        self.sems, self.per_group = sems, per_group

    def sem(self, it, shift):
        return self.sems[(it[1] + shift) % 2]

    def wait(self, eng, it, shift):
        j, base = it
        v = 16 * self.per_group * ((base + shift) // 2 + 1)
        if j is None and v <= 0:
            return
        eng.wait_ge(self.sem(it, shift), v if j is None else j * (16 * self.per_group) + v)


def sample(it, shift, s):
    j, base = it
    b = G * (base + shift) + s
    return b if j is None else j * (2 * G) + b


def span(it, shift, n=G):
    b = sample(it, shift, 0)
    return slice(b, b + n) if isinstance(b, int) else bass.ds(b, n)


def run_iterations(eng, body):
    body((None, -2))
    body((None, -1))
    with eng.Fori(0, (NG - 2) // 2) as j:
        body((j, 0))
        body((j, 1))
    body((None, NG - 2))
    body((None, NG - 1))


def slot(tensor, r):
    return r if tensor == 0 else PARTS - 1 - r


def started(it, shift):
    return it[0] is not None or 0 <= it[1] + shift < NG




def embed(nc, ctx, A, k):
    with ExitStack() as c:
        def sb(name, shape, dt=F32):
            return c.enter_context(nc.sbuf_tensor(name, shape, dt))

        def sem(name):
            return c.enter_context(nc.semaphore(name))

        HB = B // 2
        PR = HB * GRID
        ximg = [sb(f"ximg{h}", [PR, CH, PATCH, SIDE]) for h in range(2)]
        pstat = sb("pstat", [PR, 2, GRID, 2, 6])
        pmv = sb("pmv", [PR, 2, GRID, 2])
        pve = sb("pve", [PR, 2, GRID])
        prs = sb("prs", [PR, 2, GRID])
        nhalf = sb("nhalf", [PR, GRID])
        patch = sb("patch", [PR, GRID, PD])
        xT = sb("xT", [128, 2, PCH, PR])
        wraw = sb("wraw", [128, PCH, D])
        wg = sb("wg", [128, PCH, D])
        g1 = sb("g1", [128, PCH])
        b1 = sb("b1", [128, PCH])
        b1b = sb("b1b", [128, PCH, 128])
        bproj = sb("bproj", [PR, D])
        ybias = sb("ybias", [PR, D])
        y = sb("y", [PR, GRID, D])
        ystat = sb("ystat", [PR, GRID, 6])
        ymv = sb("ymv", [PR, GRID, 2])
        yve = sb("yve", [PR, GRID])
        yrs = sb("yrs", [PR, GRID])
        g2 = sb("g2", [PR, D])
        b2 = sb("b2", [PR, D])
        pos = sb("pos", [PR, GRID, D])
        cls = sb("cls", [B, 2, D])
        cls_out = sb("cls_out", [B, D])
        idx = sb("idx", [GATHER_P, GATHER_N], I32)
        coef = sb("coef", [GATHER_P, GATHER_N, NB])
        cmax = sb("cmax", [GATHER_P, GATHER_N])
        csum = sb("csum", [GATHER_P, GATHER_N])
        crec = sb("crec", [GATHER_P, GATHER_N])
        coefT = sb("coefT", [NB + 1, B * TXT])
        base = sb("base", [NB + 1, D])
        lang = sb("lang", [NB + 1, D])
        bscale = sb("bscale", [NB + 1, 1])
        base5 = sb("base5", [NB + 1, D])
        lin_raw = {n: sb(f"lraw_{n}", [128, KC, D]) for n in ("q", "k")}
        m_raw = {n: sb(f"mraw_{n}", [128, KC, D]) for n in PROJ}
        u_raw = {n: sb(f"uraw_{n}", [128, KC, ER]) for n in PROJ}
        v_raw = {n: sb(f"vraw_{n}", [ER, D]) for n in PROJ}
        gw1_raw = sb("gw1_raw", [GH, D])
        gw2_raw = sb("gw2_raw", [E, GH])
        psX = [c.enter_context(nc.psum_tensor(f"psX{n}", [128, 512], F32)) for n in range(4)]
        psY = [c.enter_context(nc.psum_tensor(f"psY{n}", [128, 512], F32)) for n in range(2)]
        psW = [c.enter_context(nc.psum_tensor(f"psW{n}", [128, 512], F32)) for n in range(2)]
        tok = nc.dram_tensor("tok_scratch", (B, IMG, D), F32).ap()

        x_loaded = [sem("x_loaded0"), sem("x_loaded1")]
        tokw_loaded = sem("tokw_loaded")
        tokc_loaded = sem("tokc_loaded")
        mat_loaded = {n: sem(f"mat_loaded_{n}") for n in PROJ}
        gate_loaded = sem("gate_loaded")
        lin_loaded = sem("lin_loaded")
        rest_loaded = sem("rest_loaded")
        base_loaded = sem("base_loaded")
        cls_loaded = sem("cls_loaded")
        idx_loaded = sem("idx_loaded")
        gathered = sem("gathered")
        tok_stored = sem("tok_stored")
        tok_loaded = sem("tok_loaded")
        const_ready = sem("const_ready")
        wprep = sem("wprep")
        b1_ready = sem("b1_ready")
        pst = sem("pst")
        prs_ready = sem("prs_ready")
        xnorm = sem("xnorm")
        yb_filled, yb_ready = sem("yb_filled"), sem("yb_ready")
        xt_filled, xt_ready = sem("xt_filled_e"), sem("xt_ready_e")
        y_filled, y_ready = sem("y_filled"), sem("y_ready")
        yst = sem("yst")
        yrs_ready = sem("yrs_ready")
        yn = sem("yn")
        z_ready = sem("z_ready")
        wt_filled, wt_ready = sem("wt_filled"), sem("wt_ready")
        cls_ready = sem("cls_ready")
        soft = sem("soft")
        cexp = sem("cexp")
        base_ready = sem("base_ready")
        ct_filled, ct_ready = sem("ct_filled"), sem("ct_ready")
        txt_filled, txt_ready = sem("txt_filled"), sem("txt_ready")

        NCT = -(-GATHER_N // G)

        with nc.Block() as block:
            @block.sync
            def _(sp):
                for h in range(2):
                    for ch in range(CH):
                        sp.dma_start(ximg[h][:, ch].rearrange("p y x -> p (y x)"),
                                     A["x"][h * HB:(h + 1) * HB, ch].rearrange("b (h y) x -> b h (y x)", h=GRID)
                                     ).then_inc(x_loaded[h], 16)
                for ch in range(CH):
                    sp.dma_start(wraw[:, 2 * ch:2 * ch + 2],
                                 A["tok_W_proj"].rearrange("(h p c) e -> c p h e", c=CH, h=2)[ch]
                                 ).then_inc(tokw_loaded, 16)
                for t, name in ((g1, "tok_ln1_g"), (b1, "tok_ln1_b")):
                    sp.dma_start(t[:].rearrange("p (c h) -> p c h", c=CH),
                                 A[name].rearrange("(h p c) -> p c h", c=CH, h=2),
                                 allow_slow_non_contiguous=True).then_inc(tokw_loaded, 16)
                for t, name in ((bproj, "tok_b_proj"), (g2, "tok_ln2_g"), (b2, "tok_ln2_b")):
                    sp.dma_start(t[:], A[name].partition_broadcast(PR)).then_inc(tokc_loaded, 16)
                patch_pos = A["tok_pos_emb"][0, 1:IMG].rearrange("(h w) e -> h w e", h=GRID)
                sp.dma_start(pos[:], patch_pos.unsqueeze(0).broadcast_to([HB, GRID, GRID, D])
                             ).then_inc(tokc_loaded, 16)
                sp.dma_start(cls[:, 0], A["tok_cls_token"][0, 0].partition_broadcast(B)).then_inc(cls_loaded, 16)
                sp.dma_start(cls[:, 1], A["tok_pos_emb"][0, 0].partition_broadcast(B)).then_inc(cls_loaded, 16)
                sp.wait_ge(cls_ready, 1)
                sp.dma_start(tok[:, 0], cls_out[:]).then_inc(tok_stored, 16)
                for h in range(2):
                    sp.wait_ge(z_ready, h + 1)
                    sp.dma_start(tok[h * HB:(h + 1) * HB, 1:].rearrange("b (h w) e -> b h (w e)", h=GRID),
                                 y[:].rearrange("p w e -> p (w e)")).then_inc(tok_stored, 16)
                    sp.wait_ge(tok_stored, 16 * (h + 2))
                    sp.dma_start(k["hid"][TXT:T, h * HB:(h + 1) * HB],
                                 tok[h * HB:(h + 1) * HB].rearrange("b n e -> n b e")).then_inc(tok_loaded, 16)
                sp.wait_ge(tok_loaded, 32)

            @block.scalar
            def _(act):
                act.dma_start(base[0:NB], A["txt_base_embed_weight"]).then_inc(base_loaded, 16)
                act.dma_start(base[NB:NB + 1], A["txt_lang_bias"][2:3]).then_inc(base_loaded, 16)
                act.wait_ge(const_ready, 2)
                act.dma_start(lang[0:NB], A["txt_lang_bias"]).then_inc(base_loaded, 16)
                for n in PROJ:
                    act.dma_start(m_raw[n][:], A[f"ffn_{n}Wm"].rearrange("(c p) d -> p c d", p=128)
                                  ).then_inc(mat_loaded[n], 16)
                    act.dma_start(v_raw[n][:], A[f"ffn_{n}V"].rearrange("e r d -> (e r) d")
                                  ).then_inc(mat_loaded[n], 16)
                    for oc in range(KC):
                        act.dma_start(u_raw[n][:, oc].rearrange("p (e r) -> p e r", e=E),
                                      A[f"ffn_{n}U"][:, oc * 128:(oc + 1) * 128].rearrange("e p r -> p e r")
                                      ).then_inc(mat_loaded[n], 16)
                act.dma_start(gw1_raw[:], A["ffn_gw1"]).then_inc(gate_loaded, 16)
                act.dma_start(gw2_raw[:], A["ffn_gw2"]).then_inc(gate_loaded, 16)
                for n in ("q", "k"):
                    act.dma_start(lin_raw[n][:], A[f"attn_w{n}"].rearrange("(c p) e -> p c e", p=128)
                                  ).then_inc(lin_loaded, 16)
                for n in ("v", "o"):
                    act.dma_start(k[f"lw_{n}"][:], A[f"attn_w{n}"].rearrange("(c p) e -> p c e", p=128)
                                  ).then_inc(rest_loaded, 16)
                act.dma_start(k["gw2T"][GH:GH + 1], A["ffn_gb2"].partition_broadcast(1)).then_inc(rest_loaded, 16)
                act.dma_start(k["gb1"][:], A["ffn_gb1"].unsqueeze(1)).then_inc(rest_loaded, 16)
                for i, n in enumerate(PROJ):
                    act.dma_start(k["svals"][:, i:i + 1], A[f"ffn_{n}S"].rearrange("e r -> (e r)").unsqueeze(1)
                                  ).then_inc(rest_loaded, 16)
                for n in ("q", "k"):
                    for cc in range(KC):
                        act.dma_start(k[f"bias_{n}"][:, cc:cc + 1],
                                      A[f"ffn_{n}b"][cc * 128:(cc + 1) * 128].rearrange("(h d o) -> d h o", d=HD, o=1),
                                      allow_slow_non_contiguous=True).then_inc(rest_loaded, 16)
                act.dma_start(k["bias_v"][:], A["ffn_vb"].rearrange("(c p) -> p c", p=128),
                              allow_slow_non_contiguous=True).then_inc(rest_loaded, 16)
                act.dma_start(k["ob"][:], A["ffn_ob"].partition_broadcast(T)).then_inc(rest_loaded, 16)
                for i, n in enumerate(PROJ):
                    act.wait_ge(wt_filled, 2 * i + 1)
                    src = psW[0][:]
                    dst = k[f"mT_{n}"][:].rearrange("p c o -> p (c o)")
                    if n in "qk":
                        src = src.rearrange("p (a h d) -> p a h d", a=2 * KC, h=HALF_HEADS)
                        dst = dst.rearrange("p (a d h) -> p a h d", a=2 * KC, h=HALF_HEADS)
                    nc.scalar.activation(dst, src, ACT.Copy).then_inc(wt_ready, 1)
                    act.wait_ge(wt_filled, 2 * i + 2)
                    nc.scalar.activation(k[f"vT_{n}"][:].rearrange("p c r -> p (c r)"), psW[1][:, 0:256],
                                         ACT.Copy).then_inc(wt_ready, 1)
                    src, dst = psW[1][:, 256:512], k[f"uT_{n}"][:]
                    if n in "qk":
                        src = src.rearrange("p (a h d) -> p a h d", a=KC, h=HALF_HEADS)
                        dst = dst.rearrange("p (a d h) -> p a h d", a=KC, h=HALF_HEADS)
                    nc.scalar.activation(dst, src, ACT.Copy).then_inc(wt_ready, 1)
                act.wait_ge(wt_filled, 9)
                nc.scalar.activation(k["gw1T"][:].rearrange("p c g -> p (c g)"), psW[0][:, 0:KC * GH],
                                     ACT.Copy).then_inc(wt_ready, 1)
                nc.scalar.activation(k["gw2T"][0:GH], psW[0][0:GH, 128:128 + E], ACT.Copy).then_inc(wt_ready, 1)
                for n in range(2 * GRID):
                    for a in range(2):
                        act.wait_ge(xt_filled, 2 * n + a + 1)
                        if n >= 2:
                            act.wait_ge(y_filled, n - 1)
                        nc.scalar.activation(xT[:, n % 2, 3 * a:3 * a + 3].rearrange("p c r -> p (c r)"),
                                             psX[2 * (n % 2) + a][:, 0:3 * PR], ACT.Copy).then_inc(xt_ready, 1)
                act.wait_ge(soft, 2)
                nc.scalar.activation(coef[:], coef[:], ACT.Exp).then_inc(cexp, 1)
                for n in range(B // 2):
                    act.wait_ge(txt_filled, n + 1)
                    nc.scalar.activation(k["hid"][0:TXT, 2 * n:2 * n + 2].rearrange("p b e -> p (b e)"),
                                         psY[n % 2][0:TXT], ACT.Copy).then_inc(txt_ready, 1)
                act.wait_ge(rest_loaded, 16 * (2 + 2 + 4 + 4 + 2))

            @block.gpsimd
            def _(pool):
                pool.dma_start(idx[:], A["x_txt"].rearrange("b t -> (b t)").rearrange("(p n) -> p n", p=GATHER_P)
                               ).then_inc(idx_loaded, 16)
                nc.gpsimd.memset(nhalf[:], -0.5).then_inc(const_ready, 1)
                nc.gpsimd.memset(lang[:], 0.0).then_inc(const_ready, 1)
                nc.gpsimd.memset(bscale[:], 0.1).then_inc(const_ready, 1)
                nc.gpsimd.memset(k["ident"][:], 0.0).then_inc(const_ready, 1)
                pool.wait_ge(const_ready, 4)
                nc.gpsimd.affine_select(out=k["ident"][:], in_=k["ident"][:], compare_op=ALU.not_equal, fill=1.0,
                                        base=0, pattern=[[-1, 128]], channel_multiplier=1).then_inc(const_ready, 1)
                nc.gpsimd.affine_select(out=bscale[:], in_=bscale[:], compare_op=ALU.is_ge, fill=float(D) ** 0.5,
                                        base=-NB, pattern=[[0, 1]], channel_multiplier=1).then_inc(const_ready, 1)
                pool.wait_ge(idx_loaded, 16)
                for n in range(GATHER_N):
                    nc.gpsimd.indirect_dma_start(
                        coef[:, n], None, A["txt_coeff_weight"],
                        bass.IndirectOffsetOnAxis(ap=idx[:, n:n + 1], axis=0)).then_inc(gathered, 16)
                nc.gpsimd.memset(k["mask"][:], 1.0).then_inc(const_ready, 1)
                nc.gpsimd.memset(k["lneps_half"][:], -0.5).then_inc(const_ready, 1)
                nc.gpsimd.memset(coefT[:], 1.0).then_inc(const_ready, 1)
                nc.gpsimd.memset(k["h1"][:], 1.0).then_inc(const_ready, 1)
                pool.wait_ge(const_ready, 10)
                nc.gpsimd.affine_select(out=k["mask"][0:TXT, 0:TXT], in_=k["mask"][0:TXT, 0:TXT],
                                        compare_op=ALU.is_ge, fill=0.0, base=0, pattern=[[1, TXT]],
                                        channel_multiplier=-1).then_inc(const_ready, 1)
                nc.gpsimd.affine_select(out=k["mask"][:, TXT:T], in_=k["mask"][:, TXT:T],
                                        compare_op=ALU.is_ge, fill=0.0, base=TXT, pattern=[[1, IMG]],
                                        channel_multiplier=-1).then_inc(const_ready, 1)
                pool.wait_ge(const_ready, 12)
                nc.gpsimd.affine_select(out=k["mask"][:, TXT:T], in_=k["mask"][:, TXT:T],
                                        compare_op=ALU.is_ge, fill=0.0, base=-TXT, pattern=[[0, IMG]],
                                        channel_multiplier=1).then_inc(const_ready, 1)
                nc.gpsimd.iota(k["iota"][:], pattern=[[1, E]], base=0, channel_multiplier=0).then_inc(const_ready, 1)
                pool.wait_ge(const_ready, 14)
                nc.gpsimd.tensor_copy(k["iotaf"][:], k["iota"][:]).then_inc(const_ready, 1)
                for h in range(2):
                    pool.wait_ge(pst, 19 * h + 19)
                    nc.gpsimd.tensor_tensor(prs[:, h], pve[:, h], nhalf[:], ALU.pow).then_inc(prs_ready, 1)
                for h in range(2):
                    pool.wait_ge(yst, 13 * h + 13)
                    nc.gpsimd.tensor_tensor(yrs[:], yve[:], nhalf[:], ALU.pow).then_inc(yrs_ready, 1)

            @block.vector
            def _(dve):
                def patch_stats(h):
                    dve.wait_ge(x_loaded[h], 16 * CH)
                    for w in range(GRID):
                        for a in range(2):
                            nc.vector.bn_stats(pstat[:, h, w, a],
                                               ximg[h][:, :, a * 8:a * 8 + 8, w * PATCH:(w + 1) * PATCH]
                                               ).then_inc(pst, 1)
                    dve.wait_ge(pst, 19 * h + 12)
                    for w in range(GRID):
                        nc.vector.bn_aggr(pmv[:, h, w], pstat[:, h, w].rearrange("p a s -> p (a s)")
                                          ).then_inc(pst, 1)
                    dve.wait_ge(pst, 19 * h + 18)
                    nc.vector.tensor_scalar(pve[:, h], pmv[:, h, :, 1], LN_EPS, None, ALU.add).then_inc(pst, 1)

                def patch_norm(h, ws=range(GRID)):
                    dve.wait_ge(prs_ready, h + 1)
                    for w in ws:
                        if h:
                            dve.wait_ge(xt_filled, 2 * (w + 1))
                        xs = ximg[h][:, :, :, w * PATCH:(w + 1) * PATCH]
                        nc.vector.tensor_scalar(patch[:, w].rearrange("p (c y x) -> p c y x", c=CH, y=PATCH), xs, pmv[:, h, w, 0:1], prs[:, h, w:w + 1],
                                                ALU.subtract, ALU.mult).then_inc(xnorm, 1)

                dve.wait_ge(tokw_loaded, 16 * (CH + 2))
                nc.vector.tensor_tensor(wg[:], wraw[:], g1[:].unsqueeze(2).broadcast_to([128, PCH, D]),
                                        ALU.mult).then_inc(wprep, 1)
                nc.vector.tensor_copy(b1b[:], b1[:].unsqueeze(2).broadcast_to([128, PCH, 128])).then_inc(b1_ready, 1)
                patch_stats(0)
                patch_stats(1)
                patch_norm(0)
                dve.wait_ge(lin_loaded, 32)
                for n in ("q", "k"):
                    nc.vector.tensor_copy(k[f"lw_{n}"][:].rearrange("p c (a d h) -> p (c a) h d", a=KC, h=HALF_HEADS),
                                          lin_raw[n][:].rearrange("p c (a h d) -> p (c a) h d", a=KC, h=HALF_HEADS)
                                          ).then_inc(wprep, 1)
                dve.wait_ge(cls_loaded, 32)
                nc.vector.tensor_tensor(cls_out[:], cls[:, 0], cls[:, 1], ALU.add).then_inc(cls_ready, 1)
                dve.wait_ge(tokc_loaded, 64)
                nc.vector.tensor_tensor(pos[:], pos[:], b2[:].unsqueeze(1).broadcast_to([PR, GRID, D]),
                                        ALU.add).then_inc(yb_ready, 1)
                dve.wait_ge(yb_filled, 1)
                nc.vector.tensor_tensor(ybias[:], psY[0][0:PR, 0:D], bproj[:], ALU.add).then_inc(yb_ready, 1)
                dve.wait_ge(yb_ready, 2)
                for h in range(2):
                    if h:
                        dve.wait_ge(tok_stored, 32)
                    for w in range(GRID):
                        n = GRID * h + w
                        if h == 0:
                            patch_norm(1, [w])
                        dve.wait_ge(y_filled, n + 1)
                        nc.vector.tensor_tensor(y[:, w], psY[n % 2][0:PR, 0:D], ybias[:], ALU.add).then_inc(y_ready, 1)
                        dve.wait_ge(y_ready, n + 1)
                        nc.vector.bn_stats(ystat[:, w], y[:, w]).then_inc(yst, 1)
                    dve.wait_ge(yst, 13 * h + 6)
                    for w in range(GRID):
                        nc.vector.bn_aggr(ymv[:, w], ystat[:, w]).then_inc(yst, 1)
                    dve.wait_ge(yst, 13 * h + 12)
                    nc.vector.tensor_scalar(yve[:], ymv[:, :, 1], LN_EPS, None, ALU.add).then_inc(yst, 1)
                    dve.wait_ge(yrs_ready, h + 1)
                    for w in range(GRID):
                        nc.vector.tensor_scalar(y[:, w], y[:, w], ymv[:, w, 0:1], yrs[:, w:w + 1],
                                                ALU.subtract, ALU.mult).then_inc(yn, 1)
                    dve.wait_ge(yn, 7 * h + 6)
                    nc.vector.tensor_tensor(y[:], y[:], g2[:].unsqueeze(1).broadcast_to([PR, GRID, D]),
                                            ALU.mult).then_inc(yn, 1)
                    dve.wait_ge(yn, 7 * h + 7)
                    nc.vector.tensor_tensor(y[:], y[:], pos[:], ALU.add).then_inc(z_ready, 1)
                dve.wait_ge(gathered, 16 * GATHER_N)
                nc.vector.tensor_reduce(cmax[:], coef[:], AX.X, ALU.max).then_inc(soft, 1)
                dve.wait_ge(soft, 1)
                cb = [GATHER_P, GATHER_N, NB]
                nc.vector.tensor_tensor(coef[:], coef[:], cmax[:].unsqueeze(2).broadcast_to(cb),
                                        ALU.subtract).then_inc(soft, 1)
                dve.wait_ge(cexp, 1)
                nc.vector.tensor_reduce(csum[:], coef[:], AX.X, ALU.add).then_inc(soft, 1)
                dve.wait_ge(soft, 3)
                nc.vector.reciprocal(crec[:], csum[:]).then_inc(soft, 1)
                dve.wait_ge(soft, 4)
                nc.vector.tensor_tensor(coef[:], coef[:], crec[:].unsqueeze(2).broadcast_to(cb),
                                        ALU.mult).then_inc(soft, 1)
                dve.wait_ge(base_loaded, 48)
                dve.wait_ge(const_ready, 15)
                nc.vector.tensor_tensor(base5[:], base[:], lang[:], ALU.add).then_inc(base_ready, 1)
                dve.wait_ge(base_ready, 1)
                nc.vector.tensor_scalar(base5[:], base5[:], bscale[:, 0:1], None, ALU.mult).then_inc(base_ready, 1)
                cT = coefT[0:NB].rearrange("q (p n) -> q n p", n=GATHER_N)
                for m in range(NCT):
                    w = min(G, GATHER_N - G * m)
                    dve.wait_ge(ct_filled, m + 1)
                    nc.vector.tensor_copy(cT[:, G * m:G * m + w],
                                          psW[m % 2][0:NB, 0:w * GATHER_P].rearrange("q (n p) -> q n p", n=w)
                                          ).then_inc(ct_ready, 1)

            @block.tensor
            def _(pe):
                pe.wait_ge(const_ready, 5)
                ident = k["ident"]
                for i, n in enumerate(PROJ):
                    pe.wait_ge(mat_loaded[n], 64)
                    if i:
                        pe.wait_ge(wt_ready, 3 * i - 2)
                    for kc in range(KC):
                        for oc in range(KC):
                            at = (kc * KC + oc) * 128
                            mm = nc.tensor.transpose(psW[0][:, at:at + 128],
                                                     m_raw[n][:, oc, kc * 128:(kc + 1) * 128], ident[:])
                    mm.then_inc(wt_filled, 1)
                    if i:
                        pe.wait_ge(wt_ready, 3 * i)
                    for kc in range(KC):
                        nc.tensor.transpose(psW[1][:, kc * 128:(kc + 1) * 128],
                                            v_raw[n][:, kc * 128:(kc + 1) * 128], ident[:])
                    for oc in range(KC):
                        mm = nc.tensor.transpose(psW[1][:, 256 + oc * 128:384 + oc * 128], u_raw[n][:, oc], ident[:])
                    mm.then_inc(wt_filled, 1)
                pe.wait_ge(gate_loaded, 32)
                pe.wait_ge(wt_ready, 10)
                for kc in range(KC):
                    nc.tensor.transpose(psW[0][:, kc * GH:(kc + 1) * GH], gw1_raw[:, kc * 128:(kc + 1) * 128],
                                        ident[0:GH, 0:GH])
                nc.tensor.transpose(psW[0][0:GH, 128:128 + E], gw2_raw[:], ident[0:E, 0:E]).then_inc(wt_filled, 1)
                pe.wait_ge(b1_ready, 1)
                pe.wait_ge(tokw_loaded, 16 * (CH + 2))
                for kc in range(PCH):
                    mm = nc.tensor.matmul(psY[0][:, 0:D], b1b[:, kc], wraw[:, kc], start=(kc == 0),
                                          stop=(kc == PCH - 1))
                mm.then_inc(yb_filled, 1)
                pe.wait_ge(wprep, 1)

                def patch_transposes(n):
                    h, w = divmod(n, GRID)
                    pe.wait_ge(xnorm, n + 1)
                    for a in range(2):
                        if n >= 2:
                            pe.wait_ge(xt_ready, 2 * (n - 2) + a + 1)
                        for i in range(3):
                            mm = nc.tensor.transpose(psX[2 * (n % 2) + a][:, i * PR:(i + 1) * PR],
                                                     patch[:, w, (3 * a + i) * 128:(3 * a + i + 1) * 128],
                                                     ident[0:PR, 0:PR])
                        mm.then_inc(xt_filled, 1)

                patch_transposes(0)
                for n in range(2 * GRID):
                    if n + 1 < 2 * GRID:
                        patch_transposes(n + 1)
                    pe.wait_ge(xt_ready, 2 * n + 2)
                    if n == 0:
                        pe.wait_ge(yb_ready, 2)
                    if n >= 2:
                        pe.wait_ge(y_ready, n - 1)
                    for kc in range(PCH):
                        mm = nc.tensor.matmul(psY[n % 2][0:PR, 0:D], xT[:, n % 2, kc], wg[:, kc], start=(kc == 0),
                                              stop=(kc == PCH - 1))
                    mm.then_inc(y_filled, 1)
                pe.wait_ge(soft, 5)
                pe.wait_ge(wt_ready, 14)
                for m in range(NCT):
                    if m >= 2:
                        pe.wait_ge(ct_ready, m - 1)
                    for i in range(min(G, GATHER_N - G * m)):
                        mm = nc.tensor.transpose(psW[m % 2][0:NB, i * GATHER_P:(i + 1) * GATHER_P],
                                                 coef[:, G * m + i], ident[0:GATHER_P, 0:GATHER_P])
                    mm.then_inc(ct_filled, 1)
                pe.wait_ge(ct_ready, NCT)
                pe.wait_ge(base_ready, 2)
                pe.wait_ge(y_ready, 2 * GRID)
                for n in range(B // 2):
                    if n >= 2:
                        pe.wait_ge(txt_ready, n - 1)
                    for i in range(2):
                        b = 2 * n + i
                        mm = nc.tensor.matmul(psY[n % 2][0:TXT, i * D:(i + 1) * D],
                                              coefT[:, b * TXT:(b + 1) * TXT], base5[:], start=True, stop=True)
                    mm.then_inc(txt_filled, 1)



LINEAR_STEPS = (
    ("LN",), ("AV", 0), ("V", 0), ("LNX",), ("TN", 0), ("S", 1), ("TC", 0), ("XT",), ("OUT", 0),
    ("AV", 1), ("QK", 0), ("TN", 1), ("S", 2), ("TC", 1), ("QK", 1), ("OUT", 1),
    ("AV", 2), ("QK", 2), ("TN", 2), ("S", 3), ("TC", 2), ("QK", 3), ("OUT", 2),
    ("PACK",), ("AV", 3), ("TN", 3), ("S", 4), ("TC", 3), ("V", 1), ("OUT", 3),
)
MIXTURE_STEPS = (
    ("LN",), ("HB",), ("AV", 0), ("V", 0), ("LNX",), ("TN", 0), ("S", 1), ("TC", 0), ("XT",), ("OV", 0),
    ("G", 0), ("OUT", 0),
    ("AV", 1), ("M", 0), ("G", 1), ("TN", 1), ("S", 2), ("TC", 1), ("M", 1), ("OV", 1), ("M", 2), ("OUT", 1),
    ("AV", 2), ("G", 2), ("M", 3), ("TN", 2), ("MT",), ("S", 3), ("XV", 0), ("TC", 2), ("XV", 1), ("OV", 2),
    ("QK", 0), ("OUT", 2),
    ("AV", 3), ("QK", 1), ("TN", 3), ("QK", 2), ("TC", 3), ("XV", 2), ("OV", 3), ("V", 1), ("OUT", 3),
    ("S", 4), ("QK", 3), ("PACK",), ("STORE",),
)
GROUP_OF = dict(LN=2, LNX=2, XT=2, QK=2, PACK=2, G=2, XV=2, V=1, M=1, MT=1, HB=1,
                AV=0, TN=0, TC=0, OV=0, OUT=0, STORE=0)


def attention(nc, A, k, out, mixture):
    steps = MIXTURE_STEPS if mixture else LINEAR_STEPS
    L = "m" if mixture else "l"
    with ExitStack() as c:
        def sb(name, shape, dt=F32):
            return c.enter_context(nc.sbuf_tensor(f"{L}_{name}", shape, dt))

        def psum(name, shape):
            return c.enter_context(nc.psum_tensor(f"{L}_{name}", shape, F32))

        def sem(name):
            return c.enter_context(nc.semaphore(f"{L}_{name}"))

        def event(name, per_group=1, unit=1):
            return Event(sem(name), per_group, unit)

        hid, ident = k["hid"], k["ident"]
        stat = sb("stat", [T, G, 6])
        mv = sb("mv", [T, G, 2])
        ve = sb("ve", [T, G])
        rstd = sb("rstd", [T, G])
        xn = sb("xn", [T, G, D])
        xnT = [sb(f"xnT{p}", [128, KC, GT]) for p in range(2)]
        qx = [sb(f"{n}x", [128, KC, GT]) for n in "qk"]
        parts = [sb(f"{n}_parts", [128, PARTS, KC, GT], BF16) for n in "qk"]
        pack = [[sb(f"{n}_pack{p}", [128, HEADS, GT], BF16) for p in range(2)] for n in "qk"]
        v_ext = [sb(f"v_ext{p}", [T, G, HEADS, VW]) for p in range(2)]
        probs = [sb(f"probs{p}", [T, HEADS, T]) for p in range(2)]
        avT = sb("avT", [128, G, T])
        den = sb("den", [T, HEADS])
        rden = sb("rden", [T, HEADS])
        ctxt = sb("ctxt", [T, HEADS, HD])
        ctxT = sb("ctxT", [128, KC, T])
        psS = psum("psS", [128, 4, 512])
        psA = [psum(f"psA{n}", [128, 512]) for n in range(2)]
        psO = psum("psO", [128, 512])
        psN = psum("psN", [128, 512])
        scratch = [[nc.dram_tensor(f"{L}_{n}_scratch{p}", (PARTS, HD, HALF_HEADS, KC, GT), BF16).ap()
                    for p in range(2)] for n in "qk"]
        if mixture:
            pooled = sb("pooled", [128, KC, G])
            lg = sb("lg", [G, E])
            top = sb("top", [G, 8])
            topi = sb("topi", [G, 8], U32)
            topf = sb("topf", [G, 2])
            gdiff = sb("gdiff", [G, 1])
            gexp = sb("gexp", [G, 1])
            gden = sb("gden", [G, 1])
            gval = sb("gval", [G, 2])
            gsel = sb("gsel", [G, 2, E])
            gates = sb("gates", [G, E])
            gwide = sb("gwide", [G, E, R])
            cT = sb("cT", [128, 4, B])
            xvs = [sb("xvs_q", [128, GT]), sb("xvs_k", [128, GT])]
            xvs_v = [sb(f"xvs_v{p}", [128, GT]) for p in range(2)]
            xvo = sb("xvo", [128, T])
            mrow = sb("mrow", [T, HEADS, G])
            mneg = sb("mneg", [HEADS * G, T])
            mparts = sb("mparts", [HEADS * G, PARTS, T], BF16)
        else:
            pass

        init = sem("init")
        INIT = 6 if mixture else 4
        passed = {n: sem(f"{n}_passed") for n in ("sp", "pe", "dve")}
        ln_stats, ln_aggr, ln_var = event("ln_stats", G), event("ln_aggr", G), event("ln_var")
        ln_rstd, xn_ready = event("ln_rstd"), event("xn_ready", G)
        xt_filled, xnT_ready = event("xt_filled", KC), event("xnT_ready", KC)
        qk_filled, qx_ready = event("qk_filled", 4), event("qx_ready", 4)
        qk_exp, qk_min = event("qk_exp", 4), event("qk_min", 4)
        p1_ready, r_ready = event("p1_ready", 2), event("r_ready", 2)
        p2_ready, p3_ready = event("p2_ready", 2), event("p3_ready", 2)
        stored = [event(f"{n}_stored", 1, 16) for n in "qk"]
        packed = [ParityEvent([sem(f"{n}_packed{p}") for p in range(2)], 3) for n in "qk"]
        v_filled, v_ready = event("v_filled", 2), event("v_ready", 2)
        s_filled, probs_ready = event("s_filled", 2 * G), event("probs_ready", 2 * G)
        av_filled, avT_ready = event("av_filled", G), event("avT_ready", G)
        tn_filled, den_ready = event("tn_filled", G), event("den_ready", G)
        rden_ready, ctx_ready = event("rden_ready", G), event("ctx_ready", G)
        tc_filled, ctxT_ready = event("tc_filled", G), event("ctxT_ready", 2 * G)
        out_filled, res_ready = event("out_filled", G), event("res_ready", G)
        if mixture:
            pool_ready, h1_filled, h1_ready = event("pool_ready"), event("h1_filled"), event("h1_ready")
            lg_filled, gate, gexp_ready = event("lg_filled"), event("gate", 13), event("gexp_ready")
            gt_filled, cT_ready = event("gt_filled"), event("cT_ready", 4)
            xv_filled, xvs_ready = event("xv_filled", 3), event("xvs_ready", 3)
            ov_filled, xvo_ready = event("ov_filled", G), event("xvo_ready", G)
            m_filled, max_done = event("m_filled", 2 * G), event("max_done", 2 * G)
            mt_filled, mneg_ready = event("mt_filled"), event("mneg_ready")
            mpart, mpacked = event("mpart", 4), event("mpacked", 3, 16)
            hob_ready, stores = event("hob_ready"), event("stores", 2, 16)

        def active(it, step):
            if step[0] == "S":
                shift = 1 if step[1] == G else 0
            else:
                shift = GROUP_OF[step[0]]
            return shift, started(it, shift)

        def pair(p):
            return psS[0:T, 2 * p:2 * p + 2, 0:GT].rearrange("p a (h t) -> p a h t", h=G)

        with nc.Block() as block:
            @block.tensor
            def _(pe):
                occupant = {}

                def fill(it, bank, event_, shift, n):
                    if bank in occupant:
                        ev, sh, m = occupant[bank]
                        ev.wait(pe, it, sh, m)
                    occupant[bank] = (event_, shift, n)

                turn = [0]

                def next_a(it, event_, shift, n):
                    a = turn[0]
                    turn[0] = 1 - a
                    fill(it, ("A", a), event_, shift, n)
                    return psA[a]

                def proj(ps, w, src, par_cols, extra=None):
                    pairs = [(w[kc], src[kc]) for kc in range(KC)] + ([extra] if extra else [])
                    for n, (a, b) in enumerate(pairs):
                        mm = nc.tensor.matmul(ps, a, b, start=(n == 0), stop=(n == len(pairs) - 1))
                    return mm

                def XT(it, sh, live):
                    src = xn
                    for kc in range(KC):
                        ps = next_a(it, xnT_ready, sh, kc)
                        if not live:
                            continue
                        if kc == 0:
                            xn_ready.wait(pe, it, sh, G - 1)
                        for s in range(G):
                            mm = nc.tensor.transpose(ps[:, s * T:(s + 1) * T],
                                                     src[:, s, kc * 128:(kc + 1) * 128], ident[0:T, 0:T])
                        mm.then_inc(xt_filled.sem, 1)

                def QK(it, sh, live, n):
                    tensor, cc = divmod(n, KC)
                    ps = next_a(it, qx_ready, sh, n)
                    if not live:
                        return
                    x = xnT[(it[1] + sh) % 2]
                    if n == 0:
                        xnT_ready.wait(pe, it, sh, KC - 1)
                    w = k[("mT_" if mixture else "lw_") + "qk"[tensor]]
                    extra = None
                    if mixture:
                        if cc == 0:
                            xvs_ready.wait(pe, it, sh, tensor)
                        extra = (k["uT_" + "qk"[tensor]][:, cc * 128:(cc + 1) * 128], xvs[tensor][:])
                    proj(ps[:, 0:GT], [w[:, kc, cc * 128:(cc + 1) * 128] for kc in range(KC)],
                         [x[:, kc] for kc in range(KC)], None, extra).then_inc(qk_filled.sem, 1)

                def V(it, sh, live, n):
                    ps = next_a(it, v_ready, sh, n)
                    if not live:
                        return
                    par = (it[1] + sh) % 2
                    w = k["mT_v" if mixture else "lw_v"]
                    if mixture:
                        xvs_ready.wait(pe, it, sh, 2)
                    for i in range(2):
                        cols = slice((2 * n + i) * T, (2 * n + i + 1) * T)
                        extra = (xvs_v[par][:, cols], k["uT_v"][:]) if mixture else None
                        mm = proj(ps[0:T, i * D:(i + 1) * D], [xnT[par][:, kc, cols] for kc in range(KC)],
                                  [w[:, kc] for kc in range(KC)], None, extra)
                    mm.then_inc(v_filled.sem, 1)

                def heads(it, sh, s, rows, stationary, moving, filled, p):
                    par = (it[1] + sh) % 2
                    cols = slice(s * T, (s + 1) * T)
                    for n in range(8 * p, 8 * p + 8):
                        mm = nc.tensor.matmul(psS[0:T, n // G, (n % G) * T:(n % G + 1) * T],
                                              stationary[par][0:rows, n, cols], moving[par][0:rows, n, cols],
                                              start=True, stop=True)
                    mm.then_inc(filled.sem, 1)

                def S(it, sh, live, s):
                    s %= G
                    for p in range(2):
                        fill(it, ("S", p), probs_ready, sh, 2 * s + p)
                        if not live:
                            continue
                        if s == 0 and p == 0:
                            if mixture:
                                mpacked.wait(pe, it, sh, 2)
                            else:
                                packed[0].wait(pe, it, sh)
                                packed[1].wait(pe, it, sh)
                        heads(it, sh, s, ROWS + PARTS if mixture else ROWS, pack[1], pack[0], s_filled, p)

                def M(it, sh, live, s):
                    for p in range(2):
                        fill(it, ("S", p), max_done, sh, 2 * s + p)
                        if not live:
                            continue
                        if s == 0 and p == 0:
                            packed[0].wait(pe, it, sh)
                            packed[1].wait(pe, it, sh)
                        heads(it, sh, s, ROWS, pack[0], pack[1], m_filled, p)

                def MT(it, sh, live):
                    ps = next_a(it, mneg_ready, sh, 0)
                    if live:
                        max_done.wait(pe, it, sh, 2 * G - 1, alone=passed["pe"])
                        nc.tensor.transpose(ps[0:HEADS * G, 0:T], mrow[:].rearrange("p h b -> p (h b)"),
                                            ident[0:T, 0:T]).then_inc(mt_filled.sem, 1)

                def G_(it, sh, live, n):
                    if n == 0:
                        ps = next_a(it, h1_ready, sh, 0)
                        if live:
                            pool_ready.wait(pe, it, sh, 0)
                            for kc in range(KC):
                                mm = nc.tensor.matmul(ps[0:GH, 0:G], k["gw1T"][:, kc], pooled[:, kc],
                                                      start=(kc == 0), stop=(kc == KC - 1))
                            mm.then_inc(h1_filled.sem, 1)
                    elif n == 1:
                        ps = next_a(it, gate, sh, 0)
                        if live:
                            h1_ready.wait(pe, it, sh, 0)
                            nc.tensor.matmul(ps[0:G, 0:E], k["h1"][:], k["gw2T"][:], start=True, stop=True
                                             ).then_inc(lg_filled.sem, 1)
                    else:
                        ps = next_a(it, cT_ready, sh, 3)
                        if live:
                            gate.wait(pe, it, sh, 12, alone=passed["pe"])
                            nc.tensor.transpose(ps[:, 0:G], gwide[:].rearrange("p e r -> p (e r)"), ident[0:G, 0:G]
                                                ).then_inc(gt_filled.sem, 1)

                def XV(it, sh, live, n):
                    ps = next_a(it, xvs_ready, sh, n)
                    if live:
                        par = (it[1] + sh) % 2
                        w = k["vT_" + PROJ[n]]
                        proj(ps[:, 0:GT], [w[:, kc] for kc in range(KC)], [xnT[par][:, kc] for kc in range(KC)],
                             None).then_inc(xv_filled.sem, 1)

                def AV(it, sh, live, s):
                    fill(it, "O", avT_ready, sh, s)
                    if not live:
                        return
                    if s % 2 == 0:
                        v_ready.wait(pe, it, sh, s // 2)
                    for p in range(2):
                        probs_ready.wait(pe, it, sh, 2 * s + p)
                        for n in range(8 * p, 8 * p + 8):
                            h = (n % KC) * HALF_HEADS + n // KC
                            mm = nc.tensor.matmul(psO[VW * (h % 4):VW * (h % 4 + 1), (h // 4) * T:(h // 4 + 1) * T],
                                                  v_ext[(it[1] + sh) % 2][:, s, h], probs[s % 2][:, n],
                                                  start=True, stop=True, skip_group_check=True)
                    mm.then_inc(av_filled.sem, 1)

                def TN(it, sh, live, s):
                    fill(it, "N", ctx_ready, sh, s)
                    if live:
                        avT_ready.wait(pe, it, sh, s)
                        for n in range(4):
                            mm = nc.tensor.transpose(psN[0:T, n * 128:(n + 1) * 128], avT[:, n], ident[:])
                        mm.then_inc(tn_filled.sem, 1)

                def TC(it, sh, live, s):
                    fill(it, "N", ctxT_ready, sh, 2 * s + 1)
                    if live:
                        for kc in range(KC):
                            mm = nc.tensor.transpose(
                                psN[:, kc * T:(kc + 1) * T],
                                ctxt[:, kc * HALF_HEADS:(kc + 1) * HALF_HEADS].rearrange("p h d -> p (h d)"),
                                ident[0:T, 0:T])
                        mm.then_inc(tc_filled.sem, 1)

                def OV(it, sh, live, s):
                    fill(it, "O", xvo_ready, sh, s)
                    if live:
                        ctxT_ready.wait(pe, it, sh, 2 * s + 1)
                        proj(psO[:, 0:T], [k["vT_o"][:, kc] for kc in range(KC)],
                             [ctxT[:, kc] for kc in range(KC)], None).then_inc(ov_filled.sem, 1)

                def OUT(it, sh, live, s):
                    fill(it, "O", res_ready, sh, s)
                    if not live:
                        return
                    ctxT_ready.wait(pe, it, sh, 2 * s + 1)
                    w = k["mT_o" if mixture else "lw_o"]
                    extra = (xvo[:], k["uT_o"][:]) if mixture else None
                    proj(psO[0:T, 0:D], [ctxT[:, kc] for kc in range(KC)], [w[:, kc] for kc in range(KC)],
                         None, extra).then_inc(out_filled.sem, 1)

                part = dict(XT=XT, QK=QK, V=V, S=S, M=M, MT=MT, G=G_, XV=XV, AV=AV, TN=TN, TC=TC, OV=OV, OUT=OUT)

                def body(it):
                    for bank, (ev, sh, n) in occupant.items():
                        occupant[bank] = (ev, sh - 1, n)
                    for step in steps:
                        if step[0] in part:
                            sh, live = active(it, step)
                            if live or it[1] + sh < 0:
                                part[step[0]](it, sh, live, *step[1:])

                pe.wait_ge(init, INIT)
                run_iterations(pe, body)

            @block.scalar
            def _(act):
                a_turn = [0]

                def next_a():
                    a = a_turn[0]
                    a_turn[0] = 1 - a
                    return psA[a]

                def XT(it, sh, live):
                    for kc in range(KC):
                        ps = next_a()
                        if live:
                            xt_filled.wait(act, it, sh, kc)
                            nc.scalar.activation(xnT[(it[1] + sh) % 2][:, kc], ps[:, 0:GT], ACT.Copy
                                                 ).then_inc(xnT_ready.sem, 1)

                def QK(it, sh, live, n):
                    ps = next_a()
                    if not live:
                        return
                    tensor, cc = divmod(n, KC)
                    qk_filled.wait(act, it, sh, n)
                    if cc == 0:
                        p3_ready.wait(act, it, sh - 1, tensor)
                    if mixture:
                        nc.scalar.activation(qx[tensor][:, cc], ps[:, 0:GT], ACT.Identity,
                                             bias=k["bias_qs" if tensor == 0 else "bias_k"][:, cc:cc + 1],
                                             scale=Q_SCALE if tensor == 0 else 1.0).then_inc(qx_ready.sem, 1)
                    else:
                        nc.scalar.activation(qx[tensor][:, cc], ps[:, 0:GT], ACT.Exp).then_inc(qk_exp.sem, 1)
                    if cc == KC - 1:
                        qx_ready.wait(act, it, sh, n)
                        stored[tensor].wait(act, it, sh - 1, 0)
                        nc.scalar.activation(parts[tensor][:, slot(tensor, 0)], qx[tensor][:], ACT.Copy).then_inc(p1_ready.sem, 1)

                def V(it, sh, live, n):
                    ps = next_a()
                    if live:
                        v_filled.wait(act, it, sh, n)
                        nc.scalar.activation(
                            v_ext[(it[1] + sh) % 2][:, 2 * n:2 * n + 2, :, 0:HD],
                            ps[0:T].rearrange("p (b h d) -> p b h d", b=2, h=HEADS), ACT.Copy
                        ).then_inc(v_ready.sem, 1)

                def S(it, sh, live, s):
                    s %= G
                    if not (live and mixture):
                        return
                    for p in range(2):
                        s_filled.wait(act, it, sh, 2 * s + p)
                        nc.scalar.activation(
                            probs[s % 2][:, 8 * p:8 * p + 8].rearrange("p (a h) t -> p a h t", a=2),
                            pair(p), ACT.Exp).then_inc(probs_ready.sem, 1)

                def MT(it, sh, live):
                    ps = next_a()
                    if live:
                        mt_filled.wait(act, it, sh, 0)
                        mpart.wait(act, it, sh - 1, 3)
                        nc.scalar.activation(mneg[:], ps[0:HEADS * G, 0:T], ACT.Copy, scale=-1.0
                                             ).then_inc(mneg_ready.sem, 1)

                def G_(it, sh, live, n):
                    ps = next_a()
                    if not live:
                        return
                    if n == 0:
                        h1_filled.wait(act, it, sh, 0)
                        lg_filled.wait(act, it, sh - 1, 0)
                        nc.scalar.activation(k["h1"][0:GH], ps[0:GH, 0:G], ACT.Relu, bias=k["gb1"][:, 0:1],
                                             scale=1.0 / T).then_inc(h1_ready.sem, 1)
                    if n == 1:
                        gate.wait(act, it, sh, 4)
                        nc.scalar.activation(gexp[:], gdiff[:], ACT.Exp).then_inc(gexp_ready.sem, 1)

                def XV(it, sh, live, n):
                    next_a()

                def AV(it, sh, live, s):
                    if live:
                        av_filled.wait(act, it, sh, s)
                        nc.scalar.activation(avT[:].rearrange("p g t -> p (g t)"), psO[:, 0:GT], ACT.Copy
                                             ).then_inc(avT_ready.sem, 1)

                def TC(it, sh, live, s):
                    if live:
                        tc_filled.wait(act, it, sh, s)
                        for kc in range(KC):
                            if mixture:
                                nc.scalar.activation(ctxT[:, kc], psN[:, kc * T:(kc + 1) * T], ACT.Identity,
                                                     bias=k["bias_v"][:, kc:kc + 1]).then_inc(ctxT_ready.sem, 1)
                            else:
                                nc.scalar.activation(ctxT[:, kc], psN[:, kc * T:(kc + 1) * T], ACT.Copy
                                                     ).then_inc(ctxT_ready.sem, 1)

                part = dict(XT=XT, QK=QK, V=V, S=S, MT=MT, G=G_, XV=XV, AV=AV, TC=TC)

                def body(it):
                    for step in steps:
                        if step[0] in part:
                            sh, live = active(it, step)
                            if live or it[1] + sh < 0:
                                part[step[0]](it, sh, live, *step[1:])

                act.wait_ge(init, INIT)
                if mixture:
                    bias_scaled = c.enter_context(nc.semaphore("bias_scaled"))
                    nc.scalar.mul(k["bias_qs"][:], k["bias_q"][:], Q_SCALE).then_inc(bias_scaled, 1)
                    act.wait_ge(bias_scaled, 1)
                run_iterations(act, body)

            @block.vector
            def _(dve):
                a_turn = [0]

                def next_a():
                    a = a_turn[0]
                    a_turn[0] = 1 - a
                    return psA[a]

                def LN(it, sh, live):
                    if not live:
                        return
                    for s in range(G):
                        nc.vector.bn_stats(stat[:, s], hid[:, sample(it, sh, s)]).then_inc(ln_stats.sem, 1)
                    ln_stats.wait(dve, it, sh, G - 1, alone=passed["dve"])
                    for s in range(G):
                        nc.vector.bn_aggr(mv[:, s], stat[:, s]).then_inc(ln_aggr.sem, 1)
                    ln_aggr.wait(dve, it, sh, G - 1)
                    nc.vector.tensor_scalar(ve[:], mv[:, :, 1], LN_EPS, None, ALU.add).then_inc(ln_var.sem, 1)

                def LNX(it, sh, live):
                    if not live:
                        return
                    xt_filled.wait(dve, it, sh - 1, KC - 1)
                    ln_rstd.wait(dve, it, sh, 0)
                    for s in range(G):
                        nc.vector.tensor_scalar(xn[:, s], hid[:, sample(it, sh, s)], mv[:, s, 0:1], rstd[:, s:s + 1],
                                                ALU.subtract, ALU.mult).then_inc(xn_ready.sem, 1)

                def XT(it, sh, live):
                    next_a(), next_a()

                def QK(it, sh, live, n):
                    ps = next_a()
                    if not live:
                        return
                    tensor, cc = divmod(n, KC)
                    if not mixture:
                        q = qx[tensor][:, cc]
                        qk_exp.wait(dve, it, sh, n)
                        nc.vector.tensor_scalar(q, q, 1.0, None, ALU.min).then_inc(qk_min.sem, 1)
                        qk_min.wait(dve, it, sh, n)
                        nc.vector.scalar_tensor_tensor(q, ps[:, 0:GT], 0.0, q, ALU.max, ALU.add
                                                       ).then_inc(qx_ready.sem, 1)
                    if cc == KC - 1:
                        r_ready.wait(dve, it, sh, tensor)
                        nc.vector.tensor_copy(parts[tensor][:, slot(tensor, 1)], qx[tensor][:]).then_inc(p2_ready.sem, 1)

                def V(it, sh, live, n):
                    next_a()

                def S(it, sh, live, s):
                    s %= G
                    if not live or mixture:
                        return
                    for p in range(2):
                        s_filled.wait(dve, it, sh, 2 * s + p)
                        nc.vector.tensor_tensor(
                            probs[s % 2][:, 8 * p:8 * p + 8].rearrange("p (a h) t -> p a h t", a=2), pair(p),
                            k["mask"][:].unsqueeze(1).unsqueeze(1).broadcast_to([T, 2, G, T]), ALU.mult
                        ).then_inc(probs_ready.sem, 1)

                def M(it, sh, live, s):
                    if not live:
                        return
                    for p in range(2):
                        m_filled.wait(dve, it, sh, 2 * s + p)
                        nc.vector.tensor_reduce(mrow[:, 8 * p:8 * p + 8, s].rearrange("p (a h) -> p a h", a=2),
                                                pair(p), AX.X, ALU.max).then_inc(max_done.sem, 1)

                def MT(it, sh, live):
                    next_a()
                    if not live:
                        return
                    mneg_ready.wait(dve, it, sh, 0)
                    mpacked.wait(dve, it, sh - 1, 2)
                    nc.vector.tensor_copy(mparts[:, 0], mneg[:]).then_inc(mpart.sem, 1)
                    mpart.wait(dve, it, sh, 0)
                    nc.vector.tensor_tensor(mneg[:], mneg[:], mparts[:, 0], ALU.subtract).then_inc(mpart.sem, 1)
                    mpart.wait(dve, it, sh, 1)
                    nc.vector.tensor_copy(mparts[:, 1], mneg[:]).then_inc(mpart.sem, 1)
                    mpart.wait(dve, it, sh, 2)
                    nc.vector.tensor_tensor(mparts[:, 2], mneg[:], mparts[:, 1], ALU.subtract).then_inc(mpart.sem, 1)

                def G_(it, sh, live, n):
                    ps = next_a()
                    if not live:
                        return
                    if n == 0:
                        xnT_ready.wait(dve, it, sh, KC - 1)
                        nc.vector.tensor_reduce(pooled[:], xnT[(it[1] + sh) % 2][:].rearrange(
                            "p c (b t) -> p c b t", b=G), AX.X, ALU.add).then_inc(pool_ready.sem, 1)
                    elif n == 1:
                        def chained(e, ins):
                            ins.then_inc(gate.sem, 1)
                            gate.wait(dve, it, sh, e, alone=passed["dve"])

                        lg_filled.wait(dve, it, sh, 0)
                        chained(0, nc.vector.tensor_copy(lg[:], ps[0:G, 0:E]))
                        chained(1, nc.vector.max(top[:], lg[:]))
                        chained(2, nc.vector.max_index(topi[:], top[:], lg[:]))
                        chained(3, nc.vector.tensor_copy(topf[:], topi[:, 0:2]))
                        chained(4, nc.vector.tensor_tensor(gdiff[:], top[:, 1:2], top[:, 0:1], ALU.subtract))
                        gexp_ready.wait(dve, it, sh, 0)
                        chained(5, nc.vector.tensor_scalar(gden[:], gexp[:], 1.0, None, ALU.add))
                        chained(6, nc.vector.reciprocal(gval[:, 0:1], gden[:]))
                        chained(7, nc.vector.tensor_tensor(gval[:, 1:2], gexp[:], gval[:, 0:1], ALU.mult))
                        for n_ in range(2):
                            chained(8 + n_, nc.vector.tensor_scalar(
                                gsel[:, n_], k["iotaf"][:], topf[:, n_:n_ + 1], gval[:, n_:n_ + 1],
                                ALU.is_equal, ALU.mult))
                        chained(10, nc.vector.tensor_tensor(gates[:], gsel[:, 0], gsel[:, 1], ALU.add))
                        chained(11, nc.vector.tensor_copy(gwide[:], gates[:].unsqueeze(2).broadcast_to([G, E, R])))
                        nc.vector.tensor_copy(gdiff[:], gexp[:]).then_inc(gate.sem, 1)
                    else:
                        gt_filled.wait(dve, it, sh, 0)
                        for i in range(4):
                            nc.vector.tensor_scalar(cT[:, i, span(it, sh)], ps[:, 0:G], k["svals"][:, i:i + 1], None,
                                                    ALU.mult).then_inc(cT_ready.sem, 1)

                def XV(it, sh, live, n):
                    ps = next_a()
                    if live:
                        dst = xvs[n] if n < 2 else xvs_v[(it[1] + sh) % 2]
                        xv_filled.wait(dve, it, sh, n)
                        if n == 0:
                            cT_ready.wait(dve, it, sh, 3)
                        nc.vector.tensor_tensor(
                            dst[:].rearrange("p (b t) -> p b t", b=G), ps[:, 0:GT].rearrange("p (b t) -> p b t", b=G),
                            cT[:, n, span(it, sh)].unsqueeze(2).broadcast_to([128, G, T]), ALU.mult
                        ).then_inc(xvs_ready.sem, 1)

                def TN(it, sh, live, s):
                    if not live:
                        return
                    tn_filled.wait(dve, it, sh, s)
                    ps = psN[0:T].rearrange("p (h w) -> p h w", w=VW)
                    src = ps[:, :, HD]
                    if not mixture:
                        nc.vector.tensor_scalar(den[:], src, DEN_EPS, None, ALU.add).then_inc(den_ready.sem, 1)
                        den_ready.wait(dve, it, sh, s)
                        src = den[:]
                    nc.vector.reciprocal(rden[:], src).then_inc(rden_ready.sem, 1)
                    rden_ready.wait(dve, it, sh, s)
                    nc.vector.tensor_tensor(ctxt[:], ps[:, :, 0:HD], rden[:].unsqueeze(2).broadcast_to([T, HEADS, HD]),
                                            ALU.mult).then_inc(ctx_ready.sem, 1)

                def OV(it, sh, live, s):
                    if live:
                        ov_filled.wait(dve, it, sh, s)
                        nc.vector.tensor_scalar(xvo[:], psO[:, 0:T], cT[:, 3, span(it, sh)][:, s:s + 1]
                                                if it[0] is None else cT[:, 3, bass.ds(sample(it, sh, s), 1)],
                                                None, ALU.mult).then_inc(xvo_ready.sem, 1)

                def OUT(it, sh, live, s):
                    if live:
                        hb = hid[:, sample(it, sh, s)]
                        out_filled.wait(dve, it, sh, s)
                        if mixture and s == 0:
                            hob_ready.wait(dve, it, sh, 0)
                        nc.vector.tensor_tensor(hb, psO[0:T, 0:D], hb, ALU.add).then_inc(res_ready.sem, 1)

                part = dict(LN=LN, LNX=LNX, XT=XT, QK=QK, V=V, S=S, M=M, MT=MT, G=G_, XV=XV, TN=TN, OV=OV, OUT=OUT)

                def body(it):
                    for step in steps:
                        if step[0] in part:
                            sh, live = active(it, step)
                            if live or it[1] + sh < 0:
                                part[step[0]](it, sh, live, *step[1:])

                run_iterations(dve, body)

            @block.gpsimd
            def _(pool):
                for p in range(2):
                    nc.gpsimd.memset(v_ext[p][:], 0.0).then_inc(init, 1)
                    pool.wait_ge(init, 2 * p + 1)
                    nc.gpsimd.memset(v_ext[p][:, :, :, HD:HD + 1], 1.0).then_inc(init, 1)
                    pool.wait_ge(init, 2 * p + 2)
                if mixture:
                    for p in range(2):
                        nc.gpsimd.memset(pack[1][p][ROWS:ROWS + PARTS], 1.0).then_inc(init, 1)
                        pool.wait_ge(init, p + 5)

                def LN(it, sh, live):
                    if live:
                        ln_var.wait(pool, it, sh, 0)
                        nc.gpsimd.tensor_tensor(rstd[:], ve[:], k["lneps_half"][:], ALU.pow).then_inc(ln_rstd.sem, 1)

                def QK(it, sh, live, n):
                    tensor, cc = divmod(n, KC)
                    if not live or cc != KC - 1:
                        return
                    p1_ready.wait(pool, it, sh, tensor)
                    nc.gpsimd.tensor_tensor(qx[tensor][:], qx[tensor][:], parts[tensor][:, slot(tensor, 0)], ALU.subtract
                                            ).then_inc(r_ready.sem, 1)
                    p2_ready.wait(pool, it, sh, tensor)
                    nc.gpsimd.tensor_tensor(parts[tensor][:, slot(tensor, 2)], qx[tensor][:], parts[tensor][:, slot(tensor, 1)], ALU.subtract
                                            ).then_inc(p3_ready.sem, 1)

                def HB(it, sh, live):
                    if live:
                        hg = hid[:, span(it, sh)]
                        xn_ready.wait(pool, it, sh, G - 1)
                        nc.gpsimd.tensor_tensor(hg, hg, k["ob"][:].unsqueeze(1).broadcast_to([T, G, D]), ALU.add
                                                ).then_inc(hob_ready.sem, 1)

                part = dict(LN=LN, QK=QK, HB=HB)

                def body(it):
                    for step in steps:
                        if step[0] in part:
                            sh, live = active(it, step)
                            if live:
                                part[step[0]](it, sh, live, *step[1:])

                run_iterations(pool, body)

            @block.sync
            def _(sp):
                def PACK(it, sh):
                    par = (it[1] + sh) % 2
                    for n in range(2):
                        p3_ready.wait(sp, it, sh, n, alone=passed["sp"])
                        d = scratch[n][par].rearrange("r d h c t -> (d h) r (c t)")
                        sp.dma_start(d, parts[n][:].rearrange("p r c t -> p r (c t)")).then_inc(stored[n].sem, 16)
                    s_filled.wait(sp, it, sh - 2, 2 * G - 1, alone=passed["sp"])
                    for n in range(2):
                        stored[n].wait(sp, it, sh, 0, alone=passed["sp"])
                        src = scratch[n][par].rearrange("r d h c t -> (r d) (h c t)")
                        dst = pack[n][par][:].rearrange("p h t -> p (h t)")
                        first = 0 if n == 0 else HD
                        sp.dma_start(dst[0:3 * HD], src).then_inc(packed[n].sem(it, sh), 16)
                        sp.dma_start(dst[3 * HD:5 * HD], src[first:first + 2 * HD]).then_inc(packed[n].sem(it, sh), 16)
                        sp.dma_start(dst[5 * HD:6 * HD], src[2 * first:2 * first + HD]
                                     ).then_inc(packed[n].sem(it, sh), 16)

                def MT(it, sh):
                    par = (it[1] + sh) % 2
                    mpart.wait(sp, it, sh, 3, alone=passed["sp"])
                    for r in range(PARTS):
                        sp.dma_start(pack[0][par][ROWS + r:ROWS + r + 1].rearrange("p h t -> p (h t)"),
                                     mparts[:, r]).then_inc(mpacked.sem, 16)

                def STORE(it, sh):
                    res_ready.wait(sp, it, sh, G - 1, alone=passed["sp"])
                    bs = span(it, sh)
                    sp.dma_start(out[bs, IMG:T].rearrange("b t d -> t b d"), hid[0:TXT, bs]).then_inc(stores.sem, 16)
                    sp.dma_start(out[bs, 0:IMG].rearrange("b t d -> t b d"), hid[TXT:T, bs]).then_inc(stores.sem, 16)

                part = dict(PACK=PACK, MT=MT, STORE=STORE)

                def body(it):
                    for step in steps:
                        if step[0] in part:
                            sh, live = active(it, step)
                            if live:
                                part[step[0]](it, sh)

                run_iterations(sp, body)
                if mixture:
                    sp.wait_ge(stores.sem, 16 * 2 * NG)


def program(nc, A, out):
    with ExitStack() as c:
        k = {}

        def keep(name, shape, dt=F32):
            k[name] = c.enter_context(nc.sbuf_tensor(name, shape, dt))

        keep("hid", [T, B, D])
        keep("ident", [128, 128])
        keep("mask", [T, T])
        keep("lneps_half", [T, G])
        keep("iota", [G, E], I32)
        keep("iotaf", [G, E])
        keep("h1", [GH + 1, G])
        keep("gw1T", [128, KC, GH])
        keep("gw2T", [GH + 1, E])
        keep("gb1", [GH, 1])
        keep("svals", [ER, 4])
        keep("bias_q", [128, KC])
        keep("bias_qs", [128, KC])
        keep("bias_k", [128, KC])
        keep("bias_v", [128, KC])
        keep("ob", [T, D])
        for n in PROJ:
            keep(f"lw_{n}", [128, KC, D])
            keep(f"mT_{n}", [128, KC, D])
            keep(f"vT_{n}", [128, KC, ER])
            keep(f"uT_{n}", [ER, D])
        embed(nc, c, A, k)
        attention(nc, A, k, out, mixture=False)
        attention(nc, A, k, out, mixture=True)


def kernel(**inputs):
    import numpy as np
    import concourse.bacc as bacc
    from concourse.bass_utils import run_bass_kernel_spmd

    nc = bacc.Bacc("TRN2", target_bir_lowering=False, num_devices=1)
    arrays, aps = {}, {}
    for name, value in inputs.items():
        a = np.ascontiguousarray(value)
        arrays[f"in_{name}"] = a
        aps[name.removeprefix("L0_")] = nc.dram_tensor(f"in_{name}", a.shape, mybir.dt.from_np(a.dtype),
                                                       kind="ExternalInput").ap()
    out = nc.dram_tensor("out", (B, T, D), F32, kind="ExternalOutput").ap()
    program(nc, aps, out)
    return run_bass_kernel_spmd(nc, [arrays], core_ids=[0]).results[0]["out"]
```

```python
from contextlib import ExitStack

import concourse.bass as bass
from concourse import mybir

F32 = mybir.dt.float32
BF16 = mybir.dt.bfloat16
I32 = mybir.dt.int32
U32 = mybir.dt.uint32
ALU = mybir.AluOpType
ACT = mybir.ActivationFunctionType
AX = mybir.AxisListType

B = 32
D = 256
KC = D // 128
HEADS, HD = 16, 16
HALF_HEADS = HEADS // 2
PATCH, CH, SIDE = 16, 3, 96
GRID = SIDE // PATCH
NP = GRID * GRID
PD = CH * PATCH * PATCH
PCH = PD // 128
TXT = 77
IMG = NP + 1
T = TXT + IMG
G = 4
GT = G * T
NG = B // G
NB = 4
GATHER_P = 112
GATHER_N = B * TXT // GATHER_P
E, R, GH = 8, 16, 64
ER = E * R
VW = 32
LN_EPS = 1e-5
DEN_EPS = 1e-6
Q_SCALE = HD ** -0.5
PROJ = ("q", "k", "v", "o")
PARTS = 3
ROWS = 6 * HD


class Event:

    def __init__(self, sem, per_group=1, unit=1, first=0, bias=0):
        self.sem, self.per_group, self.unit, self.first, self.bias = sem, per_group, unit, first, bias

    def of(self, it, shift):
        return self

    def wait(self, eng, it, shift, n, alone=None):
        j, base = it
        done = self.per_group * (base + shift - self.first) + n + 1
        v = self.unit * done + self.bias
        if j is None:
            if done > 0:
                eng.wait_ge(self.sem, v)
            return
        assert v > 0
        eng.wait_ge(self.sem, j * (2 * self.unit * self.per_group) + v)
        if alone is not None:
            eng.sem_inc(alone, 1)


class LayerEvent:

    def __init__(self, linear, mixture, per_group):
        self.events = (Event(linear, per_group), Event(mixture, per_group, first=NG))

    def of(self, it, shift):
        return self.events[is_mixture(it, shift)]

    def wait(self, eng, it, shift, n, alone=None):
        self.of(it, shift).wait(eng, it, shift, n, alone)


class ParityEvent:

    def __init__(self, sems, per_group):
        self.sems, self.per_group = sems, per_group

    def sem(self, it, shift):
        return self.sems[(it[1] + shift) % 2]

    def wait(self, eng, it, shift):
        j, base = it
        v = 16 * self.per_group * ((base + shift) // 2 + 1)
        if j is not None or v > 0:
            eng.wait_ge(self.sem(it, shift), v if j is None else j * (16 * self.per_group) + v)


def is_mixture(it, shift):
    return it[1] + shift >= NG


def sample(it, shift, s):
    j, base = it
    b = G * (base + shift - NG * is_mixture(it, shift)) + s
    return b if j is None else j * (2 * G) + b


def span(it, shift, n=G):
    b = sample(it, shift, 0)
    return slice(b, b + n) if isinstance(b, int) else bass.ds(b, n)


def slot(tensor, r):
    return r if tensor == 0 else PARTS - 1 - r


def run_iterations(eng, body):
    body((None, -2))
    body((None, -1))
    for first in (0, NG):
        with eng.Fori(0, (NG - 2) // 2) as j:
            body((j, first))
            body((j, first + 1))
        body((None, first + NG - 2))
        body((None, first + NG - 1))


def steps_of(it):
    found = []
    for name, *args in LINEAR_STEPS if it[1] < NG - 2 else MIXTURE_STEPS:
        if name in ("S", "SX"):
            shift = 1 if args[0] == G else 0
        elif name.endswith("+"):
            name, shift = name[:-1], 1
            if not is_mixture(it, shift):
                continue
        else:
            shift = GROUP_OF[name]
        group = it[1] + shift
        if it[0] is None and group >= 2 * NG or name in MIXTURE_ONLY and not is_mixture(it, shift):
            continue
        found.append((name, args, shift, it[0] is not None or group >= 0))
    return found




def embed(nc, ctx, A, k):
    with ExitStack() as c:
        def sb(name, shape, dt=F32):
            return c.enter_context(nc.sbuf_tensor(name, shape, dt))

        def sem(name):
            return c.enter_context(nc.semaphore(name))

        HB = B // 2
        PR = HB * GRID
        ximg = [sb(f"ximg{h}", [PR, CH, PATCH, SIDE]) for h in range(2)]
        pstat = sb("pstat", [PR, 2, GRID, 2, 6])
        pmv = sb("pmv", [PR, 2, GRID, 2])
        pve = sb("pve", [PR, 2, GRID])
        prs = sb("prs", [PR, 2, GRID])
        nhalf = sb("nhalf", [PR, GRID])
        patch = sb("patch", [PR, GRID, PD])
        xT = sb("xT", [128, 2, PCH, PR])
        wraw = sb("wraw", [128, PCH, D])
        wg = sb("wg", [128, PCH, D])
        g1 = sb("g1", [128, PCH])
        b1 = sb("b1", [128, PCH])
        b1b = sb("b1b", [128, PCH, 128])
        bproj = sb("bproj", [PR, D])
        ybias = sb("ybias", [PR, D])
        y = sb("y", [PR, GRID, D])
        ystat = sb("ystat", [PR, GRID, 6])
        ymv = sb("ymv", [PR, GRID, 2])
        yve = sb("yve", [PR, GRID])
        yrs = sb("yrs", [PR, GRID])
        g2 = sb("g2", [PR, D])
        b2 = sb("b2", [PR, D])
        pos = sb("pos", [PR, GRID, D])
        cls = sb("cls", [B, 2, D])
        cls_out = sb("cls_out", [B, D])
        idx = sb("idx", [GATHER_P, GATHER_N], I32)
        coef = sb("coef", [GATHER_P, GATHER_N, NB])
        cmax = sb("cmax", [GATHER_P, GATHER_N])
        csum = sb("csum", [GATHER_P, GATHER_N])
        crec = sb("crec", [GATHER_P, GATHER_N])
        coefT = sb("coefT", [NB + 1, B * TXT])
        base = sb("base", [NB + 1, D])
        lang = sb("lang", [NB + 1, D])
        bscale = sb("bscale", [NB + 1, 1])
        base5 = sb("base5", [NB + 1, D])
        lin_raw = {n: sb(f"lraw_{n}", [128, KC, D]) for n in ("q", "k")}
        m_raw = {n: sb(f"mraw_{n}", [128, KC, D]) for n in PROJ}
        u_raw = {n: sb(f"uraw_{n}", [128, KC, ER]) for n in PROJ}
        v_raw = {n: sb(f"vraw_{n}", [ER, D]) for n in PROJ}
        gw1_raw = sb("gw1_raw", [GH, D])
        gw2_raw = sb("gw2_raw", [E, GH])
        psX = [c.enter_context(nc.psum_tensor(f"psX{n}", [128, 512], F32)) for n in range(4)]
        psY = [c.enter_context(nc.psum_tensor(f"psY{n}", [128, 512], F32)) for n in range(2)]
        psW = [c.enter_context(nc.psum_tensor(f"psW{n}", [128, 512], F32)) for n in range(2)]
        tok = nc.dram_tensor("tok_scratch", (B, IMG, D), F32).ap()

        x_loaded = [sem("x_loaded0"), sem("x_loaded1")]
        tokw_loaded = sem("tokw_loaded")
        tokc_loaded = sem("tokc_loaded")
        mat_loaded = {n: sem(f"mat_loaded_{n}") for n in PROJ}
        gate_loaded = sem("gate_loaded")
        lin_loaded = sem("lin_loaded")
        rest_loaded = sem("rest_loaded")
        base_loaded = sem("base_loaded")
        cls_loaded = sem("cls_loaded")
        idx_loaded = sem("idx_loaded")
        gathered = sem("gathered")
        tok_stored = sem("tok_stored")
        tok_loaded = sem("tok_loaded")
        const_ready = sem("const_ready")
        wprep = sem("wprep")
        b1_ready = sem("b1_ready")
        pst = sem("pst")
        prs_ready = sem("prs_ready")
        xnorm = sem("xnorm")
        yb_filled, yb_ready = sem("yb_filled"), sem("yb_ready")
        xt_filled, xt_ready = sem("xt_filled_e"), sem("xt_ready_e")
        y_filled, y_ready = sem("y_filled"), sem("y_ready")
        yst = sem("yst")
        yrs_ready = sem("yrs_ready")
        yn = sem("yn")
        z_ready = sem("z_ready")
        wt_filled, wt_ready = sem("wt_filled"), sem("wt_ready")
        cls_ready = sem("cls_ready")
        soft = sem("soft")
        cexp = sem("cexp")
        base_ready = sem("base_ready")
        ct_filled, ct_ready = sem("ct_filled"), sem("ct_ready")
        txt_filled, txt_ready = sem("txt_filled"), sem("txt_ready")

        NCT = -(-GATHER_N // G)

        with nc.Block() as block:
            @block.sync
            def _(sp):
                for h in range(2):
                    for ch in range(CH):
                        sp.dma_start(ximg[h][:, ch].rearrange("p y x -> p (y x)"),
                                     A["x"][h * HB:(h + 1) * HB, ch].rearrange("b (h y) x -> b h (y x)", h=GRID)
                                     ).then_inc(x_loaded[h], 16)
                for ch in range(CH):
                    sp.dma_start(wraw[:, 2 * ch:2 * ch + 2],
                                 A["tok_W_proj"].rearrange("(h p c) e -> c p h e", c=CH, h=2)[ch]
                                 ).then_inc(tokw_loaded, 16)
                for t, name in ((g1, "tok_ln1_g"), (b1, "tok_ln1_b")):
                    sp.dma_start(t[:].rearrange("p (c h) -> p c h", c=CH),
                                 A[name].rearrange("(h p c) -> p c h", c=CH, h=2),
                                 allow_slow_non_contiguous=True).then_inc(tokw_loaded, 16)
                for t, name in ((bproj, "tok_b_proj"), (g2, "tok_ln2_g"), (b2, "tok_ln2_b")):
                    sp.dma_start(t[:], A[name].partition_broadcast(PR)).then_inc(tokc_loaded, 16)
                patch_pos = A["tok_pos_emb"][0, 1:IMG].rearrange("(h w) e -> h w e", h=GRID)
                sp.dma_start(pos[:], patch_pos.unsqueeze(0).broadcast_to([HB, GRID, GRID, D])
                             ).then_inc(tokc_loaded, 16)
                sp.dma_start(cls[:, 0], A["tok_cls_token"][0, 0].partition_broadcast(B)).then_inc(cls_loaded, 16)
                sp.dma_start(cls[:, 1], A["tok_pos_emb"][0, 0].partition_broadcast(B)).then_inc(cls_loaded, 16)
                sp.wait_ge(cls_ready, 1)
                sp.dma_start(tok[:, 0], cls_out[:]).then_inc(tok_stored, 16)
                for h in range(2):
                    sp.wait_ge(z_ready, h + 1)
                    sp.dma_start(tok[h * HB:(h + 1) * HB, 1:].rearrange("b (h w) e -> b h (w e)", h=GRID),
                                 y[:].rearrange("p w e -> p (w e)")).then_inc(tok_stored, 16)
                    sp.wait_ge(tok_stored, 16 * (h + 2))
                    sp.dma_start(k["hid"][TXT:T, h * HB:(h + 1) * HB],
                                 tok[h * HB:(h + 1) * HB].rearrange("b n e -> n b e")).then_inc(tok_loaded, 16)
                sp.wait_ge(tok_loaded, 32)

            @block.scalar
            def _(act):
                act.dma_start(base[0:NB], A["txt_base_embed_weight"]).then_inc(base_loaded, 16)
                act.dma_start(base[NB:NB + 1], A["txt_lang_bias"][2:3]).then_inc(base_loaded, 16)
                act.wait_ge(const_ready, 2)
                act.dma_start(lang[0:NB], A["txt_lang_bias"]).then_inc(base_loaded, 16)
                for n in PROJ:
                    act.dma_start(m_raw[n][:], A[f"ffn_{n}Wm"].rearrange("(c p) d -> p c d", p=128)
                                  ).then_inc(mat_loaded[n], 16)
                    act.dma_start(v_raw[n][:], A[f"ffn_{n}V"].rearrange("e r d -> (e r) d")
                                  ).then_inc(mat_loaded[n], 16)
                    for oc in range(KC):
                        act.dma_start(u_raw[n][:, oc].rearrange("p (e r) -> p e r", e=E),
                                      A[f"ffn_{n}U"][:, oc * 128:(oc + 1) * 128].rearrange("e p r -> p e r")
                                      ).then_inc(mat_loaded[n], 16)
                act.dma_start(gw1_raw[:], A["ffn_gw1"]).then_inc(gate_loaded, 16)
                act.dma_start(gw2_raw[:], A["ffn_gw2"]).then_inc(gate_loaded, 16)
                for n in ("q", "k"):
                    act.dma_start(lin_raw[n][:], A[f"attn_w{n}"].rearrange("(c p) e -> p c e", p=128)
                                  ).then_inc(lin_loaded, 16)
                for n in ("v", "o"):
                    act.dma_start(k[f"lw_{n}"][:], A[f"attn_w{n}"].rearrange("(c p) e -> p c e", p=128)
                                  ).then_inc(rest_loaded, 16)
                act.dma_start(k["gw2T"][GH:GH + 1], A["ffn_gb2"].partition_broadcast(1)).then_inc(rest_loaded, 16)
                act.dma_start(k["gb1"][:], A["ffn_gb1"].unsqueeze(1)).then_inc(rest_loaded, 16)
                for i, n in enumerate(PROJ):
                    act.dma_start(k["svals"][:, i:i + 1], A[f"ffn_{n}S"].rearrange("e r -> (e r)").unsqueeze(1)
                                  ).then_inc(rest_loaded, 16)
                for n in ("q", "k"):
                    for cc in range(KC):
                        act.dma_start(k[f"bias_{n}"][:, cc:cc + 1],
                                      A[f"ffn_{n}b"][cc * 128:(cc + 1) * 128].rearrange("(h d o) -> d h o", d=HD, o=1),
                                      allow_slow_non_contiguous=True).then_inc(rest_loaded, 16)
                act.dma_start(k["bias_v"][:], A["ffn_vb"].rearrange("(c p) -> p c", p=128),
                              allow_slow_non_contiguous=True).then_inc(rest_loaded, 16)
                act.dma_start(k["ob"][:], A["ffn_ob"].partition_broadcast(T)).then_inc(rest_loaded, 16)
                for i, n in enumerate(PROJ):
                    act.wait_ge(wt_filled, 2 * i + 1)
                    src = psW[0][:]
                    dst = k[f"mT_{n}"][:].rearrange("p c o -> p (c o)")
                    if n in "qk":
                        src = src.rearrange("p (a h d) -> p a h d", a=2 * KC, h=HALF_HEADS)
                        dst = dst.rearrange("p (a d h) -> p a h d", a=2 * KC, h=HALF_HEADS)
                    nc.scalar.activation(dst, src, ACT.Copy).then_inc(wt_ready, 1)
                    act.wait_ge(wt_filled, 2 * i + 2)
                    nc.scalar.activation(k[f"vT_{n}"][:].rearrange("p c r -> p (c r)"), psW[1][:, 0:256],
                                         ACT.Copy).then_inc(wt_ready, 1)
                    src, dst = psW[1][:, 256:512], k[f"uT_{n}"][:]
                    if n in "qk":
                        src = src.rearrange("p (a h d) -> p a h d", a=KC, h=HALF_HEADS)
                        dst = dst.rearrange("p (a d h) -> p a h d", a=KC, h=HALF_HEADS)
                    nc.scalar.activation(dst, src, ACT.Copy).then_inc(wt_ready, 1)
                act.wait_ge(wt_filled, 9)
                nc.scalar.activation(k["gw1T"][:].rearrange("p c g -> p (c g)"), psW[0][:, 0:KC * GH],
                                     ACT.Copy).then_inc(wt_ready, 1)
                nc.scalar.activation(k["gw2T"][0:GH], psW[0][0:GH, 128:128 + E], ACT.Copy).then_inc(wt_ready, 1)
                for n in range(2 * GRID):
                    for a in range(2):
                        act.wait_ge(xt_filled, 2 * n + a + 1)
                        if n >= 2:
                            act.wait_ge(y_filled, n - 1)
                        nc.scalar.activation(xT[:, n % 2, 3 * a:3 * a + 3].rearrange("p c r -> p (c r)"),
                                             psX[2 * (n % 2) + a][:, 0:3 * PR], ACT.Copy).then_inc(xt_ready, 1)
                act.wait_ge(soft, 2)
                nc.scalar.activation(coef[:], coef[:], ACT.Exp).then_inc(cexp, 1)
                for n in range(B // 2):
                    act.wait_ge(txt_filled, n + 1)
                    nc.scalar.activation(k["hid"][0:TXT, 2 * n:2 * n + 2].rearrange("p b e -> p (b e)"),
                                         psY[n % 2][0:TXT], ACT.Copy).then_inc(txt_ready, 1)
                act.wait_ge(rest_loaded, 16 * (2 + 2 + 4 + 4 + 2))

            @block.gpsimd
            def _(pool):
                pool.dma_start(idx[:], A["x_txt"].rearrange("b t -> (b t)").rearrange("(p n) -> p n", p=GATHER_P)
                               ).then_inc(idx_loaded, 16)
                nc.gpsimd.memset(nhalf[:], -0.5).then_inc(const_ready, 1)
                nc.gpsimd.memset(lang[:], 0.0).then_inc(const_ready, 1)
                nc.gpsimd.memset(bscale[:], 0.1).then_inc(const_ready, 1)
                nc.gpsimd.memset(k["ident"][:], 0.0).then_inc(const_ready, 1)
                pool.wait_ge(const_ready, 4)
                nc.gpsimd.affine_select(out=k["ident"][:], in_=k["ident"][:], compare_op=ALU.not_equal, fill=1.0,
                                        base=0, pattern=[[-1, 128]], channel_multiplier=1).then_inc(const_ready, 1)
                nc.gpsimd.affine_select(out=bscale[:], in_=bscale[:], compare_op=ALU.is_ge, fill=float(D) ** 0.5,
                                        base=-NB, pattern=[[0, 1]], channel_multiplier=1).then_inc(const_ready, 1)
                pool.wait_ge(idx_loaded, 16)
                for n in range(GATHER_N):
                    nc.gpsimd.indirect_dma_start(
                        coef[:, n], None, A["txt_coeff_weight"],
                        bass.IndirectOffsetOnAxis(ap=idx[:, n:n + 1], axis=0)).then_inc(gathered, 16)
                nc.gpsimd.memset(k["mask"][:], 1.0).then_inc(const_ready, 1)
                nc.gpsimd.memset(k["lneps_half"][:], -0.5).then_inc(const_ready, 1)
                nc.gpsimd.memset(coefT[:], 1.0).then_inc(const_ready, 1)
                nc.gpsimd.memset(k["h1"][:], 1.0).then_inc(const_ready, 1)
                pool.wait_ge(const_ready, 10)
                nc.gpsimd.affine_select(out=k["mask"][0:TXT, 0:TXT], in_=k["mask"][0:TXT, 0:TXT],
                                        compare_op=ALU.is_ge, fill=0.0, base=0, pattern=[[1, TXT]],
                                        channel_multiplier=-1).then_inc(const_ready, 1)
                nc.gpsimd.affine_select(out=k["mask"][:, TXT:T], in_=k["mask"][:, TXT:T],
                                        compare_op=ALU.is_ge, fill=0.0, base=TXT, pattern=[[1, IMG]],
                                        channel_multiplier=-1).then_inc(const_ready, 1)
                pool.wait_ge(const_ready, 12)
                nc.gpsimd.affine_select(out=k["mask"][:, TXT:T], in_=k["mask"][:, TXT:T],
                                        compare_op=ALU.is_ge, fill=0.0, base=-TXT, pattern=[[0, IMG]],
                                        channel_multiplier=1).then_inc(const_ready, 1)
                nc.gpsimd.iota(k["iota"][:], pattern=[[1, E]], base=0, channel_multiplier=0).then_inc(const_ready, 1)
                pool.wait_ge(const_ready, 14)
                nc.gpsimd.tensor_copy(k["iotaf"][:], k["iota"][:]).then_inc(const_ready, 1)
                for p in range(2):
                    nc.gpsimd.memset(k[f"v_ext{p}"][:], 0.0).then_inc(const_ready, 1)
                pool.wait_ge(const_ready, 17)
                for p in range(2):
                    nc.gpsimd.memset(k[f"v_ext{p}"][:, :, :, HD:HD + 1], 1.0).then_inc(const_ready, 1)
                pool.wait_ge(const_ready, 19)
                for h in range(2):
                    pool.wait_ge(pst, 19 * h + 19)
                    nc.gpsimd.tensor_tensor(prs[:, h], pve[:, h], nhalf[:], ALU.pow).then_inc(prs_ready, 1)
                for h in range(2):
                    pool.wait_ge(yst, 13 * h + 13)
                    nc.gpsimd.tensor_tensor(yrs[:], yve[:], nhalf[:], ALU.pow).then_inc(yrs_ready, 1)

            @block.vector
            def _(dve):
                def patch_stats(h):
                    dve.wait_ge(x_loaded[h], 16 * CH)
                    for w in range(GRID):
                        for a in range(2):
                            nc.vector.bn_stats(pstat[:, h, w, a],
                                               ximg[h][:, :, a * 8:a * 8 + 8, w * PATCH:(w + 1) * PATCH]
                                               ).then_inc(pst, 1)
                    dve.wait_ge(pst, 19 * h + 12)
                    for w in range(GRID):
                        nc.vector.bn_aggr(pmv[:, h, w], pstat[:, h, w].rearrange("p a s -> p (a s)")
                                          ).then_inc(pst, 1)
                    dve.wait_ge(pst, 19 * h + 18)
                    nc.vector.tensor_scalar(pve[:, h], pmv[:, h, :, 1], LN_EPS, None, ALU.add).then_inc(pst, 1)

                def patch_norm(h, ws=range(GRID)):
                    dve.wait_ge(prs_ready, h + 1)
                    for w in ws:
                        if h:
                            dve.wait_ge(xt_filled, 2 * (w + 1))
                        xs = ximg[h][:, :, :, w * PATCH:(w + 1) * PATCH]
                        nc.vector.tensor_scalar(patch[:, w].rearrange("p (c y x) -> p c y x", c=CH, y=PATCH), xs, pmv[:, h, w, 0:1], prs[:, h, w:w + 1],
                                                ALU.subtract, ALU.mult).then_inc(xnorm, 1)

                dve.wait_ge(tokw_loaded, 16 * (CH + 2))
                nc.vector.tensor_tensor(wg[:], wraw[:], g1[:].unsqueeze(2).broadcast_to([128, PCH, D]),
                                        ALU.mult).then_inc(wprep, 1)
                nc.vector.tensor_copy(b1b[:], b1[:].unsqueeze(2).broadcast_to([128, PCH, 128])).then_inc(b1_ready, 1)
                patch_stats(0)
                patch_stats(1)
                patch_norm(0)
                dve.wait_ge(lin_loaded, 32)
                for n in ("q", "k"):
                    nc.vector.tensor_copy(k[f"lw_{n}"][:].rearrange("p c (a d h) -> p (c a) h d", a=KC, h=HALF_HEADS),
                                          lin_raw[n][:].rearrange("p c (a h d) -> p (c a) h d", a=KC, h=HALF_HEADS)
                                          ).then_inc(wprep, 1)
                dve.wait_ge(cls_loaded, 32)
                nc.vector.tensor_tensor(cls_out[:], cls[:, 0], cls[:, 1], ALU.add).then_inc(cls_ready, 1)
                dve.wait_ge(tokc_loaded, 64)
                nc.vector.tensor_tensor(pos[:], pos[:], b2[:].unsqueeze(1).broadcast_to([PR, GRID, D]),
                                        ALU.add).then_inc(yb_ready, 1)
                dve.wait_ge(yb_filled, 1)
                nc.vector.tensor_tensor(ybias[:], psY[0][0:PR, 0:D], bproj[:], ALU.add).then_inc(yb_ready, 1)
                dve.wait_ge(yb_ready, 2)
                for h in range(2):
                    if h:
                        dve.wait_ge(tok_stored, 32)
                    for w in range(GRID):
                        n = GRID * h + w
                        if h == 0:
                            patch_norm(1, [w])
                        dve.wait_ge(y_filled, n + 1)
                        nc.vector.tensor_tensor(y[:, w], psY[n % 2][0:PR, 0:D], ybias[:], ALU.add).then_inc(y_ready, 1)
                        dve.wait_ge(y_ready, n + 1)
                        nc.vector.bn_stats(ystat[:, w], y[:, w]).then_inc(yst, 1)
                    dve.wait_ge(yst, 13 * h + 6)
                    for w in range(GRID):
                        nc.vector.bn_aggr(ymv[:, w], ystat[:, w]).then_inc(yst, 1)
                    dve.wait_ge(yst, 13 * h + 12)
                    nc.vector.tensor_scalar(yve[:], ymv[:, :, 1], LN_EPS, None, ALU.add).then_inc(yst, 1)
                    dve.wait_ge(yrs_ready, h + 1)
                    for w in range(GRID):
                        nc.vector.tensor_scalar(y[:, w], y[:, w], ymv[:, w, 0:1], yrs[:, w:w + 1],
                                                ALU.subtract, ALU.mult).then_inc(yn, 1)
                    dve.wait_ge(yn, 7 * h + 6)
                    nc.vector.tensor_tensor(y[:], y[:], g2[:].unsqueeze(1).broadcast_to([PR, GRID, D]),
                                            ALU.mult).then_inc(yn, 1)
                    dve.wait_ge(yn, 7 * h + 7)
                    nc.vector.tensor_tensor(y[:], y[:], pos[:], ALU.add).then_inc(z_ready, 1)
                dve.wait_ge(gathered, 16 * GATHER_N)
                nc.vector.tensor_reduce(cmax[:], coef[:], AX.X, ALU.max).then_inc(soft, 1)
                dve.wait_ge(soft, 1)
                cb = [GATHER_P, GATHER_N, NB]
                nc.vector.tensor_tensor(coef[:], coef[:], cmax[:].unsqueeze(2).broadcast_to(cb),
                                        ALU.subtract).then_inc(soft, 1)
                dve.wait_ge(cexp, 1)
                nc.vector.tensor_reduce(csum[:], coef[:], AX.X, ALU.add).then_inc(soft, 1)
                dve.wait_ge(soft, 3)
                nc.vector.reciprocal(crec[:], csum[:]).then_inc(soft, 1)
                dve.wait_ge(soft, 4)
                nc.vector.tensor_tensor(coef[:], coef[:], crec[:].unsqueeze(2).broadcast_to(cb),
                                        ALU.mult).then_inc(soft, 1)
                dve.wait_ge(base_loaded, 48)
                dve.wait_ge(const_ready, 15)
                nc.vector.tensor_tensor(base5[:], base[:], lang[:], ALU.add).then_inc(base_ready, 1)
                dve.wait_ge(base_ready, 1)
                nc.vector.tensor_scalar(base5[:], base5[:], bscale[:, 0:1], None, ALU.mult).then_inc(base_ready, 1)
                cT = coefT[0:NB].rearrange("q (p n) -> q n p", n=GATHER_N)
                for m in range(NCT):
                    w = min(G, GATHER_N - G * m)
                    dve.wait_ge(ct_filled, m + 1)
                    nc.vector.tensor_copy(cT[:, G * m:G * m + w],
                                          psW[m % 2][0:NB, 0:w * GATHER_P].rearrange("q (n p) -> q n p", n=w)
                                          ).then_inc(ct_ready, 1)

            @block.tensor
            def _(pe):
                pe.wait_ge(const_ready, 5)
                ident = k["ident"]
                for i, n in enumerate(PROJ):
                    pe.wait_ge(mat_loaded[n], 64)
                    if i:
                        pe.wait_ge(wt_ready, 3 * i - 2)
                    for kc in range(KC):
                        for oc in range(KC):
                            at = (kc * KC + oc) * 128
                            mm = nc.tensor.transpose(psW[0][:, at:at + 128],
                                                     m_raw[n][:, oc, kc * 128:(kc + 1) * 128], ident[:])
                    mm.then_inc(wt_filled, 1)
                    if i:
                        pe.wait_ge(wt_ready, 3 * i)
                    for kc in range(KC):
                        nc.tensor.transpose(psW[1][:, kc * 128:(kc + 1) * 128],
                                            v_raw[n][:, kc * 128:(kc + 1) * 128], ident[:])
                    for oc in range(KC):
                        mm = nc.tensor.transpose(psW[1][:, 256 + oc * 128:384 + oc * 128], u_raw[n][:, oc], ident[:])
                    mm.then_inc(wt_filled, 1)
                pe.wait_ge(gate_loaded, 32)
                pe.wait_ge(wt_ready, 10)
                for kc in range(KC):
                    nc.tensor.transpose(psW[0][:, kc * GH:(kc + 1) * GH], gw1_raw[:, kc * 128:(kc + 1) * 128],
                                        ident[0:GH, 0:GH])
                nc.tensor.transpose(psW[0][0:GH, 128:128 + E], gw2_raw[:], ident[0:E, 0:E]).then_inc(wt_filled, 1)
                pe.wait_ge(b1_ready, 1)
                pe.wait_ge(tokw_loaded, 16 * (CH + 2))
                for kc in range(PCH):
                    mm = nc.tensor.matmul(psY[0][:, 0:D], b1b[:, kc], wraw[:, kc], start=(kc == 0),
                                          stop=(kc == PCH - 1))
                mm.then_inc(yb_filled, 1)
                pe.wait_ge(wprep, 1)

                def patch_transposes(n):
                    h, w = divmod(n, GRID)
                    pe.wait_ge(xnorm, n + 1)
                    for a in range(2):
                        if n >= 2:
                            pe.wait_ge(xt_ready, 2 * (n - 2) + a + 1)
                        for i in range(3):
                            mm = nc.tensor.transpose(psX[2 * (n % 2) + a][:, i * PR:(i + 1) * PR],
                                                     patch[:, w, (3 * a + i) * 128:(3 * a + i + 1) * 128],
                                                     ident[0:PR, 0:PR])
                        mm.then_inc(xt_filled, 1)

                patch_transposes(0)
                for n in range(2 * GRID):
                    if n + 1 < 2 * GRID:
                        patch_transposes(n + 1)
                    pe.wait_ge(xt_ready, 2 * n + 2)
                    if n == 0:
                        pe.wait_ge(yb_ready, 2)
                    if n >= 2:
                        pe.wait_ge(y_ready, n - 1)
                    for kc in range(PCH):
                        mm = nc.tensor.matmul(psY[n % 2][0:PR, 0:D], xT[:, n % 2, kc], wg[:, kc], start=(kc == 0),
                                              stop=(kc == PCH - 1))
                    mm.then_inc(y_filled, 1)
                pe.wait_ge(soft, 5)
                pe.wait_ge(wt_ready, 14)
                for m in range(NCT):
                    if m >= 2:
                        pe.wait_ge(ct_ready, m - 1)
                    for i in range(min(G, GATHER_N - G * m)):
                        mm = nc.tensor.transpose(psW[m % 2][0:NB, i * GATHER_P:(i + 1) * GATHER_P],
                                                 coef[:, G * m + i], ident[0:GATHER_P, 0:GATHER_P])
                    mm.then_inc(ct_filled, 1)
                pe.wait_ge(ct_ready, NCT)
                pe.wait_ge(base_ready, 2)
                pe.wait_ge(y_ready, 2 * GRID)
                for n in range(B // 2):
                    if n >= 2:
                        pe.wait_ge(txt_ready, n - 1)
                    for i in range(2):
                        b = 2 * n + i
                        mm = nc.tensor.matmul(psY[n % 2][0:TXT, i * D:(i + 1) * D],
                                              coefT[:, b * TXT:(b + 1) * TXT], base5[:], start=True, stop=True)
                    mm.then_inc(txt_filled, 1)



LINEAR_STEPS = (
    ("LN",),
    ("AV", 0), ("S", 1), ("SX", 1, 0), ("TN", 0), ("V", 0), ("LNX",), ("TC", 0), ("SX", 1, 1), ("V", 1),
    ("AV", 1), ("S", 2), ("SX", 2, 0), ("TN", 1), ("OUT", 0), ("XT",), ("TC", 1), ("SX", 2, 1), ("QK", 0),
    ("AV", 2), ("S", 3), ("SX", 3, 0), ("TN", 2), ("OUT", 1), ("QK", 1), ("TC", 2), ("SX", 3, 1), ("P", 0), ("QK", 2),
    ("AV", 3), ("S", 4), ("SX", 4, 0), ("TN", 3), ("OUT", 2), ("D", 0), ("SX", 4, 1), ("PACK", 0), ("TC", 3),
    ("QK", 3), ("P", 1), ("OUT", 3), ("D", 1), ("PACK", 1),
)
MIXTURE_STEPS = (
    ("LN",), ("HB",),
    ("AV", 0), ("S", 1), ("SX", 1, 0), ("SX", 1, 1), ("D+", 1), ("TN", 0), ("V", 0), ("LNX",), ("TC", 0),
    ("PACK+", 1), ("XT",), ("OV", 0),
    ("AV", 1), ("S", 2), ("SX", 2, 0), ("SX", 2, 1), ("TN", 1), ("OUT", 0), ("V", 1), ("G", 0), ("TC", 1), ("G", 1),
    ("M", 0), ("OV", 1),
    ("AV", 2), ("S", 3), ("SX", 3, 0), ("SX", 3, 1), ("TN", 2), ("OUT", 1), ("G", 2), ("XV", 0), ("TC", 2),
    ("M", 1), ("XV", 1), ("OV", 2), ("M", 2), ("QK", 0),
    ("AV", 3), ("M", 3), ("TN", 3), ("OUT", 2), ("QK", 1), ("TC", 3), ("MT",), ("P", 0), ("XV", 2), ("OV", 3),
    ("QK", 2), ("D", 0), ("OUT", 3), ("PACK", 0), ("S", 4), ("SX", 4, 0), ("SX", 4, 1), ("QK", 3), ("P", 1),
    ("STORE",),
)
GROUP_OF = dict(LN=2, LNX=2, XT=2, QK=2, P=2, D=2, PACK=2, G=2, XV=2, V=1, M=1, MT=1, HB=1,
                AV=0, TN=0, TC=0, OV=0, OUT=0, STORE=0)
MIXTURE_ONLY = ("HB", "G", "XV", "M", "MT", "OV", "STORE")


def attention(nc, A, k, out):
    with ExitStack() as c:
        def sb(name, shape, dt=F32):
            return c.enter_context(nc.sbuf_tensor(f"a_{name}", shape, dt))

        def psum(name, shape):
            return c.enter_context(nc.psum_tensor(f"a_{name}", shape, F32))

        def sem(name):
            return c.enter_context(nc.semaphore(f"a_{name}"))

        def event(name, per_group=1, unit=1, first=0, bias=0):
            return Event(sem(name), per_group, unit, first, bias)

        def layer_event(name, per_group):
            return LayerEvent(sem(f"{name}_lin"), sem(f"{name}_mix"), per_group)

        hid, ident = k["hid"], k["ident"]
        v_ext = [k["v_ext0"], k["v_ext1"]]
        stat = sb("stat", [T, G, 6])
        mv = sb("mv", [T, G, 2])
        ve = sb("ve", [T, G])
        rstd = sb("rstd", [T, G])
        xn = sb("xn", [T, G, D])
        xnT = [sb(f"xnT{p}", [128, KC, GT]) for p in range(2)]
        relu = [sb(f"relu{p}", [128, GT]) for p in range(2)]
        qx = [sb(f"{n}x", [128, KC, GT]) for n in "qk"]
        parts = [sb(f"{n}_parts", [128, PARTS, KC, GT], BF16) for n in "qk"]
        pack = [[sb(f"{n}_pack{p}", [128, HEADS, GT], BF16) for p in range(2)] for n in "qk"]
        probs = [sb(f"probs{p}", [T, HEADS, T]) for p in range(2)]
        avT = sb("avT", [128, G, T])
        den = sb("den", [T, HEADS])
        rden = sb("rden", [T, HEADS])
        ctxt = sb("ctxt", [T, HEADS, HD])
        ctxT = sb("ctxT", [128, KC, T])
        pooled = sb("pooled", [128, KC, G])
        top = sb("top", [G, 8])
        topi = sb("topi", [G, 8], U32)
        topf = sb("topf", [G, 2])
        gdiff = sb("gdiff", [G, 1])
        gexp = sb("gexp", [G, 1])
        gden = sb("gden", [G, 1])
        gval = sb("gval", [G, 2])
        gsel = sb("gsel", [G, 2, E])
        gates = sb("gates", [G, E])
        gwide = sb("gwide", [G, E, R])
        minus1 = sb("minus1", [G, 1])
        cT = sb("cT", [128, 4, B])
        xvs = [sb("xvs_q", [128, GT]), sb("xvs_k", [128, GT])]
        xvs_v = [sb(f"xvs_v{p}", [128, GT]) for p in range(2)]
        xvo = sb("xvo", [128, T])
        mrow = sb("mrow", [T, HEADS, G])
        mneg = sb("mneg", [HEADS * G, T])
        mparts = sb("mparts", [HEADS * G, PARTS, T], BF16)
        psS = psum("psS", [128, 4, 512])
        psA = [psum(f"psA{n}", [128, 512]) for n in range(2)]
        psO = psum("psO", [128, 512])
        psN = psum("psN", [128, 512])
        scratch = [[nc.dram_tensor(f"{n}_scratch{p}", (PARTS, HD, HALF_HEADS, KC, GT), BF16).ap()
                    for p in range(2)] for n in "qk"]

        init_pool, init_act = sem("init_pool"), sem("init_act")
        passed = {n: sem(f"{n}_passed") for n in ("sp", "pe", "dve", "pool")}
        ln_stats, ln_aggr, ln_var = event("ln_stats", G), event("ln_aggr", G), event("ln_var")
        ln_rstd, xn_ready = event("ln_rstd"), event("xn_ready", G)
        xt_filled, xnT_ready = event("xt_filled", KC), event("xnT_ready", KC)
        qk_filled, qx_ready = event("qk_filled", 4), layer_event("qx_ready", 4)
        qk_relu = event("qk_relu", 4)
        p1_ready = event("p1_ready", 2)
        r_ready = [layer_event(f"{n}r_ready", 1) for n in "qk"]
        p2_ready = [layer_event(f"{n}p2_ready", 1) for n in "qk"]
        p3_ready = [layer_event(f"{n}p3_ready", 1) for n in "qk"]
        stored = [event(f"{n}_stored", 1, 16) for n in "qk"]
        packed = [ParityEvent([sem(f"{n}_packed{p}") for p in range(2)], 3) for n in "qk"]
        v_filled, v_ready = event("v_filled", 2), event("v_ready", 2)
        s_filled, probs_ready = event("s_filled", 2 * G), layer_event("probs_ready", 2 * G)
        av_filled, avT_ready = event("av_filled", G), event("avT_ready", G)
        tn_filled, den_ready = event("tn_filled", G), event("den_ready", G)
        rden_ready, ctx_ready = event("rden_ready", G), event("ctx_ready", G)
        tc_filled, ctxT_ready = event("tc_filled", G), event("ctxT_ready", KC * G, bias=1)
        out_filled, res_ready = event("out_filled", G), event("res_ready", G, bias=1)

        def mixture_event(name, per_group=1, unit=1):
            return event(name, per_group, unit, NG)

        pool_ready, h1_filled = mixture_event("pool_ready"), mixture_event("h1_filled")
        h1_ready, lg_filled = mixture_event("h1_ready"), mixture_event("lg_filled")
        top_ready, gate = mixture_event("top_ready", 2), mixture_event("gate", 9)
        gexp_ready = mixture_event("gexp_ready")
        gt_filled, cT_ready = mixture_event("gt_filled"), mixture_event("cT_ready", 4)
        xv_filled, xvs_ready = mixture_event("xv_filled", 3), mixture_event("xvs_ready", 3)
        ov_filled, xvo_ready = mixture_event("ov_filled", G), mixture_event("xvo_ready", G)
        m_filled, max_done = mixture_event("m_filled", 2 * G), mixture_event("max_done", 2 * G)
        mt_filled, mneg_ready = mixture_event("mt_filled"), mixture_event("mneg_ready")
        mpart, mpacked = mixture_event("mpart", 4), mixture_event("mpacked", 3, 16)
        hob_ready, stores = mixture_event("hob_ready"), mixture_event("stores", 2, 16)

        def pair(p):
            return psS[0:T, 2 * p:2 * p + 2, 0:GT].rearrange("p a (h t) -> p a h t", h=G)

        def buffer(it, sh):
            return (it[1] + sh) % 2

        class Ring:

            def __init__(self):
                self.turn = 1

            def take(self):
                self.turn = 1 - self.turn
                return self.turn

        def body_of(part, ring=None):
            def body(it):
                for name, args, sh, live in steps_of(it):
                    if name in part:
                        part[name](it, sh, live, *args)
                    elif ring is not None and name in USES_RING:
                        for _ in range(USES_RING[name]):
                            ring.take()
            return body

        USES_RING = dict(XT=KC, QK=1, V=1, MT=1, G=1, XV=1)

        with nc.Block() as block:
            @block.tensor
            def _(pe):
                occupant = {}
                ring = Ring()

                def fill(it, bank, event_, shift, n):
                    if bank in occupant:
                        ev, sh, m = occupant[bank]
                        ev.wait(pe, it, sh, m)
                    occupant[bank] = (event_, shift, n)

                def next_a(it, event_, shift, n):
                    a = ring.take()
                    fill(it, ("A", a), event_, shift, n)
                    return psA[a]

                def accumulate(ps, *products):
                    for n, (lhsT, rhs) in enumerate(products):
                        mm = nc.tensor.matmul(ps, lhsT, rhs, start=(n == 0), stop=(n == len(products) - 1))
                    return mm

                def XT(it, sh, live):
                    for kc in range(KC):
                        ps = next_a(it, xnT_ready, sh, kc)
                        if not live:
                            continue
                        if kc == 0:
                            xn_ready.wait(pe, it, sh, G - 1)
                        for s in range(G):
                            mm = nc.tensor.transpose(ps[:, s * T:(s + 1) * T],
                                                     xn[:, s, kc * 128:(kc + 1) * 128], ident[0:T, 0:T])
                        mm.then_inc(xt_filled.sem, 1)

                def QK(it, sh, live, n):
                    mix = is_mixture(it, sh)
                    ps = next_a(it, qx_ready if mix else qk_relu, sh, n)
                    if not live:
                        return
                    tensor, cc = divmod(n, KC)
                    x, name = xnT[buffer(it, sh)], "qk"[tensor]
                    if n == 0:
                        xnT_ready.wait(pe, it, sh, KC - 1)
                    cols = slice(cc * 128, (cc + 1) * 128)
                    w = k[("mT_" if mix else "lw_") + name]
                    products = [(w[:, kc, cols], x[:, kc]) for kc in range(KC)]
                    if mix:
                        if cc == 0:
                            xvs_ready.wait(pe, it, sh, tensor)
                        products.append((k["uT_" + name][:, cols], xvs[tensor][:]))
                    accumulate(ps[:, 0:GT], *products).then_inc(qk_filled.sem, 1)

                def V(it, sh, live, n):
                    mix = is_mixture(it, sh)
                    ps = next_a(it, v_ready, sh, n)
                    if not live:
                        return
                    w, x = k["mT_v" if mix else "lw_v"], xnT[buffer(it, sh)]
                    if mix:
                        xvs_ready.wait(pe, it, sh, 2)
                    for i in range(2):
                        cols = slice((2 * n + i) * T, (2 * n + i + 1) * T)
                        products = [(x[:, kc, cols], w[:, kc]) for kc in range(KC)]
                        if mix:
                            products.append((xvs_v[buffer(it, sh)][:, cols], k["uT_v"][:]))
                        mm = accumulate(ps[0:T, i * D:(i + 1) * D], *products)
                    mm.then_inc(v_filled.sem, 1)

                def heads(it, sh, s, rows, stationary, moving, filled, p):
                    par = buffer(it, sh)
                    cols = slice(s * T, (s + 1) * T)
                    for n in range(8 * p, 8 * p + 8):
                        mm = nc.tensor.matmul(psS[0:T, n // G, (n % G) * T:(n % G + 1) * T],
                                              stationary[par][0:rows, n, cols], moving[par][0:rows, n, cols],
                                              start=True, stop=True)
                    mm.then_inc(filled.sem, 1)

                def S(it, sh, live, s):
                    s %= G
                    mix = is_mixture(it, sh)
                    for p in range(2):
                        fill(it, ("S", p), probs_ready, sh, 2 * s + p)
                        if not live:
                            continue
                        if s == 0 and p == 0:
                            if mix:
                                mpacked.wait(pe, it, sh, 2)
                                if it[0] is None:
                                    pe.wait_ge(init_pool, 3)
                            else:
                                packed[0].wait(pe, it, sh)
                                packed[1].wait(pe, it, sh)
                        heads(it, sh, s, ROWS + PARTS if mix else ROWS, pack[1], pack[0], s_filled, p)

                def M(it, sh, live, s):
                    for p in range(2):
                        fill(it, ("S", p), max_done, sh, 2 * s + p)
                        if s == 0 and p == 0:
                            packed[0].wait(pe, it, sh)
                            packed[1].wait(pe, it, sh)
                        heads(it, sh, s, ROWS, pack[0], pack[1], m_filled, p)

                def MT(it, sh, live):
                    ps = next_a(it, mneg_ready, sh, 0)
                    max_done.wait(pe, it, sh, 2 * G - 1, alone=passed["pe"])
                    nc.tensor.transpose(ps[0:HEADS * G, 0:T], mrow[:].rearrange("p h b -> p (h b)"),
                                        ident[0:T, 0:T]).then_inc(mt_filled.sem, 1)

                def G_(it, sh, live, n):
                    if n == 0:
                        ps = next_a(it, h1_ready, sh, 0)
                        pool_ready.wait(pe, it, sh, 0)
                        accumulate(ps[0:GH, 0:G], *((k["gw1T"][:, kc], pooled[:, kc]) for kc in range(KC))
                                   ).then_inc(h1_filled.sem, 1)
                    elif n == 1:
                        ps = next_a(it, top_ready, sh, 1)
                        h1_ready.wait(pe, it, sh, 0)
                        nc.tensor.matmul(ps[0:G, 0:E], k["h1"][:], k["gw2T"][:], start=True, stop=True
                                         ).then_inc(lg_filled.sem, 1)
                    else:
                        ps = next_a(it, cT_ready, sh, 3)
                        gate.wait(pe, it, sh, 8, alone=passed["pe"])
                        nc.tensor.transpose(ps[:, 0:G], gwide[:].rearrange("p e r -> p (e r)"), ident[0:G, 0:G]
                                            ).then_inc(gt_filled.sem, 1)

                def XV(it, sh, live, n):
                    ps = next_a(it, xvs_ready, sh, n)
                    w, x = k["vT_" + PROJ[n]], xnT[buffer(it, sh)]
                    accumulate(ps[:, 0:GT], *((w[:, kc], x[:, kc]) for kc in range(KC))).then_inc(xv_filled.sem, 1)

                def AV(it, sh, live, s):
                    fill(it, "O", avT_ready, sh, s)
                    if not live:
                        return
                    if s % 2 == 0:
                        v_ready.wait(pe, it, sh, s // 2)
                    for p in range(2):
                        probs_ready.wait(pe, it, sh, 2 * s + p)
                        for n in range(8 * p, 8 * p + 8):
                            h = (n % KC) * HALF_HEADS + n // KC
                            mm = nc.tensor.matmul(psO[VW * (h % 4):VW * (h % 4 + 1), (h // 4) * T:(h // 4 + 1) * T],
                                                  v_ext[buffer(it, sh)][:, s, h], probs[s % 2][:, n],
                                                  start=True, stop=True, skip_group_check=True)
                    mm.then_inc(av_filled.sem, 1)

                def TN(it, sh, live, s):
                    fill(it, "N", ctx_ready, sh, s)
                    if live:
                        avT_ready.wait(pe, it, sh, s)
                        for n in range(4):
                            mm = nc.tensor.transpose(psN[0:T, n * 128:(n + 1) * 128], avT[:, n], ident[:])
                        mm.then_inc(tn_filled.sem, 1)

                def TC(it, sh, live, s):
                    fill(it, "N", ctxT_ready, sh, 2 * s + 1)
                    if live:
                        for kc in range(KC):
                            mm = nc.tensor.transpose(
                                psN[:, kc * T:(kc + 1) * T],
                                ctxt[:, kc * HALF_HEADS:(kc + 1) * HALF_HEADS].rearrange("p h d -> p (h d)"),
                                ident[0:T, 0:T])
                        mm.then_inc(tc_filled.sem, 1)

                def OV(it, sh, live, s):
                    fill(it, "N", xvo_ready, sh, s)
                    ctxT_ready.wait(pe, it, sh, 2 * s + 1)
                    accumulate(psN[:, 0:T], *((k["vT_o"][:, kc], ctxT[:, kc]) for kc in range(KC))
                               ).then_inc(ov_filled.sem, 1)

                def OUT(it, sh, live, s):
                    mix = is_mixture(it, sh)
                    fill(it, "O", res_ready, sh, s)
                    if not live:
                        return
                    ctxT_ready.wait(pe, it, sh, 2 * s + 1)
                    w = k["mT_o" if mix else "lw_o"]
                    products = [(ctxT[:, kc], w[:, kc]) for kc in range(KC)]
                    if mix:
                        xvo_ready.wait(pe, it, sh, s)
                        products.append((xvo[:], k["uT_o"][:]))
                    accumulate(psO[0:T, 0:D], *products).then_inc(out_filled.sem, 1)

                run = body_of(dict(XT=XT, QK=QK, V=V, S=S, M=M, MT=MT, G=G_, XV=XV, AV=AV, TN=TN, TC=TC, OV=OV,
                                   OUT=OUT))

                def body(it):
                    for bank, (ev, sh, n) in occupant.items():
                        occupant[bank] = (ev, sh - 1, n)
                    run(it)

                run_iterations(pe, body)

            @block.scalar
            def _(act):
                ring = Ring()

                def XT(it, sh, live):
                    for kc in range(KC):
                        ps = psA[ring.take()]
                        if live:
                            xt_filled.wait(act, it, sh, kc)
                            nc.scalar.activation(xnT[buffer(it, sh)][:, kc], ps[:, 0:GT], ACT.Copy
                                                 ).then_inc(xnT_ready.sem, 1)

                def QK(it, sh, live, n):
                    ps = psA[ring.take()]
                    if not live:
                        return
                    tensor, cc = divmod(n, KC)
                    qk_filled.wait(act, it, sh, n)
                    if cc == 0:
                        p3_ready[tensor].wait(act, it, sh - 1, 0)
                    if is_mixture(it, sh):
                        nc.scalar.activation(qx[tensor][:, cc], ps[:, 0:GT], ACT.Identity,
                                             bias=k["bias_qs" if tensor == 0 else "bias_k"][:, cc:cc + 1],
                                             scale=Q_SCALE if tensor == 0 else 1.0
                                             ).then_inc(qx_ready.of(it, sh).sem, 1)
                    else:
                        if n >= 2:
                            qx_ready.wait(act, it, sh, n - 2)
                        else:
                            qx_ready.wait(act, it, sh - 1, n + 2)
                        nc.scalar.activation(qx[tensor][:, cc], ps[:, 0:GT], ACT.Exp)
                        nc.scalar.activation(relu[n % 2][:], ps[:, 0:GT], ACT.Relu).then_inc(qk_relu.sem, 1)

                def P(it, sh, live, tensor):
                    if live:
                        qx_ready.wait(act, it, sh, KC * tensor + KC - 1)
                        stored[tensor].wait(act, it, sh - 1, 0)
                        nc.scalar.activation(parts[tensor][:, slot(tensor, 0)], qx[tensor][:], ACT.Copy
                                             ).then_inc(p1_ready.sem, 1)

                def D_(it, sh, live, tensor):
                    if live and (tensor == 1 or not is_mixture(it, sh)):
                        r_ready[tensor].wait(act, it, sh, 0)
                        nc.scalar.activation(parts[tensor][:, slot(tensor, 1)], qx[tensor][:], ACT.Copy
                                             ).then_inc(p2_ready[tensor].of(it, sh).sem, 1)

                def V(it, sh, live, n):
                    ps = psA[ring.take()]
                    if live:
                        v_filled.wait(act, it, sh, n)
                        nc.scalar.activation(
                            v_ext[buffer(it, sh)][:, 2 * n:2 * n + 2, :, 0:HD],
                            ps[0:T].rearrange("p (b h d) -> p b h d", b=2, h=HEADS), ACT.Copy
                        ).then_inc(v_ready.sem, 1)

                def SX(it, sh, live, s, p):
                    s %= G
                    if live and is_mixture(it, sh):
                        s_filled.wait(act, it, sh, 2 * s + p)
                        nc.scalar.activation(
                            probs[s % 2][:, 8 * p:8 * p + 8].rearrange("p (a h) t -> p a h t", a=2),
                            pair(p), ACT.Exp).then_inc(probs_ready.of(it, sh).sem, 1)

                def MT(it, sh, live):
                    ps = psA[ring.take()]
                    mt_filled.wait(act, it, sh, 0)
                    if it[0] is not None or not it[1] + sh == NG:
                        mpart.wait(act, it, sh - 1, 3)
                    nc.scalar.activation(mneg[:], ps[0:HEADS * G, 0:T], ACT.Copy, scale=-1.0
                                         ).then_inc(mneg_ready.sem, 1)

                def G_(it, sh, live, n):
                    ps = psA[ring.take()]
                    if n == 0:
                        h1_filled.wait(act, it, sh, 0)
                        nc.scalar.activation(k["h1"][0:GH], ps[0:GH, 0:G], ACT.Relu, bias=k["gb1"][:, 0:1],
                                             scale=1.0 / T).then_inc(h1_ready.sem, 1)
                    if n == 1:
                        gate.wait(act, it, sh, 1)
                        nc.scalar.activation(gexp[:], gdiff[:], ACT.Exp).then_inc(gexp_ready.sem, 1)

                def AV(it, sh, live, s):
                    if live:
                        av_filled.wait(act, it, sh, s)
                        nc.scalar.activation(avT[:].rearrange("p g t -> p (g t)"), psO[:, 0:GT], ACT.Copy
                                             ).then_inc(avT_ready.sem, 1)

                def TC(it, sh, live, s):
                    if live:
                        tc_filled.wait(act, it, sh, s)
                        for kc in range(KC):
                            src = psN[:, kc * T:(kc + 1) * T]
                            if is_mixture(it, sh):
                                nc.scalar.activation(ctxT[:, kc], src, ACT.Identity, bias=k["bias_v"][:, kc:kc + 1]
                                                     ).then_inc(ctxT_ready.sem, 1)
                            else:
                                nc.scalar.activation(ctxT[:, kc], src, ACT.Copy).then_inc(ctxT_ready.sem, 1)

                act.sem_inc(ctxT_ready.sem, 1)
                nc.scalar.mul(k["bias_qs"][:], k["bias_q"][:], Q_SCALE).then_inc(init_act, 1)
                act.wait_ge(init_act, 1)
                run_iterations(act, body_of(dict(XT=XT, QK=QK, P=P, D=D_, V=V, SX=SX, MT=MT, G=G_, AV=AV, TC=TC), ring))

            @block.vector
            def _(dve):
                ring = Ring()

                def LN(it, sh, live):
                    if not live:
                        return
                    for s in range(G):
                        nc.vector.bn_stats(stat[:, s], hid[:, sample(it, sh, s)]).then_inc(ln_stats.sem, 1)
                    ln_stats.wait(dve, it, sh, G - 1, alone=passed["dve"])
                    for s in range(G):
                        nc.vector.bn_aggr(mv[:, s], stat[:, s]).then_inc(ln_aggr.sem, 1)
                    ln_aggr.wait(dve, it, sh, G - 1)
                    nc.vector.tensor_scalar(ve[:], mv[:, :, 1], LN_EPS, None, ALU.add).then_inc(ln_var.sem, 1)

                def LNX(it, sh, live):
                    if not live:
                        return
                    xt_filled.wait(dve, it, sh - 1, KC - 1)
                    ln_rstd.wait(dve, it, sh, 0)
                    for s in range(G):
                        nc.vector.tensor_scalar(xn[:, s], hid[:, sample(it, sh, s)], mv[:, s, 0:1], rstd[:, s:s + 1],
                                                ALU.subtract, ALU.mult).then_inc(xn_ready.sem, 1)

                def QK(it, sh, live, n):
                    ring.take()
                    if live and not is_mixture(it, sh):
                        tensor, cc = divmod(n, KC)
                        q = qx[tensor][:, cc]
                        qk_relu.wait(dve, it, sh, n)
                        nc.vector.scalar_tensor_tensor(q, q, 1.0, relu[n % 2][:], ALU.min, ALU.add
                                                       ).then_inc(qx_ready.of(it, sh).sem, 1)

                def P(it, sh, live, tensor):
                    if tensor == 1 and is_mixture(it, sh):
                        p1_ready.wait(dve, it, sh, tensor)
                        nc.vector.tensor_tensor(qx[1][:], qx[1][:], parts[1][:, slot(1, 0)], ALU.subtract
                                                ).then_inc(r_ready[1].of(it, sh).sem, 1)

                def D_(it, sh, live, tensor):
                    if not is_mixture(it, sh):
                        return
                    if tensor == 0:
                        r_ready[0].wait(dve, it, sh, 0)
                        nc.vector.tensor_copy(parts[0][:, slot(0, 1)], qx[0][:]
                                              ).then_inc(p2_ready[0].of(it, sh).sem, 1)
                    else:
                        p2_ready[1].wait(dve, it, sh, 0)
                        nc.vector.tensor_tensor(parts[1][:, slot(1, 2)], qx[1][:], parts[1][:, slot(1, 1)],
                                                ALU.subtract).then_inc(p3_ready[1].of(it, sh).sem, 1)

                def SX(it, sh, live, s, p):
                    s %= G
                    if live and not is_mixture(it, sh):
                        s_filled.wait(dve, it, sh, 2 * s + p)
                        nc.vector.tensor_tensor(
                            probs[s % 2][:, 8 * p:8 * p + 8].rearrange("p (a h) t -> p a h t", a=2), pair(p),
                            k["mask"][:].unsqueeze(1).unsqueeze(1).broadcast_to([T, 2, G, T]), ALU.mult
                        ).then_inc(probs_ready.of(it, sh).sem, 1)

                def M(it, sh, live, s):
                    for p in range(2):
                        m_filled.wait(dve, it, sh, 2 * s + p)
                        nc.vector.tensor_reduce(mrow[:, 8 * p:8 * p + 8, s].rearrange("p (a h) -> p a h", a=2),
                                                pair(p), AX.X, ALU.max).then_inc(max_done.sem, 1)

                def MT(it, sh, live):
                    ring.take()
                    mneg_ready.wait(dve, it, sh, 0)
                    if it[0] is not None or not it[1] + sh == NG:
                        mpacked.wait(dve, it, sh - 1, 2)
                    nc.vector.tensor_copy(mparts[:, 0], mneg[:]).then_inc(mpart.sem, 1)
                    mpart.wait(dve, it, sh, 0)
                    nc.vector.tensor_tensor(mneg[:], mneg[:], mparts[:, 0], ALU.subtract).then_inc(mpart.sem, 1)
                    mpart.wait(dve, it, sh, 1)
                    nc.vector.tensor_copy(mparts[:, 1], mneg[:]).then_inc(mpart.sem, 1)
                    mpart.wait(dve, it, sh, 2)
                    nc.vector.tensor_tensor(mparts[:, 2], mneg[:], mparts[:, 1], ALU.subtract).then_inc(mpart.sem, 1)

                def G_(it, sh, live, n):
                    ps = psA[ring.take()]
                    if n == 0:
                        xnT_ready.wait(dve, it, sh, KC - 1)
                        nc.vector.tensor_reduce(pooled[:], xnT[buffer(it, sh)][:].rearrange(
                            "p c (b t) -> p c b t", b=G), AX.X, ALU.add).then_inc(pool_ready.sem, 1)
                    elif n == 1:
                        lg_filled.wait(dve, it, sh, 0, alone=passed["dve"])
                        nc.vector.max(top[:], ps[0:G, 0:E]).then_inc(top_ready.sem, 1)
                        top_ready.wait(dve, it, sh, 0, alone=passed["dve"])
                        nc.vector.max_index(topi[:], top[:], ps[0:G, 0:E]).then_inc(top_ready.sem, 1)
                    else:
                        gt_filled.wait(dve, it, sh, 0)
                        for i in range(4):
                            nc.vector.tensor_scalar(cT[:, i, span(it, sh)], ps[:, 0:G], k["svals"][:, i:i + 1], None,
                                                    ALU.mult).then_inc(cT_ready.sem, 1)

                def XV(it, sh, live, n):
                    ps = psA[ring.take()]
                    dst = xvs[n] if n < 2 else xvs_v[buffer(it, sh)]
                    xv_filled.wait(dve, it, sh, n)
                    if n == 0:
                        cT_ready.wait(dve, it, sh, 3)
                    nc.vector.tensor_tensor(
                        dst[:].rearrange("p (b t) -> p b t", b=G), ps[:, 0:GT].rearrange("p (b t) -> p b t", b=G),
                        cT[:, n, span(it, sh)].unsqueeze(2).broadcast_to([128, G, T]), ALU.mult
                    ).then_inc(xvs_ready.sem, 1)

                def TN(it, sh, live, s):
                    if not live:
                        return
                    tn_filled.wait(dve, it, sh, s)
                    ps = psN[0:T].rearrange("p (h w) -> p h w", w=VW)
                    nc.vector.tensor_scalar(den[:], ps[:, :, HD], 0.0 if is_mixture(it, sh) else DEN_EPS, None,
                                            ALU.add).then_inc(den_ready.sem, 1)
                    den_ready.wait(dve, it, sh, s)
                    nc.vector.reciprocal(rden[:], den[:]).then_inc(rden_ready.sem, 1)
                    rden_ready.wait(dve, it, sh, s)
                    nc.vector.tensor_tensor(ctxt[:], ps[:, :, 0:HD], rden[:].unsqueeze(2).broadcast_to([T, HEADS, HD]),
                                            ALU.mult).then_inc(ctx_ready.sem, 1)

                def OV(it, sh, live, s):
                    b = sample(it, sh, s)
                    ov_filled.wait(dve, it, sh, s)
                    nc.vector.tensor_scalar(xvo[:], psN[:, 0:T],
                                            cT[:, 3, slice(b, b + 1) if it[0] is None else bass.ds(b, 1)],
                                            None, ALU.mult).then_inc(xvo_ready.sem, 1)

                def OUT(it, sh, live, s):
                    if live:
                        hb = hid[:, sample(it, sh, s)]
                        out_filled.wait(dve, it, sh, s)
                        if is_mixture(it, sh) and s == 0:
                            hob_ready.wait(dve, it, sh, 0)
                        nc.vector.tensor_tensor(hb, psO[0:T, 0:D], hb, ALU.add).then_inc(res_ready.sem, 1)

                dve.sem_inc(res_ready.sem, 1)
                run_iterations(dve, body_of(dict(LN=LN, LNX=LNX, QK=QK, P=P, D=D_, SX=SX, M=M, MT=MT, G=G_, XV=XV,
                                                 TN=TN, OV=OV, OUT=OUT), ring))

            @block.gpsimd
            def _(pool):
                def LN(it, sh, live):
                    if live:
                        ln_var.wait(pool, it, sh, 0)
                        nc.gpsimd.tensor_tensor(rstd[:], ve[:], k["lneps_half"][:], ALU.pow).then_inc(ln_rstd.sem, 1)

                def P(it, sh, live, tensor):
                    if live and (tensor == 0 or not is_mixture(it, sh)):
                        p1_ready.wait(pool, it, sh, tensor)
                        nc.gpsimd.tensor_tensor(qx[tensor][:], qx[tensor][:], parts[tensor][:, slot(tensor, 0)],
                                                ALU.subtract).then_inc(r_ready[tensor].of(it, sh).sem, 1)

                def D_(it, sh, live, tensor):
                    if live and (tensor == 0 or not is_mixture(it, sh)):
                        p2_ready[tensor].wait(pool, it, sh, 0)
                        nc.gpsimd.tensor_tensor(parts[tensor][:, slot(tensor, 2)], qx[tensor][:],
                                                parts[tensor][:, slot(tensor, 1)], ALU.subtract
                                                ).then_inc(p3_ready[tensor].of(it, sh).sem, 1)

                def G_(it, sh, live, n):
                    if n != 1:
                        return

                    def chained(e, ins):
                        ins.then_inc(gate.sem, 1)
                        gate.wait(pool, it, sh, e, alone=passed["pool"])

                    top_ready.wait(pool, it, sh, 1, alone=passed["pool"])
                    chained(0, nc.gpsimd.tensor_copy(topf[:], topi[:, 0:2]))
                    chained(1, nc.gpsimd.tensor_tensor(gdiff[:], top[:, 1:2], top[:, 0:1], ALU.subtract))
                    gexp_ready.wait(pool, it, sh, 0, alone=passed["pool"])
                    chained(2, nc.gpsimd.tensor_scalar(gden[:], gexp[:], 1.0, None, ALU.add))
                    chained(3, nc.gpsimd.tensor_tensor(gval[:, 0:1], gden[:], minus1[:], ALU.pow))
                    chained(4, nc.gpsimd.tensor_tensor(gval[:, 1:2], gexp[:], gval[:, 0:1], ALU.mult))
                    for i in range(2):
                        chained(5 + i, nc.gpsimd.tensor_scalar(
                            gsel[:, i], k["iotaf"][:], topf[:, i:i + 1], gval[:, i:i + 1], ALU.is_equal, ALU.mult))
                    chained(7, nc.gpsimd.tensor_tensor(gates[:], gsel[:, 0], gsel[:, 1], ALU.add))
                    chained(8, nc.gpsimd.tensor_copy(gwide[:], gates[:].unsqueeze(2).broadcast_to([G, E, R])))

                def HB(it, sh, live):
                    hg = hid[:, span(it, sh)]
                    xn_ready.wait(pool, it, sh, G - 1)
                    nc.gpsimd.tensor_tensor(hg, hg, k["ob"][:].unsqueeze(1).broadcast_to([T, G, D]), ALU.add
                                            ).then_inc(hob_ready.sem, 1)

                for p in range(2):
                    nc.gpsimd.memset(pack[1][p][ROWS:ROWS + PARTS], 1.0).then_inc(init_pool, 1)
                    pool.wait_ge(init_pool, p + 1)
                nc.gpsimd.memset(minus1[:], -1.0).then_inc(init_pool, 1)
                pool.wait_ge(init_pool, 3)
                run_iterations(pool, body_of(dict(LN=LN, P=P, D=D_, G=G_, HB=HB)))

            @block.sync
            def _(sp):
                def PACK(it, sh, live, n):
                    if not live:
                        return
                    par, done = buffer(it, sh), packed[n].sem(it, sh)
                    p3_ready[n].wait(sp, it, sh, 0, alone=passed["sp"])
                    sp.dma_start(scratch[n][par].rearrange("r d h c t -> (d h) r (c t)"),
                                 parts[n][:].rearrange("p r c t -> p r (c t)")).then_inc(stored[n].sem, 16)
                    s_filled.wait(sp, it, sh - 2, 2 * G - 1, alone=passed["sp"])
                    stored[n].wait(sp, it, sh, 0, alone=passed["sp"])
                    src = scratch[n][par].rearrange("r d h c t -> (r d) (h c t)")
                    dst = pack[n][par][:].rearrange("p h t -> p (h t)")
                    first = 0 if n == 0 else HD
                    sp.dma_start(dst[0:3 * HD], src).then_inc(done, 16)
                    sp.dma_start(dst[3 * HD:5 * HD], src[first:first + 2 * HD]).then_inc(done, 16)
                    sp.dma_start(dst[5 * HD:6 * HD], src[2 * first:2 * first + HD]).then_inc(done, 16)

                def MT(it, sh, live):
                    mpart.wait(sp, it, sh, 3, alone=passed["sp"])
                    for r in range(PARTS):
                        sp.dma_start(pack[0][buffer(it, sh)][ROWS + r:ROWS + r + 1].rearrange("p h t -> p (h t)"),
                                     mparts[:, r]).then_inc(mpacked.sem, 16)

                def STORE(it, sh, live):
                    res_ready.wait(sp, it, sh, G - 1, alone=passed["sp"])
                    bs = span(it, sh)
                    sp.dma_start(out[bs, IMG:T].rearrange("b t d -> t b d"), hid[0:TXT, bs]).then_inc(stores.sem, 16)
                    sp.dma_start(out[bs, 0:IMG].rearrange("b t d -> t b d"), hid[TXT:T, bs]).then_inc(stores.sem, 16)

                run_iterations(sp, body_of(dict(PACK=PACK, MT=MT, STORE=STORE)))
                sp.wait_ge(stores.sem, 16 * 2 * NG)


def program(nc, A, out):
    with ExitStack() as c:
        k = {}

        def keep(name, shape, dt=F32):
            k[name] = c.enter_context(nc.sbuf_tensor(name, shape, dt))

        keep("hid", [T, B, D])
        keep("ident", [128, 128])
        keep("mask", [T, T])
        keep("lneps_half", [T, G])
        keep("iota", [G, E], I32)
        keep("iotaf", [G, E])
        keep("h1", [GH + 1, G])
        keep("gw1T", [128, KC, GH])
        keep("gw2T", [GH + 1, E])
        keep("gb1", [GH, 1])
        keep("svals", [ER, 4])
        keep("bias_q", [128, KC])
        keep("bias_qs", [128, KC])
        keep("bias_k", [128, KC])
        keep("bias_v", [128, KC])
        keep("ob", [T, D])
        for n in PROJ:
            keep(f"lw_{n}", [128, KC, D])
            keep(f"mT_{n}", [128, KC, D])
            keep(f"vT_{n}", [128, KC, ER])
            keep(f"uT_{n}", [ER, D])
        for p in range(2):
            keep(f"v_ext{p}", [T, G, HEADS, VW])
        embed(nc, c, A, k)
        attention(nc, A, k, out)


def kernel(**inputs):
    import numpy as np
    import concourse.bacc as bacc
    from concourse.bass_utils import run_bass_kernel_spmd

    nc = bacc.Bacc("TRN2", target_bir_lowering=False, num_devices=1)
    arrays, aps = {}, {}
    for name, value in inputs.items():
        a = np.ascontiguousarray(value)
        arrays[f"in_{name}"] = a
        aps[name.removeprefix("L0_")] = nc.dram_tensor(f"in_{name}", a.shape, mybir.dt.from_np(a.dtype),
                                                       kind="ExternalInput").ap()
    out = nc.dram_tensor("out", (B, T, D), F32, kind="ExternalOutput").ap()
    program(nc, aps, out)
    return run_bass_kernel_spmd(nc, [arrays], core_ids=[0]).results[0]["out"]
```

```python
from contextlib import ExitStack

import concourse.bass as bass
from concourse import mybir

F32 = mybir.dt.float32
F32R = mybir.dt.float32r
BF16 = mybir.dt.bfloat16
I32 = mybir.dt.int32
U32 = mybir.dt.uint32
ALU = mybir.AluOpType
ACT = mybir.ActivationFunctionType
AX = mybir.AxisListType

B = 32
D = 256
KC = D // 128
HEADS, HD = 16, 16
HALF_HEADS = HEADS // 2
PATCH, CH, SIDE = 16, 3, 96
GRID = SIDE // PATCH
NP = GRID * GRID
PD = CH * PATCH * PATCH
PCH = PD // 128
TXT = 77
IMG = NP + 1
T = TXT + IMG
G = 4
GT = G * T
NG = B // G
NB = 4
GATHER_P = 112
GATHER_N = B * TXT // GATHER_P
E, R, GH = 8, 16, 64
ER = E * R
VW = 32
LN_EPS = 1e-5
DEN_EPS = 1e-6
Q_SCALE = HD ** -0.5
PROJ = ("q", "k", "v", "o")
PARTS = 3
SPLIT_WEIGHTS = tuple(w + n for w in ("lw_", "mT_", "vT_") for n in "qkv")
ROWS = 6 * HD


class Event:

    def __init__(self, sem, per_group=1, unit=1, first=0, bias=0):
        self.sem, self.per_group, self.unit, self.first, self.bias = sem, per_group, unit, first, bias

    def of(self, it, shift):
        return self

    def wait(self, eng, it, shift, n, alone=None):
        j, base = it
        done = self.per_group * (base + shift - self.first) + n + 1
        v = self.unit * done + self.bias
        if j is None:
            if done > 0:
                eng.wait_ge(self.sem, v)
            return
        assert v > 0
        eng.wait_ge(self.sem, j * (2 * self.unit * self.per_group) + v)
        if alone is not None:
            eng.sem_inc(alone, 1)


class LayerEvent:

    def __init__(self, linear, mixture, per_group):
        self.events = (Event(linear, per_group), Event(mixture, per_group, first=NG))

    def of(self, it, shift):
        return self.events[is_mixture(it, shift)]

    def wait(self, eng, it, shift, n, alone=None):
        self.of(it, shift).wait(eng, it, shift, n, alone)


class ParityEvent:

    def __init__(self, sems, per_group):
        self.sems, self.per_group = sems, per_group

    def sem(self, it, shift):
        return self.sems[(it[1] + shift) % 2]

    def wait(self, eng, it, shift):
        j, base = it
        v = 16 * self.per_group * ((base + shift) // 2 + 1)
        if j is not None or v > 0:
            eng.wait_ge(self.sem(it, shift), v if j is None else j * (16 * self.per_group) + v)


def is_mixture(it, shift):
    return it[1] + shift >= NG


def sample(it, shift, s):
    j, base = it
    b = G * (base + shift - NG * is_mixture(it, shift)) + s
    return b if j is None else j * (2 * G) + b


def span(it, shift, n=G):
    b = sample(it, shift, 0)
    return slice(b, b + n) if isinstance(b, int) else bass.ds(b, n)


def slot(tensor, r):
    return r if tensor == 0 else PARTS - 1 - r


def run_iterations(eng, body):
    body((None, -2))
    body((None, -1))
    for first in (0, NG):
        with eng.Fori(0, (NG - 2) // 2) as j:
            body((j, first))
            body((j, first + 1))
        body((None, first + NG - 2))
        body((None, first + NG - 1))


def steps_of(it, engine):
    found = []
    for name, *args in (LINEAR_ORDER if it[1] < NG - 2 else MIXTURE_ORDER)[engine]:
        if name in ("S", "SX"):
            shift = 1 if args[0] == G else 0
        elif name.endswith("+"):
            name, shift = name[:-1], 1
            if not is_mixture(it, shift):
                continue
        else:
            shift = GROUP_OF[name]
        group = it[1] + shift
        if it[0] is None and group >= 2 * NG or name in MIXTURE_ONLY and not is_mixture(it, shift):
            continue
        found.append((name, args, shift, it[0] is not None or group >= 0))
    return found




def embed(nc, ctx, A, k):
    with ExitStack() as c:
        def sb(name, shape, dt=F32):
            return c.enter_context(nc.sbuf_tensor(name, shape, dt))

        def sem(name):
            return c.enter_context(nc.semaphore(name))

        HB = B // 2
        PR = HB * GRID
        ximg = [sb(f"ximg{h}", [PR, CH, PATCH, SIDE]) for h in range(2)]
        pstat = sb("pstat", [PR, 2, GRID, 2, 6])
        pmv = sb("pmv", [PR, 2, GRID, 2])
        pve = sb("pve", [PR, 2, GRID])
        prs = sb("prs", [PR, 2, GRID])
        nhalf = sb("nhalf", [PR, GRID])
        patch = sb("patch", [PR, GRID, PD])
        xT = sb("xT", [128, 2, PCH, PR])
        wraw = sb("wraw", [128, PCH, D])
        wg = sb("wg", [128, PCH, D])
        g1 = sb("g1", [128, PCH])
        b1 = sb("b1", [128, PCH])
        b1b = sb("b1b", [128, PCH, PR])
        bproj = sb("bproj", [PR, D])
        ybias = bproj
        y = [sb("y0", [PR, GRID, D]), k["y1"][0:PR]]
        ystat = sb("ystat", [PR, 2, GRID, 6])
        ymv = sb("ymv", [PR, 2, GRID, 2])
        yve = sb("yve", [PR, 2, GRID])
        yrs = sb("yrs", [PR, 2, GRID])
        g2 = sb("g2", [PR, D])
        b2 = sb("b2", [PR, D])
        pos = sb("pos", [PR, GRID, D])
        cls = sb("cls", [B, 2, D])
        idx = sb("idx", [GATHER_P, GATHER_N], I32)
        coef = sb("coef", [GATHER_P, GATHER_N, NB + 1])
        crest = sb("crest", [GATHER_P, GATHER_N, NB + 1])
        cpart = [sb(f"cpart{n}", [GATHER_P, GATHER_N, NB + 1], BF16) for n in range(2)]
        cparts = sb("cparts", [GATHER_P, GATHER_N, 6, NB + 1])
        cmax = sb("cmax", [GATHER_P, GATHER_N])
        csum = sb("csum", [GATHER_P, GATHER_N])
        crec = sb("crec", [GATHER_P, GATHER_N])
        coefT = sb("coefT", [6 * (NB + 1), B * TXT], BF16)
        base = sb("base", [NB + 1, D])
        lang = sb("lang", [NB + 1, D])
        base5 = lang
        bscale = sb("bscale", [NB + 1, 1])
        bparts = sb("bparts", [NB + 1, PARTS, D], BF16)
        bases = sb("bases", [6 * (NB + 1), D], BF16)
        lin_raw = {n: sb(f"lraw_{n}", [128, KC, D]) for n in ("q", "k")}
        raw = [(sb(f"mraw{p}", [128, KC, D]), sb(f"uraw{p}", [128, KC, ER]), sb(f"vraw{p}", [ER, D]))
               for p in range(2)]
        m_raw, u_raw, v_raw = ({n: raw[i % 2][kind] for i, n in enumerate(PROJ)} for kind in range(3))
        ones = sb("ones", [PARTS, T], BF16)
        gw1_raw = sb("gw1_raw", [GH, D])
        gw2_raw = sb("gw2_raw", [E, GH])
        psX = [c.enter_context(nc.psum_tensor(f"psX{n}", [128, 512], F32)) for n in range(4)]
        psY = [c.enter_context(nc.psum_tensor(f"psY{n}", [128, 512], F32)) for n in range(2)]
        psW = [c.enter_context(nc.psum_tensor(f"psW{n}", [128, 512], F32)) for n in range(2)]
        tok = k["tok"]

        x_loaded = [sem("x_loaded0"), sem("x_loaded1")]
        tokw_loaded = sem("tokw_loaded")
        tokc_loaded = sem("tokc_loaded")
        mat_loaded = {n: sem(f"mat_loaded_{n}") for n in PROJ}
        gate_loaded = sem("gate_loaded")
        lin_loaded = sem("lin_loaded")
        rest_loaded = sem("rest_loaded")
        base_loaded = sem("base_loaded")
        cls_loaded = sem("cls_loaded")
        idx_loaded = sem("idx_loaded")
        gathered = sem("gathered")
        tok_stored = sem("tok_stored")
        tok_loaded = sem("tok_loaded")
        const_ready = sem("const_ready")
        wprep = sem("wprep")
        pst = sem("pst")
        prs_ready = sem("prs_ready")
        xnorm = sem("xnorm")
        yb_filled, yb_ready = sem("yb_filled"), sem("yb_ready")
        xt_filled, xt_ready = sem("xt_filled_e"), sem("xt_ready_e")
        y_filled, y_ready = sem("y_filled"), sem("y_ready")
        ymv_ready = sem("ymv_ready")
        yst = sem("yst")
        wg_ready, b1_spread = sem("wg_ready"), sem("b1_spread")
        split = sem("split")
        bases_loaded = sem("bases_loaded")
        yrs_ready = sem("yrs_ready")
        yn, yg = sem("yn"), sem("yg")
        z_ready = sem("z_ready")
        wt_filled, wt_ready = sem("wt_filled"), sem("wt_ready")
        cls_ready = sem("cls_ready")
        soft = sem("soft")
        cexp = sem("cexp")
        base_ready = sem("base_ready")
        ct_filled, ct_ready = sem("ct_filled"), sem("ct_ready")
        txt_filled = sem("txt_filled")
        ones_ready, ones_stored = sem("ones_ready"), sem("ones_stored")
        v_upper = sem("v_upper")
        e_upper, e_lower = sem("e_upper"), sem("e_lower")
        txt_ready = [sem("txt_ready_act"), sem("txt_ready_dve")]

        NCT = -(-GATHER_N // G)

        def text_to_vector(n):
            return n % 2 == 1 and n >= 7

        def weights_before(n):
            return {0: (0, 1), GRID: (2,), GRID + 3: (3,)}.get(n, ())

        with nc.Block() as block:
            @block.sync
            def _(sp):
                def load_images(h):
                    for ch in range(CH):
                        sp.dma_start(ximg[h][:, ch].rearrange("p y x -> p (y x)"),
                                     A["x"][h * HB:(h + 1) * HB, ch].rearrange("b (h y) x -> b h (y x)", h=GRID)
                                     ).then_inc(x_loaded[h], 16)

                load_images(0)
                for ch in range(CH):
                    sp.dma_start(wraw[:, 2 * ch:2 * ch + 2],
                                 A["tok_W_proj"].rearrange("(h p c) e -> c p h e", c=CH, h=2)[ch]
                                 ).then_inc(tokw_loaded, 16)
                for t, name in ((g1, "tok_ln1_g"), (b1, "tok_ln1_b")):
                    sp.dma_start(t[:].rearrange("p (c h) -> p c h", c=CH),
                                 A[name].rearrange("(h p c) -> p c h", c=CH, h=2),
                                 allow_slow_non_contiguous=True).then_inc(tokw_loaded, 16)
                def load_matrices(n):
                    sp.dma_start(m_raw[n][:], A[f"ffn_{n}Wm"].rearrange("(c p) d -> p c d", p=128)
                                  ).then_inc(mat_loaded[n], 16)
                    sp.dma_start(v_raw[n][:], A[f"ffn_{n}V"].rearrange("e r d -> (e r) d")
                                  ).then_inc(mat_loaded[n], 16)
                    for oc in range(KC):
                        sp.dma_start(u_raw[n][:, oc].rearrange("p (e r) -> p e r", e=E),
                                      A[f"ffn_{n}U"][:, oc * 128:(oc + 1) * 128].rearrange("e p r -> p e r")
                                      ).then_inc(mat_loaded[n], 16)

                for n in PROJ[0:2]:
                    load_matrices(n)
                load_images(1)
                for t, name in ((bproj, "tok_b_proj"), (g2, "tok_ln2_g"), (b2, "tok_ln2_b")):
                    sp.dma_start(t[:], A[name].partition_broadcast(PR)).then_inc(tokc_loaded, 16)
                patch_pos = A["tok_pos_emb"][0, 1:IMG].rearrange("(h w) e -> h w e", h=GRID)
                sp.dma_start(pos[:], patch_pos.unsqueeze(0).broadcast_to([HB, GRID, GRID, D])
                             ).then_inc(tokc_loaded, 16)
                sp.dma_start(cls[:, 0], A["tok_cls_token"][0, 0].partition_broadcast(B)).then_inc(cls_loaded, 16)
                sp.dma_start(cls[:, 1], A["tok_pos_emb"][0, 0].partition_broadcast(B)).then_inc(cls_loaded, 16)
                for i in range(2, 4):
                    sp.wait_ge(wt_filled, 2 * i - 2)
                    load_matrices(PROJ[i])
                sp.dma_start(gw1_raw[:], A["ffn_gw1"]).then_inc(gate_loaded, 16)
                sp.dma_start(gw2_raw[:], A["ffn_gw2"]).then_inc(gate_loaded, 16)
                for n in ("q", "k"):
                    sp.dma_start(lin_raw[n][:], A[f"attn_w{n}"].rearrange("(c p) e -> p c e", p=128)
                                 ).then_inc(lin_loaded, 16)
                sp.dma_start(k["lw_v"][:], A["attn_wv"].rearrange("(c p) e -> p c e", p=128)
                             ).then_inc(lin_loaded, 16)
                sp.dma_start(k["lw_o"][:], A["attn_wo"].rearrange("(c p) e -> p c e", p=128)
                             ).then_inc(rest_loaded, 16)
                sp.dma_start(k["gw2T"][GH:GH + 1], A["ffn_gb2"].partition_broadcast(1)).then_inc(rest_loaded, 16)
                sp.dma_start(k["gb1"][:], A["ffn_gb1"].unsqueeze(1)).then_inc(rest_loaded, 16)
                for i, n in enumerate(PROJ):
                    sp.dma_start(k["svals"][:, i:i + 1], A[f"ffn_{n}S"].rearrange("e r -> (e r)").unsqueeze(1)
                                  ).then_inc(rest_loaded, 16)
                for n in ("q", "k"):
                    for cc in range(KC):
                        sp.dma_start(k[f"bias_{n}"][:, cc:cc + 1],
                                      A[f"ffn_{n}b"][cc * 128:(cc + 1) * 128].rearrange("(h d o) -> d h o", d=HD, o=1),
                                      allow_slow_non_contiguous=True).then_inc(rest_loaded, 16)
                sp.dma_start(k["bias_v"][:], A["ffn_vb"].rearrange("(c p) -> p c", p=128),
                              allow_slow_non_contiguous=True).then_inc(rest_loaded, 16)
                sp.dma_start(k["ob"][:], A["ffn_ob"].partition_broadcast(T)).then_inc(rest_loaded, 16)
                sp.wait_ge(base_ready, 6)
                for n, part in enumerate((0, 1, 2, 1, 2, 2)):
                    sp.dma_start(bases[n * (NB + 1):(n + 1) * (NB + 1)], bparts[:, part]).then_inc(bases_loaded, 16)
                sp.wait_ge(cls_ready, 1)
                sp.dma_start(tok[:, 0], cls[:, 0]).then_inc(tok_stored, 16)
                sp.wait_ge(z_ready, 1)
                sp.dma_start(tok[0:HB, 1:].rearrange("b (h w) e -> b h (w e)", h=GRID),
                             y[0][:].rearrange("p w e -> p (w e)")).then_inc(tok_stored, 16)
                sp.wait_ge(tok_stored, 32)
                sp.dma_start(k["hid"][TXT:T, 0:HB], tok[0:HB].rearrange("b n e -> n b e")).then_inc(tok_loaded, 16)
                sp.wait_ge(ones_ready, 1)
                sp.dma_start(k["ones"], ones[:]).then_inc(ones_stored, 16)
                sp.wait_ge(ones_stored, 16)
                sp.wait_ge(tok_loaded, 16)
                sp.wait_ge(bases_loaded, 96)

            @block.scalar
            def _(act):
                act.dma_start(base[0:NB], A["txt_base_embed_weight"]).then_inc(base_loaded, 16)
                act.dma_start(base[NB:NB + 1], A["txt_lang_bias"][2:3]).then_inc(base_loaded, 16)
                act.wait_ge(const_ready, 2)
                act.dma_start(lang[0:NB], A["txt_lang_bias"]).then_inc(base_loaded, 16)
                act.wait_ge(tokw_loaded, 16 * (CH + 2))
                nc.scalar.activation(b1b[:], b1[:].unsqueeze(2).broadcast_to([128, PCH, PR]), ACT.Copy
                                     ).then_inc(b1_spread, 1)
                def weights(i, n):
                    act.wait_ge(wt_filled, 2 * i + 1)
                    src = psW[0][:]
                    dst = k[f"mT_{n}"][:].rearrange("p c o -> p (c o)")
                    if n in "qk":
                        src = src.rearrange("p (a h d) -> p a h d", a=2 * KC, h=HALF_HEADS)
                        dst = dst.rearrange("p (a d h) -> p a h d", a=2 * KC, h=HALF_HEADS)
                    nc.scalar.activation(dst, src, ACT.Copy).then_inc(wt_ready, 1)
                    act.wait_ge(wt_filled, 2 * i + 2)
                    nc.scalar.activation(k[f"vT_{n}"][:].rearrange("p c r -> p (c r)"), psW[1][:, 0:256],
                                         ACT.Copy).then_inc(wt_ready, 1)
                    if n in "qkv":
                        nc.scalar.activation(k[f"vT_{n}_upper"][:].rearrange("p c r -> p (c r)"),
                                             psW[1][:, 0:256], ACT.Copy).then_inc(v_upper, 1)
                    src, dst = psW[1][:, 256:512], k[f"uT_{n}"][:]
                    if n in "qk":
                        src = src.rearrange("p (a h d) -> p a h d", a=KC, h=HALF_HEADS)
                        dst = dst.rearrange("p (a d h) -> p a h d", a=KC, h=HALF_HEADS)
                    nc.scalar.activation(dst, src, ACT.Copy).then_inc(wt_ready, 1)

                def patches(n):
                    for a in range(2):
                        act.wait_ge(xt_filled, 2 * n + a + 1)
                        if n >= 2:
                            act.wait_ge(y_filled, n - 1)
                        nc.scalar.activation(xT[:, n % 2, 3 * a:3 * a + 3].rearrange("p c r -> p (c r)"),
                                             psX[2 * (n % 2) + a][:, 0:3 * PR], ACT.Copy).then_inc(xt_ready, 1)

                for n in range(GRID + 4):
                    for i in weights_before(n):
                        weights(i, PROJ[i])
                    patches(n)
                act.wait_ge(soft, 2)
                nc.scalar.activation(coef[:, :, 0:NB], coef[:, :, 0:NB], ACT.Exp).then_inc(cexp, 1)
                for n in range(GRID + 4, 2 * GRID):
                    patches(n)
                    if n == GRID + 4:
                        act.wait_ge(lin_loaded, 48)
                        nc.scalar.activation(k["lw_v_upper"][:], k["lw_v"][:], ACT.Copy).then_inc(e_upper, 1)
                act.wait_ge(wprep, 2)
                for n in "qk":
                    nc.scalar.activation(k[f"lw_{n}_upper"][:], k[f"lw_{n}"][:], ACT.Copy).then_inc(e_upper, 1)
                act.wait_ge(wt_filled, 9)
                nc.scalar.activation(k["gw1T"][:].rearrange("p c g -> p (c g)"), psW[0][:, 0:KC * GH],
                                     ACT.Copy).then_inc(wt_ready, 1)
                nc.scalar.activation(k["gw2T"][0:GH], psW[0][0:GH, 128:128 + E], ACT.Copy).then_inc(wt_ready, 1)
                cT = coefT[:].rearrange("q (p n) -> q n p", n=GATHER_N)
                for m in range(NCT):
                    w = min(G, GATHER_N - G * m)
                    act.wait_ge(ct_filled, m + 1)
                    nc.scalar.activation(cT[:, G * m:G * m + w],
                                         psW[m % 2][0:6 * (NB + 1), 0:w * GATHER_P].rearrange("q (n p) -> q n p", n=w),
                                         ACT.Copy).then_inc(ct_ready, 1)
                for n in range(B // 2):
                    if not text_to_vector(n):
                        act.wait_ge(txt_filled, n + 1)
                        nc.scalar.activation(k["hid"][0:TXT, 2 * n:2 * n + 2].rearrange("p b e -> p (b e)"),
                                             psX[n % 4][0:TXT], ACT.Copy).then_inc(txt_ready[text_to_vector(n)], 1)
                act.wait_ge(rest_loaded, 16 * (1 + 2 + 4 + 4 + 2))

            @block.gpsimd
            def _(pool):
                pool.dma_start(idx[:], A["x_txt"].rearrange("b t -> (b t)").rearrange("(p n) -> p n", p=GATHER_P)
                               ).then_inc(idx_loaded, 16)
                nc.gpsimd.memset(nhalf[:], -0.5).then_inc(const_ready, 1)
                nc.gpsimd.memset(lang[:], 0.0).then_inc(const_ready, 1)
                nc.gpsimd.memset(bscale[:], 0.1).then_inc(const_ready, 1)
                nc.gpsimd.memset(ones[:], 1.0).then_inc(ones_ready, 1)
                nc.gpsimd.memset(k["ident"][:], 0.0).then_inc(const_ready, 1)
                pool.wait_ge(const_ready, 4)
                nc.gpsimd.affine_select(out=k["ident"][:], in_=k["ident"][:], compare_op=ALU.not_equal, fill=1.0,
                                        base=0, pattern=[[-1, 128]], channel_multiplier=1).then_inc(const_ready, 1)
                nc.gpsimd.affine_select(out=bscale[:], in_=bscale[:], compare_op=ALU.is_ge, fill=float(D) ** 0.5,
                                        base=-NB, pattern=[[0, 1]], channel_multiplier=1).then_inc(const_ready, 1)
                pool.wait_ge(tokw_loaded, 16 * (CH + 2))
                nc.gpsimd.tensor_tensor(wg[:], wraw[:], g1[:].unsqueeze(2).broadcast_to([128, PCH, D]),
                                        ALU.mult).then_inc(wg_ready, 1)
                pool.wait_ge(pst, 19)
                nc.gpsimd.tensor_tensor(prs[:, 0], pve[:, 0], nhalf[:], ALU.pow).then_inc(prs_ready, 1)
                pool.wait_ge(idx_loaded, 16)
                for n in range(GATHER_N):
                    if n == 16:
                        pool.wait_ge(pst, 38)
                        nc.gpsimd.tensor_tensor(prs[:, 1], pve[:, 1], nhalf[:], ALU.pow).then_inc(prs_ready, 1)
                    nc.gpsimd.indirect_dma_start(
                        coef[:, n, 0:NB], None, A["txt_coeff_weight"],
                        bass.IndirectOffsetOnAxis(ap=idx[:, n:n + 1], axis=0)).then_inc(gathered, 16)
                nc.gpsimd.memset(k["mask"][:], 1.0).then_inc(const_ready, 1)
                nc.gpsimd.memset(k["lneps_half"][:], -0.5).then_inc(const_ready, 1)
                nc.gpsimd.memset(coef[:, :, NB:NB + 1], 1.0).then_inc(const_ready, 1)
                nc.gpsimd.memset(k["h1"][:], 1.0).then_inc(const_ready, 1)
                pool.wait_ge(const_ready, 10)
                nc.gpsimd.affine_select(out=k["mask"][0:TXT, 0:TXT], in_=k["mask"][0:TXT, 0:TXT],
                                        compare_op=ALU.is_ge, fill=0.0, base=0, pattern=[[1, TXT]],
                                        channel_multiplier=-1).then_inc(const_ready, 1)
                nc.gpsimd.affine_select(out=k["mask"][:, TXT:T], in_=k["mask"][:, TXT:T],
                                        compare_op=ALU.is_ge, fill=0.0, base=TXT, pattern=[[1, IMG]],
                                        channel_multiplier=-1).then_inc(const_ready, 1)
                pool.wait_ge(const_ready, 12)
                nc.gpsimd.affine_select(out=k["mask"][:, TXT:T], in_=k["mask"][:, TXT:T],
                                        compare_op=ALU.is_ge, fill=0.0, base=-TXT, pattern=[[0, IMG]],
                                        channel_multiplier=1).then_inc(const_ready, 1)
                nc.gpsimd.iota(k["iota"][:], pattern=[[1, E]], base=0, channel_multiplier=0).then_inc(const_ready, 1)
                pool.wait_ge(const_ready, 14)
                nc.gpsimd.tensor_copy(k["iotaf"][:], k["iota"][:]).then_inc(const_ready, 1)
                pool.wait_ge(yst, 13)
                nc.gpsimd.tensor_tensor(yrs[:, 0], yve[:, 0], nhalf[:], ALU.pow).then_inc(yrs_ready, 1)
                for p in range(2):
                    nc.gpsimd.memset(k[f"v_ext{p}"][:], 0.0).then_inc(const_ready, 1)
                pool.wait_ge(const_ready, 17)
                for p in range(2):
                    nc.gpsimd.memset(k[f"v_ext{p}"][:, :, :, HD:HD + 1], 1.0).then_inc(const_ready, 1)
                pool.wait_ge(const_ready, 19)
                def lower(n):
                    nc.gpsimd.tensor_tensor(k[f"{n}_lower"][:], k[n][:], k[f"{n}_upper"][:].bitcast(F32),
                                            ALU.subtract).then_inc(e_lower, 1)

                for i in range(2):
                    pool.wait_ge(v_upper, i + 1)
                    pool.wait_ge(wt_ready, 3 * i + 2)
                    lower(f"vT_{PROJ[i]}")
                pool.wait_ge(soft, 5)
                c5 = coef[:]
                nc.gpsimd.tensor_copy(cpart[0][:], c5).then_inc(split, 1)
                pool.wait_ge(split, 1)
                nc.gpsimd.tensor_tensor(crest[:], c5, cpart[0][:], ALU.subtract).then_inc(split, 1)
                pool.wait_ge(split, 2)
                nc.gpsimd.tensor_copy(cpart[1][:], crest[:]).then_inc(split, 1)
                pool.wait_ge(split, 3)
                nc.gpsimd.tensor_tensor(cparts[:, :, 2], crest[:], cpart[1][:], ALU.subtract).then_inc(split, 1)
                for slots, part in (((0, 3, 5), 0), ((1, 4), 1)):
                    for n in slots:
                        nc.gpsimd.tensor_copy(cparts[:, :, n], cpart[part][:]).then_inc(split, 1)
                for i, n in enumerate("vqk"):
                    pool.wait_ge(e_upper, i + 1)
                    if n == "k":
                        pool.wait_ge(yst, 26)
                        nc.gpsimd.tensor_tensor(yrs[:, 1], yve[:, 1], nhalf[:], ALU.pow).then_inc(yrs_ready, 1)
                    lower(f"lw_{n}")
                pool.wait_ge(v_upper, 3)
                pool.wait_ge(wt_ready, 8)
                lower("vT_v")

            @block.vector
            def _(dve):
                def patch_stats(h, w):
                    for a in range(2):
                        nc.vector.bn_stats(pstat[:, h, w, a],
                                           ximg[h][:, :, a * 8:a * 8 + 8, w * PATCH:(w + 1) * PATCH]
                                           ).then_inc(pst, 1)

                def patch_aggr(h):
                    dve.wait_ge(pst, 19 * h + 12)
                    for w in range(GRID):
                        nc.vector.bn_aggr(pmv[:, h, w], pstat[:, h, w].rearrange("p a s -> p (a s)")
                                          ).then_inc(pst, 1)
                    dve.wait_ge(pst, 19 * h + 18)
                    nc.vector.tensor_scalar(pve[:, h], pmv[:, h, :, 1], LN_EPS, None, ALU.add).then_inc(pst, 1)

                def patch_norm(h, w):
                    dve.wait_ge(prs_ready, h + 1)
                    if h:
                        dve.wait_ge(xt_filled, 2 * (w + 1))
                    nc.vector.tensor_scalar(patch[:, w].rearrange("p (c y x) -> p c y x", c=CH, y=PATCH),
                                            ximg[h][:, :, :, w * PATCH:(w + 1) * PATCH],
                                            pmv[:, h, w, 0:1], prs[:, h, w:w + 1],
                                            ALU.subtract, ALU.mult).then_inc(xnorm, 1)

                def embedded(h, w):
                    n = GRID * h + w
                    dve.wait_ge(y_filled, n + 1)
                    nc.vector.tensor_tensor(y[h][:, w], psY[n % 2][0:PR, 0:D], ybias[:], ALU.add).then_inc(y_ready, 1)
                    dve.wait_ge(y_ready, n + 1)
                    nc.vector.bn_stats(ystat[:, h, w], y[h][:, w]).then_inc(yst, 1)

                def embedded_aggr(h):
                    dve.wait_ge(yst, 13 * h + 6)
                    for w in range(GRID):
                        nc.vector.bn_aggr(ymv[:, h, w], ystat[:, h, w]).then_inc(yst, 1)
                    dve.wait_ge(yst, 13 * h + 12)
                    nc.vector.tensor_scalar(yve[:, h], ymv[:, h, :, 1], LN_EPS, None, ALU.add).then_inc(yst, 1)

                def embedded_norm(h, ws):
                    ws = list(ws)
                    done = GRID * h
                    dve.wait_ge(yrs_ready, h + 1)
                    for w in ws:
                        nc.vector.tensor_scalar(y[h][:, w], y[h][:, w], ymv[:, h, w, 0:1], yrs[:, h, w:w + 1],
                                                ALU.subtract, ALU.mult).then_inc(yn, 1)
                    for w in ws:
                        dve.wait_ge(yn, done + w + 1)
                        nc.vector.tensor_tensor(y[h][:, w], y[h][:, w], g2[:], ALU.mult).then_inc(yg, 1)
                    for w in ws:
                        dve.wait_ge(yg, done + w + 1)
                        add = nc.vector.tensor_tensor(y[h][:, w], y[h][:, w], pos[:, w], ALU.add)
                        if w == GRID - 1:
                            add.then_inc(z_ready, 1)

                dve.wait_ge(x_loaded[0], 16 * CH)
                for w in range(GRID):
                    patch_stats(0, w)
                patch_aggr(0)
                for w in range(GRID):
                    patch_norm(0, w)
                dve.wait_ge(yb_filled, 1)
                dve.wait_ge(tokc_loaded, 64)
                nc.vector.tensor_tensor(ybias[:], psY[1][0:PR, 0:D], bproj[:], ALU.add).then_inc(yb_ready, 1)
                dve.wait_ge(x_loaded[1], 16 * CH)
                patch_stats(1, 0)
                dve.wait_ge(yb_ready, 1)
                for w in range(GRID):
                    if w < 2:
                        patch_stats(1, 2 * w + 1)
                        patch_stats(1, 2 * w + 2)
                    if w == 2:
                        patch_stats(1, 5)
                        patch_aggr(1)
                    if w == 3:
                        dve.wait_ge(base_loaded, 48)
                        dve.wait_ge(const_ready, 6)
                        nc.vector.tensor_tensor(base5[:], base[:], lang[:], ALU.add).then_inc(base_ready, 1)
                        dve.wait_ge(base_ready, 1)
                        nc.vector.tensor_scalar(base5[:], base5[:], bscale[:, 0:1], None, ALU.mult).then_inc(base_ready, 1)
                    if w == 4:
                        dve.wait_ge(base_ready, 2)
                        nc.vector.tensor_copy(bparts[:, 2], base5[:]).then_inc(base_ready, 1)
                        dve.wait_ge(base_ready, 3)
                        nc.vector.tensor_tensor(base[:], base5[:], bparts[:, 2], ALU.subtract
                                                ).then_inc(base_ready, 1)
                    if w == 4:
                        patch_norm(1, 0)
                        patch_norm(1, 1)
                    embedded(0, w)
                patch_norm(1, 2)
                patch_norm(1, 3)
                embedded_aggr(0)
                dve.wait_ge(cls_loaded, 32)
                nc.vector.tensor_tensor(cls[:, 0], cls[:, 0], cls[:, 1], ALU.add).then_inc(cls_ready, 1)
                dve.wait_ge(base_ready, 4)
                nc.vector.tensor_copy(bparts[:, 1], base[:]).then_inc(base_ready, 1)
                nc.vector.tensor_tensor(pos[:], pos[:], b2[:].unsqueeze(1).broadcast_to([PR, GRID, D]),
                                        ALU.add).then_inc(yb_ready, 1)
                dve.wait_ge(base_ready, 5)
                nc.vector.tensor_tensor(bparts[:, 0], base[:], bparts[:, 1], ALU.subtract).then_inc(base_ready, 1)
                dve.wait_ge(yb_ready, 2)
                cb = [GATHER_P, GATHER_N, NB]
                c4 = coef[:, :, 0:NB]
                for w in range(GRID):
                    if w < 2:
                        patch_norm(1, w + 4)
                    embedded(1, w)
                    if w == 1:
                        dve.wait_ge(gathered, 16 * GATHER_N)
                        nc.vector.tensor_reduce(cmax[:], c4, AX.X, ALU.max).then_inc(soft, 1)
                        dve.wait_ge(soft, 1)
                        nc.vector.tensor_tensor(c4, c4, cmax[:].unsqueeze(2).broadcast_to(cb),
                                                ALU.subtract).then_inc(soft, 1)
                    embedded_norm(0, [w])
                    if w == 3:
                        dve.wait_ge(cexp, 1)
                        nc.vector.tensor_reduce(csum[:], c4, AX.X, ALU.add).then_inc(soft, 1)
                        dve.wait_ge(soft, 3)
                        nc.vector.reciprocal(crec[:], csum[:]).then_inc(soft, 1)
                        dve.wait_ge(soft, 4)
                        nc.vector.tensor_tensor(c4, c4, crec[:].unsqueeze(2).broadcast_to(cb),
                                                ALU.mult).then_inc(soft, 1)
                    if w in (4, 5):
                        n = "qk"[w - 4]
                        dve.wait_ge(lin_loaded, 48)
                        nc.vector.tensor_copy(
                            k[f"lw_{n}"][:].rearrange("p c (a d h) -> p (c a) h d", a=KC, h=HALF_HEADS),
                            lin_raw[n][:].rearrange("p c (a h d) -> p (c a) h d", a=KC, h=HALF_HEADS)
                        ).then_inc(wprep, 1)
                embedded_aggr(1)
                embedded_norm(1, range(GRID))
                for n in range(B // 2):
                    if text_to_vector(n):
                        dve.wait_ge(txt_filled, n + 1)
                        nc.vector.tensor_copy(k["hid"][0:TXT, 2 * n:2 * n + 2].rearrange("p b e -> p (b e)"),
                                              psX[n % 4][0:TXT]).then_inc(txt_ready[text_to_vector(n)], 1)

            @block.tensor
            def _(pe):
                pe.wait_ge(const_ready, 5)
                ident = k["ident"]
                def weights(i, n):
                    pe.wait_ge(mat_loaded[n], 64)
                    if i:
                        pe.wait_ge(wt_ready, 3 * i - 2)
                    for kc in range(KC):
                        for oc in range(KC):
                            at = (kc * KC + oc) * 128
                            mm = nc.tensor.transpose(psW[0][:, at:at + 128],
                                                     m_raw[n][:, oc, kc * 128:(kc + 1) * 128], ident[:])
                    mm.then_inc(wt_filled, 1)
                    if i:
                        pe.wait_ge(wt_ready, 3 * i)
                    for kc in range(KC):
                        nc.tensor.transpose(psW[1][:, kc * 128:(kc + 1) * 128],
                                            v_raw[n][:, kc * 128:(kc + 1) * 128], ident[:])
                    for oc in range(KC):
                        mm = nc.tensor.transpose(psW[1][:, 256 + oc * 128:384 + oc * 128], u_raw[n][:, oc], ident[:])
                    mm.then_inc(wt_filled, 1)

                for i in weights_before(0):
                    weights(i, PROJ[i])

                def patch_transposes(n):
                    h, w = divmod(n, GRID)
                    pe.wait_ge(xnorm, n + 1)
                    for a in range(2):
                        if n >= 2:
                            pe.wait_ge(xt_ready, 2 * (n - 2) + a + 1)
                        for i in range(3):
                            mm = nc.tensor.transpose(psX[2 * (n % 2) + a][:, i * PR:(i + 1) * PR],
                                                     patch[:, w, (3 * a + i) * 128:(3 * a + i + 1) * 128],
                                                     ident[0:PR, 0:PR])
                        mm.then_inc(xt_filled, 1)

                patch_transposes(0)
                pe.wait_ge(b1_spread, 1)
                pe.wait_ge(tokw_loaded, 16 * (CH + 2))
                for kc in range(PCH):
                    mm = nc.tensor.matmul(psY[1][0:PR, 0:D], b1b[:, kc], wraw[:, kc], start=(kc == 0),
                                          stop=(kc == PCH - 1))
                mm.then_inc(yb_filled, 1)
                for n in range(2 * GRID):
                    for i in weights_before(n + 1):
                        weights(i, PROJ[i])
                    if n + 1 < 2 * GRID:
                        patch_transposes(n + 1)
                    pe.wait_ge(xt_ready, 2 * n + 2)
                    if n == 0:
                        pe.wait_ge(wg_ready, 1)
                    if n == 1:
                        pe.wait_ge(yb_ready, 1)
                    if n >= 2:
                        pe.wait_ge(y_ready, n - 1)
                    for kc in range(PCH):
                        mm = nc.tensor.matmul(psY[n % 2][0:PR, 0:D], xT[:, n % 2, kc], wg[:, kc], start=(kc == 0),
                                              stop=(kc == PCH - 1))
                    mm.then_inc(y_filled, 1)
                pe.wait_ge(gate_loaded, 32)
                pe.wait_ge(wt_ready, 10)
                for kc in range(KC):
                    nc.tensor.transpose(psW[0][:, kc * GH:(kc + 1) * GH], gw1_raw[:, kc * 128:(kc + 1) * 128],
                                        ident[0:GH, 0:GH])
                nc.tensor.transpose(psW[0][0:GH, 128:128 + E], gw2_raw[:], ident[0:E, 0:E]).then_inc(wt_filled, 1)
                pe.wait_ge(split, 9)
                pe.wait_ge(wt_ready, 14)
                for m in range(NCT):
                    if m >= 2:
                        pe.wait_ge(ct_ready, m - 1)
                    for i in range(min(G, GATHER_N - G * m)):
                        mm = nc.tensor.transpose(psW[m % 2][0:6 * (NB + 1), i * GATHER_P:(i + 1) * GATHER_P],
                                                 cparts[:, G * m + i].rearrange("p a q -> p (a q)"),
                                                 ident[0:GATHER_P, 0:GATHER_P])
                    mm.then_inc(ct_filled, 1)
                pe.wait_ge(ct_ready, NCT)
                pe.wait_ge(bases_loaded, 96)
                for n in range(B // 2):
                    if n >= 4:
                        turn = text_to_vector(n - 4)
                        pe.wait_ge(txt_ready[turn], sum(text_to_vector(m) == turn for m in range(n - 3)))
                    for i in range(2):
                        b = 2 * n + i
                        mm = nc.tensor.matmul(psX[n % 4][0:TXT, i * D:(i + 1) * D],
                                              coefT[:, b * TXT:(b + 1) * TXT], bases[:], start=True, stop=True)
                    mm.then_inc(txt_filled, 1)



LINEAR_ORDER = dict(
    pe=(
        ("AV", 0, 0), ("AV", 0, 1), ("V", 0), ("S", 1, 0), ("S", 1, 1), ("TN", 0), ("V", 1), ("AV", 1, 0),
        ("TC", 0), ("AV", 1, 1), ("S", 2, 0), ("S", 2, 1), ("OUT", 0), ("TN", 1), ("XT",), ("TC", 1),
        ("QK", 0), ("AV", 2, 0), ("AV", 2, 1), ("S", 3, 0), ("S", 3, 1), ("TN", 2), ("QK", 1), ("OUT", 1),
        ("TC", 2), ("QK", 2), ("AV", 3, 0), ("AV", 3, 1), ("S", 4, 0), ("S", 4, 1), ("TN", 3), ("OUT", 2),
        ("TC", 3), ("QK", 3), ("OUT", 3),
    ),
    act=(
        ("SX", 1, 0), ("SX", 1, 1), ("AV", 0), ("V", 0), ("V", 1), ("AV", 1), ("TC", 0), ("SX", 2, 0), ("XT",),
        ("TC", 1), ("SX", 2, 1), ("QK", 0), ("AV", 2), ("SX", 3, 0), ("SX", 3, 1), ("QK", 1), ("P", 0),
        ("QK", 2), ("AV", 3), ("TC", 2), ("SX", 4, 0), ("D", 0), ("SX", 4, 1), ("TC", 3), ("QK", 3), ("P", 1),
        ("D", 1),
    ),
    dve=(
        ("LN",), ("SX", 1, 0), ("SX", 1, 1), ("TN", 0), ("LNX",), ("V", 0), ("V", 1), ("SX", 2, 0), ("OUT", 0),
        ("TN", 1), ("XT",), ("SX", 2, 1), ("QK", 0), ("SX", 3, 0), ("P", 0), ("TN", 2), ("SX", 3, 1), ("D", 0),
        ("OUT", 1), ("QK", 1), ("QK", 2), ("SX", 4, 0), ("TN", 3), ("OUT", 2), ("SX", 4, 1), ("P", 1),
        ("D", 1), ("QK", 3), ("OUT", 3),
    ),
    pool=(
        ("LN",), ("P", 0), ("D", 0), ("P", 1), ("D", 1),
    ),
    sp=(
        ("PACK", 0), ("PACK", 1),
    ),
)
MIXTURE_ORDER = dict(
    pe=(
        ("AV", 0, 0), ("S", 1, 0), ("S", 1, 1), ("AV", 0, 1), ("TN", 0), ("V", 0), ("AV", 1, 0), ("AV", 1, 1),
        ("TC", 0), ("XT",), ("OV", 0), ("S", 2, 0), ("S", 2, 1), ("TN", 1), ("OUT", 0), ("TC", 1), ("G", 0),
        ("V", 1), ("OV", 1), ("G", 1), ("M", 0, 0), ("M", 0, 1), ("AV", 2, 0), ("AV", 2, 1), ("S", 3, 0),
        ("S", 3, 1), ("TN", 2), ("OUT", 1), ("G", 2), ("TC", 2), ("XV", 0), ("M", 1, 0), ("M", 1, 1),
        ("XV", 1), ("OV", 2), ("M", 2, 0), ("M", 2, 1), ("AV", 3, 0), ("AV", 3, 1), ("QK", 0), ("M", 3, 0),
        ("M", 3, 1), ("TN", 3), ("MT",), ("QK", 1), ("OUT", 2), ("TC", 3), ("XV", 2), ("OV", 3), ("QK", 2),
        ("OUT", 3), ("S", 4, 0), ("S", 4, 1), ("QK", 3),
    ),
    act=(
        ("SX", 1, 0), ("AV", 0), ("D+", 1), ("SX", 1, 1), ("V", 0), ("AV", 1), ("TC", 0), ("XT",),
        ("SX", 2, 0), ("SX", 2, 1), ("TC", 1), ("G", 0), ("V", 1), ("G", 1), ("AV", 2), ("SX", 3, 0),
        ("SX", 3, 1), ("G", 2), ("XV", 0), ("XV", 1), ("TC", 2), ("AV", 3), ("QK", 0), ("MT",), ("QK", 1),
        ("P", 0), ("TC", 3), ("D", 0), ("XV", 2), ("QK", 2), ("SX", 4, 0), ("SX", 4, 1), ("QK", 3), ("P", 1),
    ),
    dve=(
        ("LN",), ("SX", 1, 0), ("D+", 1), ("TN", 0), ("SX", 1, 1), ("V", 0), ("LNX",), ("XT",), ("SX", 2, 0),
        ("OV", 0), ("TN", 1), ("SX", 2, 1), ("OUT", 0), ("G", 0), ("V", 1), ("OV", 1), ("G", 1), ("M", 0, 0),
        ("M", 0, 1), ("SX", 3, 0), ("SX", 3, 1), ("TN", 2), ("G", 2), ("OUT", 1), ("XV", 0), ("M", 1, 0),
        ("M", 1, 1), ("XV", 1), ("OV", 2), ("M", 2, 0), ("M", 2, 1), ("QK", 0), ("M", 3, 0), ("M", 3, 1),
        ("TN", 3), ("MT",), ("QK", 1), ("OUT", 2), ("XV", 2), ("P", 0), ("SX", 4, 0), ("D", 0), ("OV", 3),
        ("QK", 2), ("OUT", 3), ("QK", 3), ("SX", 4, 1), ("P", 1),
    ),
    pool=(
        ("HB",), ("D+", 1), ("G", 0), ("LN",), ("G", 1), ("P", 0), ("G", 2), ("P", 1), ("D", 0),
    ),
    sp=(
        ("PACK+", 1), ("MT",), ("PACK", 0), ("STORE",),
    ),
)
GROUP_OF = dict(LN=2, LNX=2, XT=2, QK=2, P=2, D=2, PACK=2, G=2, XV=2, V=1, M=1, MT=1, HB=1,
                AV=0, TN=0, TC=0, OV=0, OUT=0, STORE=0)
MIXTURE_ONLY = ("HB", "G", "XV", "M", "MT", "OV", "STORE")


def attention(nc, A, k, out):
    with ExitStack() as c:
        def sb(name, shape, dt=F32):
            return c.enter_context(nc.sbuf_tensor(f"a_{name}", shape, dt))

        def psum(name, shape):
            return c.enter_context(nc.psum_tensor(f"a_{name}", shape, F32))

        def sem(name):
            return c.enter_context(nc.semaphore(f"a_{name}"))

        def event(name, per_group=1, unit=1, first=0, bias=0):
            return Event(sem(name), per_group, unit, first, bias)

        def layer_event(name, per_group):
            return LayerEvent(sem(f"{name}_lin"), sem(f"{name}_mix"), per_group)

        hid, ident = k["hid"], k["ident"]
        v_ext = [k["v_ext0"], k["v_ext1"]]
        stat = sb("stat", [T, G, 6])
        mv = sb("mv", [T, G, 2])
        ve = sb("ve", [T, G])
        rstd = sb("rstd", [T, G])
        xn = sb("xn", [T, G, D])
        xnT = [sb(f"xnT{p}", [128, KC, GT], F32R) for p in range(2)]
        xnT_low = [sb(f"xnT_low{p}", [128, KC, GT], F32R) for p in range(2)]
        xvo, mrow, mneg, gwide, cT = (k[n] for n in ("xvo", "mrow", "mneg", "gwide", "cT"))
        upper = {n: k[f"{n}_upper"] for n in SPLIT_WEIGHTS}
        pair_of_rows = [sb(f"rows{p}", [128, GT]) for p in range(2)]
        relu = xvs = pair_of_rows
        qx = [sb(f"{n}x", [128, KC, GT]) for n in "qk"]
        parts = [sb(f"{n}_parts", [128, PARTS, KC, GT], BF16) for n in "qk"]
        pack = [[sb(f"{n}_pack{p}", [128, HEADS, GT], BF16) for p in range(2)] for n in "qk"]
        probs = [sb(f"probs{p}", [T, HEADS, T]) for p in range(2)]
        avT = sb("avT", [128, G, T])
        den = sb("den", [T, HEADS])
        rden = sb("rden", [T, HEADS])
        ctxt = sb("ctxt", [T, HEADS, HD])
        ctxT = sb("ctxT", [128, KC, T])
        pooled = sb("pooled", [128, KC, G])
        top = sb("top", [G, 8])
        topi = sb("topi", [G, 8], U32)
        topf = sb("topf", [G, 2])
        gdiff = sb("gdiff", [G, 1])
        gexp = sb("gexp", [G, 1])
        gden = sb("gden", [G, 1])
        gval = sb("gval", [G, 2])
        gsel = sb("gsel", [G, 2, E])
        gates = sb("gates", [G, E])
        minus1 = sb("minus1", [G, 1])
        xvs_v = sb("xvs_v", [128, GT])
        mparts = sb("mparts", [HEADS * G, PARTS, T], BF16)
        psS = psum("psS", [128, 4, 512])
        psA = [psum(f"psA{n}", [128, 512]) for n in range(2)]
        psO = psum("psO", [128, 512])
        psN = psum("psN", [128, 512])
        scratch = [[nc.dram_tensor(f"{n}_scratch{p}", (PARTS, HD, HALF_HEADS, KC, GT), BF16).ap()
                    for p in range(2)] for n in "qk"]

        init_pool, init_act = sem("init_pool"), sem("init_act")
        passed = {n: sem(f"{n}_passed") for n in ("sp", "pe", "dve", "pool")}
        ln_stats, ln_aggr, ln_var = event("ln_stats", G), event("ln_aggr", G), event("ln_var")
        ln_rstd, xn_ready = event("ln_rstd"), event("xn_ready", G)
        w_upper, w_lower = sem("w_upper"), sem("w_lower")
        xt_filled, xnT_ready, low_ready = event("xt_filled", KC), event("xnT_ready", KC), event("low_ready", KC)
        qk_filled, qx_ready = event("qk_filled", 4), layer_event("qx_ready", 4)
        qk_relu = event("qk_relu", 4)
        p1_ready = event("p1_ready", 2)
        r_ready = [layer_event(f"{n}r_ready", 1) for n in "qk"]
        p2_ready = [layer_event(f"{n}p2_ready", 1) for n in "qk"]
        p3_ready = [layer_event(f"{n}p3_ready", 1) for n in "qk"]
        stored = [event(f"{n}_stored", 1, 16) for n in "qk"]
        packed = [ParityEvent([sem(f"{n}_packed{p}") for p in range(2)], 3) for n in "qk"]
        v_filled, v_ready = event("v_filled", 2), event("v_ready", 2)
        s_filled, probs_ready = event("s_filled", 2 * G), layer_event("probs_ready", 2 * G)
        av_filled, avT_ready = event("av_filled", G), event("avT_ready", G)
        tn_filled, den_ready = event("tn_filled", G), event("den_ready", G)
        rden_ready, ctx_ready = event("rden_ready", G), event("ctx_ready", G)
        tc_filled, ctxT_ready = event("tc_filled", G), event("ctxT_ready", KC * G, bias=1)
        out_filled, res_ready = event("out_filled", G), event("res_ready", G, bias=1)

        def mixture_event(name, per_group=1, unit=1):
            return event(name, per_group, unit, NG)

        pool_ready, h1_filled = mixture_event("pool_ready", KC), mixture_event("h1_filled")
        h1_ready, lg_filled = mixture_event("h1_ready"), mixture_event("lg_filled")
        top_ready, gate = mixture_event("top_ready", 2), mixture_event("gate", 9)
        gexp_ready = mixture_event("gexp_ready")
        gt_filled, cT_ready = mixture_event("gt_filled"), mixture_event("cT_ready", 4)
        xv_filled, xvs_ready = mixture_event("xv_filled", 3), mixture_event("xvs_ready", 3)
        ov_filled, xvo_ready = mixture_event("ov_filled", G), mixture_event("xvo_ready", G)
        m_filled, max_done = mixture_event("m_filled", 2 * G), mixture_event("max_done", 2 * G)
        mt_filled, mneg_ready = mixture_event("mt_filled"), mixture_event("mneg_ready")
        mpart, mpacked = mixture_event("mpart", 4), mixture_event("mpacked", 3, 16)
        hob_ready, stores = mixture_event("hob_ready"), mixture_event("stores", 2, 16)

        def pair(p):
            return psS[0:T, 2 * p:2 * p + 2, 0:GT].rearrange("p a (h t) -> p a h t", h=G)

        def buffer(it, sh):
            return (it[1] + sh) % 2

        class Ring:

            def __init__(self):
                self.turn = 1

            def take(self):
                self.turn = 1 - self.turn
                return self.turn

        def body_of(engine, part, ring=None):
            def body(it):
                for name, args, sh, live in steps_of(it, engine):
                    if name in part:
                        part[name](it, sh, live, *args)
                    elif ring is not None and name in USES_RING:
                        for _ in range(USES_RING[name]):
                            ring.take()
            return body

        USES_RING = dict(XT=KC, QK=1, V=1, MT=1, G=1, XV=1)

        ones_loaded = sem("ones_loaded")
        half_stored, half_loaded = sem("half_stored"), sem("half_loaded")

        with nc.Block() as block:
            @block.tensor
            def _(pe):
                occupant = {}
                ring = Ring()

                def fill(it, bank, event_, shift, n):
                    if bank in occupant:
                        ev, sh, m = occupant[bank]
                        ev.wait(pe, it, sh, m)
                    occupant[bank] = (event_, shift, n)

                def next_a(it, event_, shift, n):
                    a = ring.take()
                    fill(it, ("A", a), event_, shift, n)
                    return psA[a]

                def split_products(w, w_at, x, x_at, weights_stay):
                    wh, wl = upper[w][w_at], k[w + "_lower"][w_at]
                    xh, xl = xnT[x][x_at], xnT_low[x][x_at]
                    pairs = ((wh, xl), (wl, xh), (wh, xh))
                    return list(pairs) if weights_stay else [(b, a) for a, b in pairs]

                def accumulate(ps, *products):
                    for n, (lhsT, rhs) in enumerate(products):
                        mm = nc.tensor.matmul(ps, lhsT, rhs, start=(n == 0), stop=(n == len(products) - 1))
                    return mm

                def XT(it, sh, live):
                    for kc in range(KC):
                        ps = next_a(it, pool_ready if is_mixture(it, sh) else low_ready, sh, kc)
                        if not live:
                            continue
                        if kc == 0:
                            xn_ready.wait(pe, it, sh, G - 1)
                        if is_mixture(it, sh):
                            for s in range(G):
                                nc.tensor.matmul(ps[:, GT + s:GT + s + 1], xn[:, s, kc * 128:(kc + 1) * 128],
                                                 v_ext[0][:, 0, 0, HD:HD + 1], start=True, stop=True)
                        for s in range(G):
                            mm = nc.tensor.transpose(ps[:, s * T:(s + 1) * T],
                                                     xn[:, s, kc * 128:(kc + 1) * 128], ident[0:T, 0:T])
                        mm.then_inc(xt_filled.sem, 1)

                def QK(it, sh, live, n):
                    mix = is_mixture(it, sh)
                    ps = next_a(it, qx_ready if mix else qk_relu, sh, n)
                    if not live:
                        return
                    tensor, cc = divmod(n, KC)
                    x, name = buffer(it, sh), "qk"[tensor]
                    if n == 0:
                        low_ready.wait(pe, it, sh, KC - 1)
                    cols = slice(cc * 128, (cc + 1) * 128)
                    w = ("mT_" if mix else "lw_") + name
                    products = []
                    for kc in range(KC):
                        products += split_products(w, (slice(None), kc, cols), x, (slice(None), kc), True)
                    if mix:
                        if cc == 0:
                            xvs_ready.wait(pe, it, sh, tensor)
                        products.append((k["uT_" + name][:, cols], xvs[tensor][:]))
                    accumulate(ps[:, 0:GT], *products).then_inc(qk_filled.sem, 1)

                def V(it, sh, live, n):
                    mix = is_mixture(it, sh)
                    ps = next_a(it, v_ready, sh, n)
                    if not live:
                        return
                    w, x = "mT_v" if mix else "lw_v", buffer(it, sh)
                    if mix:
                        xvs_ready.wait(pe, it, sh, 2)
                    for i in range(2):
                        cols = slice((2 * n + i) * T, (2 * n + i + 1) * T)
                        products = []
                        for kc in range(KC):
                            products += split_products(w, (slice(None), kc), x, (slice(None), kc, cols), False)
                        if mix:
                            products.append((xvs_v[:, cols], k["uT_v"][:]))
                        mm = accumulate(ps[0:T, i * D:(i + 1) * D], *products)
                    mm.then_inc(v_filled.sem, 1)

                def heads(it, sh, s, rows, stationary, moving, filled, p):
                    par = buffer(it, sh)
                    cols = slice(s * T, (s + 1) * T)
                    for n in range(8 * p, 8 * p + 8):
                        mm = nc.tensor.matmul(psS[0:T, n // G, (n % G) * T:(n % G + 1) * T],
                                              stationary[par][0:rows, n, cols], moving[par][0:rows, n, cols],
                                              start=True, stop=True)
                    mm.then_inc(filled.sem, 1)

                def S(it, sh, live, s, p):
                    s %= G
                    mix = is_mixture(it, sh)
                    fill(it, ("S", p), probs_ready, sh, 2 * s + p)
                    if not live:
                        return
                    if s == 0 and p == 0:
                        if mix:
                            mpacked.wait(pe, it, sh, 2)
                            if it[0] is None:
                                pe.wait_ge(ones_loaded, 32)
                        else:
                            packed[0].wait(pe, it, sh)
                            packed[1].wait(pe, it, sh)
                    heads(it, sh, s, ROWS + PARTS if mix else ROWS, pack[1], pack[0], s_filled, p)

                def M(it, sh, live, s, p):
                    fill(it, ("S", p), max_done, sh, 2 * s + p)
                    if s == 0 and p == 0:
                        packed[0].wait(pe, it, sh)
                        packed[1].wait(pe, it, sh)
                    heads(it, sh, s, ROWS, pack[0], pack[1], m_filled, p)

                def MT(it, sh, live):
                    ps = next_a(it, mneg_ready, sh, 0)
                    max_done.wait(pe, it, sh, 2 * G - 1, alone=passed["pe"])
                    nc.tensor.transpose(ps[0:HEADS * G, 0:T], mrow[:].rearrange("p h b -> p (h b)"),
                                        ident[0:T, 0:T]).then_inc(mt_filled.sem, 1)

                def G_(it, sh, live, n):
                    if n == 0:
                        ps = next_a(it, h1_ready, sh, 0)
                        pool_ready.wait(pe, it, sh, KC - 1)
                        accumulate(ps[0:GH, 0:G], *((k["gw1T"][:, kc], pooled[:, kc]) for kc in range(KC))
                                   ).then_inc(h1_filled.sem, 1)
                    elif n == 1:
                        ps = next_a(it, top_ready, sh, 1)
                        h1_ready.wait(pe, it, sh, 0)
                        nc.tensor.matmul(ps[0:G, 0:E], k["h1"][:], k["gw2T"][:], start=True, stop=True
                                         ).then_inc(lg_filled.sem, 1)
                    else:
                        ps = next_a(it, cT_ready, sh, 3)
                        gate.wait(pe, it, sh, 8, alone=passed["pe"])
                        nc.tensor.transpose(ps[:, 0:G], gwide[:].rearrange("p e r -> p (e r)"), ident[0:G, 0:G]
                                            ).then_inc(gt_filled.sem, 1)

                def XV(it, sh, live, n):
                    ps = next_a(it, xvs_ready, sh, n)
                    if it[0] is None and it[1] + sh == NG and n == 0:
                        pe.wait_ge(w_lower, 3)
                    products = []
                    for kc in range(KC):
                        at = (slice(None), kc)
                        products += split_products("vT_" + PROJ[n], at, buffer(it, sh), at, True)
                    accumulate(ps[:, 0:GT], *products).then_inc(xv_filled.sem, 1)

                def AV(it, sh, live, s, p):
                    if p == 0:
                        fill(it, "O", avT_ready, sh, s)
                    if not live:
                        return
                    if s % 2 == 0 and p == 0:
                        v_ready.wait(pe, it, sh, s // 2)
                    probs_ready.wait(pe, it, sh, 2 * s + p)
                    for n in range(8 * p, 8 * p + 8):
                        h = (n % KC) * HALF_HEADS + n // KC
                        mm = nc.tensor.matmul(psO[VW * (h % 4):VW * (h % 4 + 1), (h // 4) * T:(h // 4 + 1) * T],
                                              v_ext[buffer(it, sh)][:, s, h], probs[s % 2][:, n],
                                              start=True, stop=True, skip_group_check=True)
                    if p == 1:
                        mm.then_inc(av_filled.sem, 1)

                def TN(it, sh, live, s):
                    fill(it, "N", ctx_ready, sh, s)
                    if live:
                        avT_ready.wait(pe, it, sh, s)
                        for n in range(4):
                            mm = nc.tensor.transpose(psN[0:T, n * 128:(n + 1) * 128], avT[:, n], ident[:])
                        mm.then_inc(tn_filled.sem, 1)

                def TC(it, sh, live, s):
                    fill(it, "N", ctxT_ready, sh, 2 * s + 1)
                    if live:
                        for kc in range(KC):
                            mm = nc.tensor.transpose(
                                psN[:, kc * T:(kc + 1) * T],
                                ctxt[:, kc * HALF_HEADS:(kc + 1) * HALF_HEADS].rearrange("p h d -> p (h d)"),
                                ident[0:T, 0:T])
                        mm.then_inc(tc_filled.sem, 1)

                def OV(it, sh, live, s):
                    fill(it, "N", xvo_ready, sh, s)
                    ctxT_ready.wait(pe, it, sh, 2 * s + 1)
                    accumulate(psN[:, 0:T], *((k["vT_o"][:, kc], ctxT[:, kc]) for kc in range(KC))
                               ).then_inc(ov_filled.sem, 1)

                def OUT(it, sh, live, s):
                    mix = is_mixture(it, sh)
                    fill(it, "O", res_ready, sh, s)
                    if not live:
                        return
                    ctxT_ready.wait(pe, it, sh, 2 * s + 1)
                    w = k["mT_o" if mix else "lw_o"]
                    products = [(ctxT[:, kc], w[:, kc]) for kc in range(KC)]
                    if mix:
                        xvo_ready.wait(pe, it, sh, s)
                        products.append((xvo[:], k["uT_o"][:]))
                    accumulate(psO[0:T, 0:D], *products).then_inc(out_filled.sem, 1)

                run = body_of("pe", dict(XT=XT, QK=QK, V=V, S=S, M=M, MT=MT, G=G_, XV=XV, AV=AV, TN=TN, TC=TC, OV=OV,
                                   OUT=OUT))

                def body(it):
                    for bank, (ev, sh, n) in occupant.items():
                        occupant[bank] = (ev, sh - 1, n)
                    run(it)

                run_iterations(pe, body)

            @block.scalar
            def _(act):
                ring = Ring()

                def XT(it, sh, live):
                    for kc in range(KC):
                        ps = psA[ring.take()]
                        if live:
                            xt_filled.wait(act, it, sh, kc)
                            nc.scalar.activation(xnT[buffer(it, sh)][:, kc], ps[:, 0:GT], ACT.Copy
                                                 ).then_inc(xnT_ready.sem, 1)

                def split(names):
                    for n in names:
                        nc.scalar.activation(upper[n][:], k[n][:], ACT.Copy).then_inc(w_upper, 1)

                def QK(it, sh, live, n):
                    ps = psA[ring.take()]
                    if not live:
                        return
                    tensor, cc = divmod(n, KC)
                    qk_filled.wait(act, it, sh, n)
                    if cc == 0:
                        p3_ready[tensor].wait(act, it, sh - 1, 0)
                    if is_mixture(it, sh):
                        nc.scalar.activation(qx[tensor][:, cc], ps[:, 0:GT], ACT.Identity,
                                             bias=k["bias_qs" if tensor == 0 else "bias_k"][:, cc:cc + 1],
                                             scale=Q_SCALE if tensor == 0 else 1.0
                                             ).then_inc(qx_ready.of(it, sh).sem, 1)
                    else:
                        if n >= 2:
                            qx_ready.wait(act, it, sh, n - 2)
                        else:
                            qx_ready.wait(act, it, sh - 1, n + 2)
                        nc.scalar.activation(qx[tensor][:, cc], ps[:, 0:GT], ACT.Exp)
                        nc.scalar.activation(relu[n % 2][:], ps[:, 0:GT], ACT.Relu).then_inc(qk_relu.sem, 1)

                def P(it, sh, live, tensor):
                    if live:
                        qx_ready.wait(act, it, sh, KC * tensor + KC - 1)
                        stored[tensor].wait(act, it, sh - 1, 0)
                        nc.scalar.activation(parts[tensor][:, slot(tensor, 0)], qx[tensor][:], ACT.Copy
                                             ).then_inc(p1_ready.sem, 1)

                def D_(it, sh, live, tensor):
                    if live and (tensor == 1 or not is_mixture(it, sh)):
                        r_ready[tensor].wait(act, it, sh, 0)
                        nc.scalar.activation(parts[tensor][:, slot(tensor, 1)], qx[tensor][:], ACT.Copy
                                             ).then_inc(p2_ready[tensor].of(it, sh).sem, 1)

                def V(it, sh, live, n):
                    ps = psA[ring.take()]
                    if live:
                        v_filled.wait(act, it, sh, n)
                        nc.scalar.activation(
                            v_ext[buffer(it, sh)][:, 2 * n:2 * n + 2, :, 0:HD],
                            ps[0:T].rearrange("p (b h d) -> p b h d", b=2, h=HEADS), ACT.Copy
                        ).then_inc(v_ready.sem, 1)

                def SX(it, sh, live, s, p):
                    s %= G
                    if live and is_mixture(it, sh):
                        s_filled.wait(act, it, sh, 2 * s + p)
                        nc.scalar.activation(
                            probs[s % 2][:, 8 * p:8 * p + 8].rearrange("p (a h) t -> p a h t", a=2),
                            pair(p), ACT.Exp).then_inc(probs_ready.of(it, sh).sem, 1)

                def MT(it, sh, live):
                    ps = psA[ring.take()]
                    mt_filled.wait(act, it, sh, 0)
                    if it[0] is not None or not it[1] + sh == NG:
                        mpart.wait(act, it, sh - 1, 3)
                    nc.scalar.activation(mneg[:], ps[0:HEADS * G, 0:T], ACT.Copy, scale=-1.0
                                         ).then_inc(mneg_ready.sem, 1)

                def G_(it, sh, live, n):
                    ps = psA[ring.take()]
                    if n == 0:
                        h1_filled.wait(act, it, sh, 0)
                        nc.scalar.activation(k["h1"][0:GH], ps[0:GH, 0:G], ACT.Relu, bias=k["gb1"][:, 0:1],
                                             scale=1.0 / T).then_inc(h1_ready.sem, 1)
                    if n == 1:
                        gate.wait(act, it, sh, 1)
                        nc.scalar.activation(gexp[:], gdiff[:], ACT.Exp).then_inc(gexp_ready.sem, 1)

                def AV(it, sh, live, s):
                    if live:
                        av_filled.wait(act, it, sh, s)
                        nc.scalar.activation(avT[:].rearrange("p g t -> p (g t)"), psO[:, 0:GT], ACT.Copy
                                             ).then_inc(avT_ready.sem, 1)

                def TC(it, sh, live, s):
                    if live:
                        tc_filled.wait(act, it, sh, s)
                        if not is_mixture(it, sh):
                            nc.scalar.activation(ctxT[:].rearrange("p c t -> p (c t)"), psN[:, 0:KC * T], ACT.Copy
                                                 ).then_inc(ctxT_ready.sem, KC)
                            return
                        for kc in range(KC):
                            nc.scalar.activation(ctxT[:, kc], psN[:, kc * T:(kc + 1) * T], ACT.Identity,
                                                 bias=k["bias_v"][:, kc:kc + 1]).then_inc(ctxT_ready.sem, 1)

                act.sem_inc(ctxT_ready.sem, 1)
                nc.scalar.mul(k["bias_qs"][:], k["bias_q"][:], Q_SCALE).then_inc(init_act, 1)
                act.wait_ge(init_act, 1)
                body = body_of("act", dict(XT=XT, QK=QK, P=P, D=D_, V=V, SX=SX, MT=MT, G=G_, AV=AV, TC=TC), ring)

                def run(it):
                    body(it)
                    if it[0] is None and it[1] == -1:
                        act.wait_ge(half_stored, 16)
                        split([f"mT_{n}" for n in "qkv"])

                run_iterations(act, run)

            @block.vector
            def _(dve):
                ring = Ring()

                def LN(it, sh, live):
                    if not live:
                        return
                    for s in range(G):
                        nc.vector.bn_stats(stat[:, s], hid[:, sample(it, sh, s)]).then_inc(ln_stats.sem, 1)
                    ln_stats.wait(dve, it, sh, G - 1, alone=passed["dve"])
                    for s in range(G):
                        nc.vector.bn_aggr(mv[:, s], stat[:, s]).then_inc(ln_aggr.sem, 1)
                    ln_aggr.wait(dve, it, sh, G - 1)
                    nc.vector.tensor_scalar(ve[:], mv[:, :, 1], LN_EPS, None, ALU.add).then_inc(ln_var.sem, 1)

                def LNX(it, sh, live):
                    if not live:
                        return
                    xt_filled.wait(dve, it, sh - 1, KC - 1)
                    ln_rstd.wait(dve, it, sh, 0)
                    for s in range(G):
                        nc.vector.tensor_scalar(xn[:, s], hid[:, sample(it, sh, s)], mv[:, s, 0:1], rstd[:, s:s + 1],
                                                ALU.subtract, ALU.mult).then_inc(xn_ready.sem, 1)

                def QK(it, sh, live, n):
                    ring.take()
                    if live and not is_mixture(it, sh):
                        tensor, cc = divmod(n, KC)
                        q = qx[tensor][:, cc]
                        qk_relu.wait(dve, it, sh, n)
                        nc.vector.scalar_tensor_tensor(q, q, 1.0, relu[n % 2][:], ALU.min, ALU.add
                                                       ).then_inc(qx_ready.of(it, sh).sem, 1)

                def P(it, sh, live, tensor):
                    if tensor == 1 and is_mixture(it, sh):
                        p1_ready.wait(dve, it, sh, tensor)
                        nc.vector.tensor_tensor(qx[1][:], qx[1][:], parts[1][:, slot(1, 0)], ALU.subtract
                                                ).then_inc(r_ready[1].of(it, sh).sem, 1)

                def D_(it, sh, live, tensor):
                    if not is_mixture(it, sh):
                        return
                    if tensor == 0:
                        r_ready[0].wait(dve, it, sh, 0)
                        nc.vector.tensor_copy(parts[0][:, slot(0, 1)], qx[0][:]
                                              ).then_inc(p2_ready[0].of(it, sh).sem, 1)
                    else:
                        p2_ready[1].wait(dve, it, sh, 0)
                        nc.vector.tensor_tensor(parts[1][:, slot(1, 2)], qx[1][:], parts[1][:, slot(1, 1)],
                                                ALU.subtract).then_inc(p3_ready[1].of(it, sh).sem, 1)

                def SX(it, sh, live, s, p):
                    s %= G
                    if live and not is_mixture(it, sh):
                        s_filled.wait(dve, it, sh, 2 * s + p)
                        nc.vector.tensor_tensor(
                            probs[s % 2][:, 8 * p:8 * p + 8].rearrange("p (a h) t -> p a h t", a=2), pair(p),
                            k["mask"][:].unsqueeze(1).unsqueeze(1).broadcast_to([T, 2, G, T]), ALU.mult
                        ).then_inc(probs_ready.of(it, sh).sem, 1)

                def M(it, sh, live, s, p):
                    m_filled.wait(dve, it, sh, 2 * s + p)
                    nc.vector.tensor_reduce(mrow[:, 8 * p:8 * p + 8, s].rearrange("p (a h) -> p a h", a=2),
                                            pair(p), AX.X, ALU.max).then_inc(max_done.sem, 1)

                def MT(it, sh, live):
                    ring.take()
                    mneg_ready.wait(dve, it, sh, 0)
                    if it[0] is not None or not it[1] + sh == NG:
                        mpacked.wait(dve, it, sh - 1, 2)
                    nc.vector.tensor_copy(mparts[:, 0], mneg[:]).then_inc(mpart.sem, 1)
                    mpart.wait(dve, it, sh, 0)
                    nc.vector.tensor_tensor(mneg[:], mneg[:], mparts[:, 0], ALU.subtract).then_inc(mpart.sem, 1)
                    mpart.wait(dve, it, sh, 1)
                    nc.vector.tensor_copy(mparts[:, 1], mneg[:]).then_inc(mpart.sem, 1)
                    mpart.wait(dve, it, sh, 2)
                    nc.vector.tensor_tensor(mparts[:, 2], mneg[:], mparts[:, 1], ALU.subtract).then_inc(mpart.sem, 1)

                def XT(it, sh, live):
                    for kc in range(KC):
                        ps = psA[ring.take()]
                        if live:
                            xnT_ready.wait(dve, it, sh, kc)
                            p = buffer(it, sh)
                            nc.vector.tensor_tensor(xnT_low[p][:, kc], ps[:, 0:GT], xnT[p][:, kc].bitcast(F32),
                                                    ALU.subtract).then_inc(low_ready.sem, 1)
                            if is_mixture(it, sh):
                                nc.vector.tensor_copy(pooled[:, kc], ps[:, GT:GT + G]).then_inc(pool_ready.sem, 1)

                def G_(it, sh, live, n):
                    ps = psA[ring.take()]
                    if n == 0:
                        return
                    if n == 1:
                        lg_filled.wait(dve, it, sh, 0, alone=passed["dve"])
                        nc.vector.max(top[:], ps[0:G, 0:E]).then_inc(top_ready.sem, 1)
                        top_ready.wait(dve, it, sh, 0, alone=passed["dve"])
                        nc.vector.max_index(topi[:], top[:], ps[0:G, 0:E]).then_inc(top_ready.sem, 1)
                    else:
                        gt_filled.wait(dve, it, sh, 0)
                        for i in range(4):
                            nc.vector.tensor_scalar(cT[:, i, span(it, sh)], ps[:, 0:G], k["svals"][:, i:i + 1], None,
                                                    ALU.mult).then_inc(cT_ready.sem, 1)

                def XV(it, sh, live, n):
                    ps = psA[ring.take()]
                    dst = xvs[n] if n < 2 else xvs_v
                    xv_filled.wait(dve, it, sh, n)
                    if n == 0:
                        cT_ready.wait(dve, it, sh, 3)
                    nc.vector.tensor_tensor(
                        dst[:].rearrange("p (b t) -> p b t", b=G), ps[:, 0:GT].rearrange("p (b t) -> p b t", b=G),
                        cT[:, n, span(it, sh)].unsqueeze(2).broadcast_to([128, G, T]), ALU.mult
                    ).then_inc(xvs_ready.sem, 1)

                def TN(it, sh, live, s):
                    if not live:
                        return
                    tn_filled.wait(dve, it, sh, s)
                    ps = psN[0:T].rearrange("p (h w) -> p h w", w=VW)
                    sums = ps[:, :, HD]
                    if not is_mixture(it, sh):
                        nc.vector.tensor_scalar(den[:], sums, DEN_EPS, None, ALU.add).then_inc(den_ready.sem, 1)
                        den_ready.wait(dve, it, sh, s)
                        sums = den[:]
                    nc.vector.reciprocal(rden[:], sums).then_inc(rden_ready.sem, 1)
                    rden_ready.wait(dve, it, sh, s)
                    nc.vector.tensor_tensor(ctxt[:], ps[:, :, 0:HD], rden[:].unsqueeze(2).broadcast_to([T, HEADS, HD]),
                                            ALU.mult).then_inc(ctx_ready.sem, 1)

                def OV(it, sh, live, s):
                    b = sample(it, sh, s)
                    ov_filled.wait(dve, it, sh, s)
                    nc.vector.tensor_scalar(xvo[:], psN[:, 0:T],
                                            cT[:, 3, slice(b, b + 1) if it[0] is None else bass.ds(b, 1)],
                                            None, ALU.mult).then_inc(xvo_ready.sem, 1)

                def OUT(it, sh, live, s):
                    if live:
                        hb = hid[:, sample(it, sh, s)]
                        out_filled.wait(dve, it, sh, s)
                        if is_mixture(it, sh) and s == 0:
                            hob_ready.wait(dve, it, sh, 0)
                        nc.vector.tensor_tensor(hb, psO[0:T, 0:D], hb, ALU.add).then_inc(res_ready.sem, 1)

                dve.sem_inc(res_ready.sem, 1)
                body = body_of("dve", dict(LN=LN, LNX=LNX, XT=XT, QK=QK, P=P, D=D_, SX=SX, M=M, MT=MT, G=G_, XV=XV,
                                    TN=TN, OV=OV, OUT=OUT), ring)

                def run(it):
                    body(it)
                    if it[0] is None and it[1] == -1:
                        dve.wait_ge(half_loaded, 16)

                run_iterations(dve, run)

            @block.gpsimd
            def _(pool):
                def LN(it, sh, live):
                    if live:
                        ln_var.wait(pool, it, sh, 0)
                        nc.gpsimd.tensor_tensor(rstd[:], ve[:], k["lneps_half"][:], ALU.pow).then_inc(ln_rstd.sem, 1)

                def P(it, sh, live, tensor):
                    if live and (tensor == 0 or not is_mixture(it, sh)):
                        p1_ready.wait(pool, it, sh, tensor)
                        nc.gpsimd.tensor_tensor(qx[tensor][:], qx[tensor][:], parts[tensor][:, slot(tensor, 0)],
                                                ALU.subtract).then_inc(r_ready[tensor].of(it, sh).sem, 1)

                def D_(it, sh, live, tensor):
                    if live and (tensor == 0 or not is_mixture(it, sh)):
                        p2_ready[tensor].wait(pool, it, sh, 0)
                        nc.gpsimd.tensor_tensor(parts[tensor][:, slot(tensor, 2)], qx[tensor][:],
                                                parts[tensor][:, slot(tensor, 1)], ALU.subtract
                                                ).then_inc(p3_ready[tensor].of(it, sh).sem, 1)

                def G_(it, sh, live, n):
                    if n != 1:
                        return

                    def chained(e, ins):
                        ins.then_inc(gate.sem, 1)
                        gate.wait(pool, it, sh, e, alone=passed["pool"])

                    top_ready.wait(pool, it, sh, 1, alone=passed["pool"])
                    chained(0, nc.gpsimd.tensor_copy(topf[:], topi[:, 0:2]))
                    chained(1, nc.gpsimd.tensor_tensor(gdiff[:], top[:, 1:2], top[:, 0:1], ALU.subtract))
                    gexp_ready.wait(pool, it, sh, 0, alone=passed["pool"])
                    chained(2, nc.gpsimd.tensor_scalar(gden[:], gexp[:], 1.0, None, ALU.add))
                    chained(3, nc.gpsimd.tensor_tensor(gval[:, 0:1], gden[:], minus1[:], ALU.pow))
                    chained(4, nc.gpsimd.tensor_tensor(gval[:, 1:2], gexp[:], gval[:, 0:1], ALU.mult))
                    for i in range(2):
                        chained(5 + i, nc.gpsimd.tensor_scalar(
                            gsel[:, i], k["iotaf"][:], topf[:, i:i + 1], gval[:, i:i + 1], ALU.is_equal, ALU.mult))
                    chained(7, nc.gpsimd.tensor_tensor(gates[:], gsel[:, 0], gsel[:, 1], ALU.add))
                    chained(8, nc.gpsimd.tensor_copy(gwide[:], gates[:].unsqueeze(2).broadcast_to([G, E, R])))

                def HB(it, sh, live):
                    hg = hid[:, span(it, sh)]
                    xn_ready.wait(pool, it, sh, G - 1)
                    nc.gpsimd.tensor_tensor(hg, hg, k["ob"][:].unsqueeze(1).broadcast_to([T, G, D]), ALU.add
                                            ).then_inc(hob_ready.sem, 1)

                nc.gpsimd.memset(minus1[:], -1.0).then_inc(init_pool, 1)
                pool.wait_ge(init_pool, 1)
                body = body_of("pool", dict(LN=LN, P=P, D=D_, G=G_, HB=HB))

                def run(it):
                    body(it)
                    if it[0] is None and it[1] == -1:
                        for i, n in enumerate("qkv"):
                            pool.wait_ge(w_upper, i + 1)
                            nc.gpsimd.tensor_tensor(k[f"mT_{n}_lower"][:], k[f"mT_{n}"][:],
                                                    upper[f"mT_{n}"][:].bitcast(F32), ALU.subtract
                                                    ).then_inc(w_lower, 1)

                run_iterations(pool, run)

            @block.sync
            def _(sp):
                def PACK(it, sh, live, n):
                    if not live:
                        return
                    par, done = buffer(it, sh), packed[n].sem(it, sh)
                    p3_ready[n].wait(sp, it, sh, 0, alone=passed["sp"])
                    sp.dma_start(scratch[n][par].rearrange("r d h c t -> (d h) r (c t)"),
                                 parts[n][:].rearrange("p r c t -> p r (c t)")).then_inc(stored[n].sem, 16)
                    s_filled.wait(sp, it, sh - 2, 2 * G - 1, alone=passed["sp"])
                    stored[n].wait(sp, it, sh, 0, alone=passed["sp"])
                    src = scratch[n][par].rearrange("r d h c t -> (r d) (h c t)")
                    dst = pack[n][par][:].rearrange("p h t -> p (h t)")
                    first = 0 if n == 0 else HD
                    sp.dma_start(dst[0:3 * HD], src).then_inc(done, 16)
                    sp.dma_start(dst[3 * HD:5 * HD], src[first:first + 2 * HD]).then_inc(done, 16)
                    sp.dma_start(dst[5 * HD:6 * HD], src[2 * first:2 * first + HD]).then_inc(done, 16)

                def MT(it, sh, live):
                    mpart.wait(sp, it, sh, 3, alone=passed["sp"])
                    for r in range(PARTS):
                        sp.dma_start(pack[0][buffer(it, sh)][ROWS + r:ROWS + r + 1].rearrange("p h t -> p (h t)"),
                                     mparts[:, r]).then_inc(mpacked.sem, 16)

                def STORE(it, sh, live):
                    res_ready.wait(sp, it, sh, G - 1, alone=passed["sp"])
                    bs = span(it, sh)
                    sp.dma_start(out[bs, IMG:T].rearrange("b t d -> t b d"), hid[0:TXT, bs]).then_inc(stores.sem, 16)
                    sp.dma_start(out[bs, 0:IMG].rearrange("b t d -> t b d"), hid[TXT:T, bs]).then_inc(stores.sem, 16)

                half = slice(B // 2, B)
                sp.dma_start(k["tok"][half, 1:].rearrange("b (h w) e -> b h (w e)", h=GRID),
                             k["y1"][0:B // 2 * GRID].rearrange("p w e -> p (w e)")).then_inc(half_stored, 16)
                sp.wait_ge(half_stored, 16)
                sp.dma_start(hid[TXT:T, half], k["tok"][half].rearrange("b n e -> n b e")).then_inc(half_loaded, 16)
                for p in range(2):
                    sp.dma_start(pack[1][p][ROWS:ROWS + PARTS].rearrange("p h (g t) -> p (h g) t", g=G),
                                 k["ones"].unsqueeze(1).broadcast_to([PARTS, HEADS * G, T])).then_inc(ones_loaded, 16)
                run_iterations(sp, body_of("sp", dict(PACK=PACK, MT=MT, STORE=STORE)))
                sp.wait_ge(stores.sem, 16 * 2 * NG)


def program(nc, A, out):
    with ExitStack() as c:
        k = {}

        def keep(name, shape, dt=F32):
            k[name] = c.enter_context(nc.sbuf_tensor(name, shape, dt))

        def keep_in_turn(first, *later):
            name, shape = first
            with nc.sbuf_tensor(name, shape, F32) as k[name]:
                pass
            for name, shape in later:
                keep(name, shape, F32R)

        keep("hid", [T, B, D])
        keep("ident", [128, 128])
        keep("mask", [T, T])
        keep("lneps_half", [T, G])
        keep("iota", [G, E], I32)
        keep("iotaf", [G, E])
        keep("h1", [GH + 1, G])
        keep("gw1T", [128, KC, GH])
        keep("gw2T", [GH + 1, E])
        keep("gb1", [GH, 1])
        keep("svals", [ER, 4])
        keep("bias_q", [128, KC])
        keep("bias_qs", [128, KC])
        keep("bias_k", [128, KC])
        keep("bias_v", [128, KC])
        keep("ob", [T, D])
        keep_in_turn(("y1", [128, GRID, D]), *((f"mT_{n}_upper", [128, KC, D]) for n in "qkv"))
        k["ones"] = nc.dram_tensor("ones_scratch", (PARTS, T), BF16).ap()
        k["tok"] = nc.dram_tensor("tok_scratch", (B, IMG, D), F32).ap()
        for n in PROJ:
            for name, shape in ((f"lw_{n}", [128, KC, D]), (f"mT_{n}", [128, KC, D]), (f"vT_{n}", [128, KC, ER])):
                if name in SPLIT_WEIGHTS:
                    keep_in_turn((name, shape), (f"{name}_lower", shape))
                else:
                    keep(name, shape)
            keep(f"uT_{n}", [ER, D])
        for p in range(2):
            keep(f"v_ext{p}", [T, G, HEADS, VW])
        with ExitStack() as place:
            for name, shape in (("xvo", [128, T]), ("mrow", [T, HEADS, G]), ("mneg", [HEADS * G, T]),
                                ("gwide", [G, E, R]),
                                ("cT", [128, 4, B])):
                k[name] = place.enter_context(nc.sbuf_tensor(name, shape, F32))
        for n in SPLIT_WEIGHTS:
            if n[0:2] != "mT":
                keep(f"{n}_upper", k[n].shape, F32R)
        embed(nc, c, A, k)
        attention(nc, A, k, out)


def kernel(**inputs):
    import numpy as np
    import concourse.bacc as bacc
    from concourse.bass_utils import run_bass_kernel_spmd

    nc = bacc.Bacc("TRN2", target_bir_lowering=False, num_devices=1)
    arrays, aps = {}, {}
    for name, value in inputs.items():
        a = np.ascontiguousarray(value)
        arrays[f"in_{name}"] = a
        aps[name.removeprefix("L0_")] = nc.dram_tensor(f"in_{name}", a.shape, mybir.dt.from_np(a.dtype),
                                                       kind="ExternalInput").ap()
    out = nc.dram_tensor("out", (B, T, D), F32, kind="ExternalOutput").ap()
    program(nc, aps, out)
    return run_bass_kernel_spmd(nc, [arrays], core_ids=[0]).results[0]["out"]
```
